# Optimizing a Trainium2 kernel written in Bass

```python
import numpy as np
import jax
import jax.numpy as jnp

def _softmax(x, axis=-1):
    return jax.nn.softmax(x, axis=axis)

def _gelu(x):
    return jax.nn.gelu(x, approximate=True)

def _silu(x):
    return jax.nn.silu(x)

def _sigmoid(x):
    return jax.nn.sigmoid(x)

def _layernorm(x, axis=-1, eps=1e-05):
    m = jnp.mean(x, axis=axis, keepdims=True)
    v = jnp.var(x, axis=axis, keepdims=True)
    return (x - m) / jnp.sqrt(v + eps)

def _scatter_add(tgt, idx, src, axis=0):
    return tgt.at[idx].add(src)

def _segment_sum(src, seg, n):
    return jax.ops.segment_sum(src, seg, n)
kernel_name = 'mk_gnn_preln_d2_gnn_r8_5f0a21'

def setup_inputs(seed: int=0):
    np.random.seed(seed)
    _w = jnp.asarray

    def _rec_inputs():
        import jax
        import jax.numpy as jnp
        _gk = jax.random.key(seed)
        x = -0.0002949 + 1 * jax.random.normal(jax.random.fold_in(_gk, 1), (1250, 512), jnp.float32)
        src = jax.random.randint(jax.random.fold_in(_gk, 2), (20000,), 0, 1250, jnp.int32)
        dst = jax.random.randint(jax.random.fold_in(_gk, 3), (20000,), 0, 1250, jnp.int32)
        _o = jnp.argsort(dst, stable=True)
        src = src[_o]
        dst = dst[_o]
        edge_type_2 = jax.random.randint(jax.random.fold_in(_gk, 12), (20000,), 0, 2, jnp.int32)
        node_vec1 = jax.random.uniform(jax.random.fold_in(_gk, 13), (1250, 1), jnp.float32, 0.0, 0.999957)
        return (x, src, dst, edge_type_2, node_vec1)
    x, src, dst, edge_type_2, node_vec1 = _rec_inputs()

    def _L0_gnn_setup():
        import jax, jax.numpy as jnp
        import numpy as np
        N_NODES = 40962
        LATENT_DIM = 512
        N_EDGES = 81924
        NUM_BLOCKS = 4
        NUM_HEADS = 4
        NUM_FREQ = 32
        BASE_PERIOD = 16
        NOISE_EMB_DIM = 16
        EPS = 1e-05

        def _cond_layer_norm(x, cond, sw, sb, bw, bb):
            mu = jnp.mean(x, axis=-1, keepdims=True)
            var = jnp.var(x, axis=-1, keepdims=True)
            xn = (x - mu) * jax.lax.rsqrt(var + EPS)
            scale = cond @ sw + sb
            bias = cond @ bw + bb
            return xn * (1.0 + scale) + bias

        def _sparse_attention(x, src, dst, wq, bq, wk, bk, wv, bv, wo, bo):
            N, D = x.shape
            H, Dh = (NUM_HEADS, D // NUM_HEADS)
            q = (x @ wq + bq).reshape(N, H, Dh) * Dh ** (-0.5)
            k = (x @ wk + bk).reshape(N, H, Dh)
            v = (x @ wv + bv).reshape(N, H, Dh)
            scores = jnp.einsum('ehd,ehd->eh', q[src], k[dst])
            smax = jax.ops.segment_max(scores, src, num_segments=N)
            ex = jnp.exp(scores - smax[src])
            denom = jax.ops.segment_sum(ex, src, num_segments=N)
            attn = ex / denom[src]
            out = jax.ops.segment_sum(attn[:, :, None] * v[dst], src, num_segments=N)
            return out.reshape(N, D) @ wo + bo

        def _forward(x, edge_index, noise_levels, f_w1, f_b1, f_w2, f_b2, s1_w, s1_b, b1_w, b1_b, wq, bq, wk, bk, wv, bv, wo, bo, s2_w, s2_b, b2_w, b2_b, m_w1, m_b1, m_w2, m_b2):
            src, dst = (edge_index[0], edge_index[1])
            freqs = jnp.arange(1, NUM_FREQ + 1, dtype=x.dtype) * (2.0 * np.pi / BASE_PERIOD)
            ph = noise_levels * freqs
            emb = jnp.concatenate([jnp.sin(ph), jnp.cos(ph)], axis=-1)
            cond = jax.nn.silu(emb @ f_w1 + f_b1) @ f_w2 + f_b2
            for i in range(NUM_BLOCKS):
                y = _cond_layer_norm(x, cond, s1_w[i], s1_b[i], b1_w[i], b1_b[i])
                y = _sparse_attention(y, src, dst, wq[i], bq[i], wk[i], bk[i], wv[i], bv[i], wo[i], bo[i])
                x = x + y
                y = _cond_layer_norm(x, cond, s2_w[i], s2_b[i], b2_w[i], b2_b[i])
                y = jax.nn.relu(y @ m_w1[i] + m_b1[i]) @ m_w2[i] + m_b2[i]
                x = x + y
            return x
        key = jax.random.key(seed)
        ks = jax.random.split(key, 20)

        def w(k, shape, s=0.02):
            return jax.random.normal(k, shape, dtype=jnp.float32) * s
        D, B, C = (LATENT_DIM, NUM_BLOCKS, NOISE_EMB_DIM)
        z = lambda *s: jnp.zeros(s, jnp.float32)
        return {'latent_mesh_nodes': jax.random.normal(ks[0], (N_NODES, D), dtype=jnp.float32), 'edge_index': jax.random.randint(ks[1], (2, N_EDGES), 0, N_NODES, dtype=jnp.int32), 'noise_levels': jax.random.uniform(ks[2], (N_NODES, 1), dtype=jnp.float32), 'f_w1': w(ks[3], (2 * NUM_FREQ, C)), 'f_b1': z(C), 'f_w2': w(ks[4], (C, C)), 'f_b2': z(C), 's1_w': w(ks[5], (B, C, D)), 's1_b': z(B, D), 'b1_w': w(ks[6], (B, C, D)), 'b1_b': z(B, D), 'wq': w(ks[7], (B, D, D)), 'bq': z(B, D), 'wk': w(ks[8], (B, D, D)), 'bk': z(B, D), 'wv': w(ks[9], (B, D, D)), 'bv': z(B, D), 'wo': w(ks[10], (B, D, D)), 'bo': z(B, D), 's2_w': w(ks[11], (B, C, D)), 's2_b': z(B, D), 'b2_w': w(ks[12], (B, C, D)), 'b2_b': z(B, D), 'm_w1': w(ks[13], (B, D, D)), 'm_b1': z(B, D), 'm_w2': w(ks[14], (B, D, D)), 'm_b2': z(B, D)}
    _L0_gnn_all = _L0_gnn_setup()
    _L0_gnn_in = {k: v for k, v in _L0_gnn_all.items() if k in ('f_w1', 'f_b1', 'f_w2', 'f_b2', 's1_w', 's1_b', 'b1_w', 'b1_b', 'wq', 'bq', 'wk', 'bk', 'wv', 'bv', 'wo', 'bo', 's2_w', 's2_b', 'b2_w', 'b2_b', 'm_w1', 'm_b1', 'm_w2', 'm_b2')}
    del _L0_gnn_all

    def _L1_gnn_setup():
        import jax, jax.numpy as jnp
        import numpy as np
        NUM_RELATIONS = 2
        NUM_BASES = 30
        HIDDEN = 512
        N_NODES = 1250
        N_EDGES = 20000

        def rgcn_gate_layer(x, row, col, edge_type, basis, att, gate_w, root, bias):
            H = x.shape[1]
            w = jnp.einsum('rb,bio->rio', att, basis)
            x_j = x[col]
            msgs = []
            for r in range(NUM_RELATIONS):
                gate = jax.nn.sigmoid(x_j @ gate_w[r, :, 0])
                msgs.append(gate[:, None] * x_j @ w[r])
            msg = jnp.where((edge_type == 0)[:, None], msgs[0], msgs[1])
            agg = jax.ops.segment_sum(msg, row, num_segments=x.shape[0])
            return agg + x @ root + bias
        key = jax.random.key(seed)
        ks = jax.random.split(key, 16)
        H, R, B = (HIDDEN, NUM_RELATIONS, NUM_BASES)
        bound = 1.0 / np.sqrt(B * H)
        u = lambda k, shape: jax.random.uniform(k, shape, jnp.float32, -bound, bound)
        inp = {'x': jax.random.normal(ks[0], (N_NODES, H), jnp.float32), 'edge_index': jax.random.randint(ks[1], (2, N_EDGES), 0, N_NODES, jnp.int32), 'edge_type': jax.random.randint(ks[2], (N_EDGES,), 0, R, jnp.int32), 'basis1': u(ks[3], (B, H, H)), 'att1': u(ks[4], (R, B)), 'gate_w1': u(ks[5], (R, H, 1)), 'root1': u(ks[6], (H, H)), 'bias1': u(ks[7], (H,)), 'basis2': u(ks[8], (B, H, H)), 'att2': u(ks[9], (R, B)), 'gate_w2': u(ks[10], (R, H, 1)), 'root2': u(ks[11], (H, H)), 'bias2': u(ks[12], (H,))}
        return inp
    _L1_gnn_all = _L1_gnn_setup()
    _L1_gnn_in = {k: v for k, v in _L1_gnn_all.items() if k in ('basis1', 'att1', 'gate_w1', 'root1', 'bias1', 'basis2', 'att2', 'gate_w2', 'root2', 'bias2')}
    del _L1_gnn_all
    return {'x': x, 'src': src, 'dst': dst, 'edge_type_2': edge_type_2, 'node_vec1': node_vec1, 'L0_gnn_f_w1': _L0_gnn_in['f_w1'], 'L0_gnn_f_b1': _L0_gnn_in['f_b1'], 'L0_gnn_f_w2': _L0_gnn_in['f_w2'], 'L0_gnn_f_b2': _L0_gnn_in['f_b2'], 'L0_gnn_s1_w': _L0_gnn_in['s1_w'], 'L0_gnn_s1_b': _L0_gnn_in['s1_b'], 'L0_gnn_b1_w': _L0_gnn_in['b1_w'], 'L0_gnn_b1_b': _L0_gnn_in['b1_b'], 'L0_gnn_wq': _L0_gnn_in['wq'], 'L0_gnn_bq': _L0_gnn_in['bq'], 'L0_gnn_wk': _L0_gnn_in['wk'], 'L0_gnn_bk': _L0_gnn_in['bk'], 'L0_gnn_wv': _L0_gnn_in['wv'], 'L0_gnn_bv': _L0_gnn_in['bv'], 'L0_gnn_wo': _L0_gnn_in['wo'], 'L0_gnn_bo': _L0_gnn_in['bo'], 'L0_gnn_s2_w': _L0_gnn_in['s2_w'], 'L0_gnn_s2_b': _L0_gnn_in['s2_b'], 'L0_gnn_b2_w': _L0_gnn_in['b2_w'], 'L0_gnn_b2_b': _L0_gnn_in['b2_b'], 'L0_gnn_m_w1': _L0_gnn_in['m_w1'], 'L0_gnn_m_b1': _L0_gnn_in['m_b1'], 'L0_gnn_m_w2': _L0_gnn_in['m_w2'], 'L0_gnn_m_b2': _L0_gnn_in['m_b2'], 'L1_gnn_basis1': _L1_gnn_in['basis1'], 'L1_gnn_att1': _L1_gnn_in['att1'], 'L1_gnn_gate_w1': _L1_gnn_in['gate_w1'], 'L1_gnn_root1': _L1_gnn_in['root1'], 'L1_gnn_bias1': _L1_gnn_in['bias1'], 'L1_gnn_basis2': _L1_gnn_in['basis2'], 'L1_gnn_att2': _L1_gnn_in['att2'], 'L1_gnn_gate_w2': _L1_gnn_in['gate_w2'], 'L1_gnn_root2': _L1_gnn_in['root2'], 'L1_gnn_bias2': _L1_gnn_in['bias2']}

def reference(x, src, dst, edge_type_2, node_vec1, L0_gnn_f_w1, L0_gnn_f_b1, L0_gnn_f_w2, L0_gnn_f_b2, L0_gnn_s1_w, L0_gnn_s1_b, L0_gnn_b1_w, L0_gnn_b1_b, L0_gnn_wq, L0_gnn_bq, L0_gnn_wk, L0_gnn_bk, L0_gnn_wv, L0_gnn_bv, L0_gnn_wo, L0_gnn_bo, L0_gnn_s2_w, L0_gnn_s2_b, L0_gnn_b2_w, L0_gnn_b2_b, L0_gnn_m_w1, L0_gnn_m_b1, L0_gnn_m_w2, L0_gnn_m_b2, L1_gnn_basis1, L1_gnn_att1, L1_gnn_gate_w1, L1_gnn_root1, L1_gnn_bias1, L1_gnn_basis2, L1_gnn_att2, L1_gnn_gate_w2, L1_gnn_root2, L1_gnn_bias2):
    import jax
    import jax.numpy as jnp

    def _L0_gnn_ref(latent_mesh_nodes, edge_index, noise_levels, f_w1, f_b1, f_w2, f_b2, s1_w, s1_b, b1_w, b1_b, wq, bq, wk, bk, wv, bv, wo, bo, s2_w, s2_b, b2_w, b2_b, m_w1, m_b1, m_w2, m_b2):
        import jax, jax.numpy as jnp
        import numpy as np
        N_NODES = 40962
        LATENT_DIM = 512
        N_EDGES = 81924
        NUM_BLOCKS = 4
        NUM_HEADS = 4
        NUM_FREQ = 32
        BASE_PERIOD = 16
        NOISE_EMB_DIM = 16
        EPS = 1e-05

        def _cond_layer_norm(x, cond, sw, sb, bw, bb):
            mu = jnp.mean(x, axis=-1, keepdims=True)
            var = jnp.var(x, axis=-1, keepdims=True)
            xn = (x - mu) * jax.lax.rsqrt(var + EPS)
            scale = cond @ sw + sb
            bias = cond @ bw + bb
            return xn * (1.0 + scale) + bias

        def _sparse_attention(x, src, dst, wq, bq, wk, bk, wv, bv, wo, bo):
            N, D = x.shape
            H, Dh = (NUM_HEADS, D // NUM_HEADS)
            q = (x @ wq + bq).reshape(N, H, Dh) * Dh ** (-0.5)
            k = (x @ wk + bk).reshape(N, H, Dh)
            v = (x @ wv + bv).reshape(N, H, Dh)
            scores = jnp.einsum('ehd,ehd->eh', q[src], k[dst])
            smax = jax.ops.segment_max(scores, src, num_segments=N)
            ex = jnp.exp(scores - smax[src])
            denom = jax.ops.segment_sum(ex, src, num_segments=N)
            attn = ex / denom[src]
            out = jax.ops.segment_sum(attn[:, :, None] * v[dst], src, num_segments=N)
            return out.reshape(N, D) @ wo + bo

        def _forward(x, edge_index, noise_levels, f_w1, f_b1, f_w2, f_b2, s1_w, s1_b, b1_w, b1_b, wq, bq, wk, bk, wv, bv, wo, bo, s2_w, s2_b, b2_w, b2_b, m_w1, m_b1, m_w2, m_b2):
            src, dst = (edge_index[0], edge_index[1])
            freqs = jnp.arange(1, NUM_FREQ + 1, dtype=x.dtype) * (2.0 * np.pi / BASE_PERIOD)
            ph = noise_levels * freqs
            emb = jnp.concatenate([jnp.sin(ph), jnp.cos(ph)], axis=-1)
            cond = jax.nn.silu(emb @ f_w1 + f_b1) @ f_w2 + f_b2
            for i in range(NUM_BLOCKS):
                y = _cond_layer_norm(x, cond, s1_w[i], s1_b[i], b1_w[i], b1_b[i])
                y = _sparse_attention(y, src, dst, wq[i], bq[i], wk[i], bk[i], wv[i], bv[i], wo[i], bo[i])
                x = x + y
                y = _cond_layer_norm(x, cond, s2_w[i], s2_b[i], b2_w[i], b2_b[i])
                y = jax.nn.relu(y @ m_w1[i] + m_b1[i]) @ m_w2[i] + m_b2[i]
                x = x + y
            return x
        return _forward(latent_mesh_nodes, edge_index, noise_levels, f_w1, f_b1, f_w2, f_b2, s1_w, s1_b, b1_w, b1_b, wq, bq, wk, bk, wv, bv, wo, bo, s2_w, s2_b, b2_w, b2_b, m_w1, m_b1, m_w2, m_b2)

    def _L1_gnn_ref(x, edge_index, edge_type, basis1, att1, gate_w1, root1, bias1, basis2, att2, gate_w2, root2, bias2):
        import jax, jax.numpy as jnp
        import numpy as np
        NUM_RELATIONS = 2
        NUM_BASES = 30
        HIDDEN = 512
        N_NODES = 1250
        N_EDGES = 20000

        def rgcn_gate_layer(x, row, col, edge_type, basis, att, gate_w, root, bias):
            H = x.shape[1]
            w = jnp.einsum('rb,bio->rio', att, basis)
            x_j = x[col]
            msgs = []
            for r in range(NUM_RELATIONS):
                gate = jax.nn.sigmoid(x_j @ gate_w[r, :, 0])
                msgs.append(gate[:, None] * x_j @ w[r])
            msg = jnp.where((edge_type == 0)[:, None], msgs[0], msgs[1])
            agg = jax.ops.segment_sum(msg, row, num_segments=x.shape[0])
            return agg + x @ root + bias
        row, col = (edge_index[0], edge_index[1])
        h = jax.nn.relu(rgcn_gate_layer(x, row, col, edge_type, basis1, att1, gate_w1, root1, bias1))
        out = rgcn_gate_layer(h, row, col, edge_type, basis2, att2, gate_w2, root2, bias2)
        return out
    edge_index = jnp.stack([src, dst])
    h = jnp.maximum(_layernorm(x, axis=-1), 0.0)
    x = x + _L0_gnn_ref(h, edge_index, node_vec1, L0_gnn_f_w1, L0_gnn_f_b1, L0_gnn_f_w2, L0_gnn_f_b2, L0_gnn_s1_w, L0_gnn_s1_b, L0_gnn_b1_w, L0_gnn_b1_b, L0_gnn_wq, L0_gnn_bq, L0_gnn_wk, L0_gnn_bk, L0_gnn_wv, L0_gnn_bv, L0_gnn_wo, L0_gnn_bo, L0_gnn_s2_w, L0_gnn_s2_b, L0_gnn_b2_w, L0_gnn_b2_b, L0_gnn_m_w1, L0_gnn_m_b1, L0_gnn_m_w2, L0_gnn_m_b2)
    h = jnp.maximum(_layernorm(x, axis=-1), 0.0)
    x = x + _L1_gnn_ref(h, edge_index, edge_type_2, L1_gnn_basis1, L1_gnn_att1, L1_gnn_gate_w1, L1_gnn_root1, L1_gnn_bias1, L1_gnn_basis2, L1_gnn_att2, L1_gnn_gate_w2, L1_gnn_root2, L1_gnn_bias2)
    return x

_drawn_inputs = setup_inputs


def setup_inputs(seed=0):
    import zlib

    import numpy as np

    out = dict(_drawn_inputs(seed))
    spreads = {'L0_gnn_f_b1': (0.0, 0.8),
     'L0_gnn_f_b2': (0.0, 0.8),
     'L0_gnn_s1_b': (0.0, 0.737),
     'L0_gnn_b1_b': (0.0, 0.288),
     'L0_gnn_bq': (0.0, 0.8),
     'L0_gnn_bk': (0.0, 2.0),
     'L0_gnn_bv': (0.0, 0.1),
     'L0_gnn_bo': (0.0, 0.1),
     'L0_gnn_s2_b': (0.0, 0.448),
     'L0_gnn_b2_b': (0.0, 0.431),
     'L0_gnn_m_b1': (0.0, 0.1),
     'L0_gnn_m_b2': (0.0, 0.1)}
    factors = {'node_vec1': 8.0,
     'L0_gnn_f_w1': 8.0,
     'L0_gnn_f_w2': 8.0,
     'L0_gnn_s1_w': 8.0,
     'L0_gnn_b1_w': 8.0,
     'L0_gnn_wq': 4.504,
     'L0_gnn_wk': 4.368,
     'L0_gnn_s2_w': 8.0,
     'L0_gnn_b2_w': 8.0,
     'L1_gnn_basis1': 8.0,
     'L1_gnn_att1': 8.0,
     'L1_gnn_gate_w1': 8.0,
     'L1_gnn_root1': 8.0,
     'L1_gnn_bias1': 24.634,
     'L1_gnn_basis2': 8.0,
     'L1_gnn_att2': 8.0,
     'L1_gnn_gate_w2': 23.222,
     'L1_gnn_root2': 8.0,
     'L1_gnn_bias2': 23.325}
    for name, (base, spread) in spreads.items():
        noise = np.random.default_rng([zlib.crc32(name.encode()), seed]).standard_normal(out[name].shape)
        drawn = base * np.exp(spread * noise) if base else spread * noise
        out[name] = jnp.asarray(drawn.astype(out[name].dtype))
    for name, factor in factors.items():
        out[name] = (out[name] * factor).astype(out[name].dtype)
    return out
```

```python
import math
import concourse.bass as bass
from concourse import mybir
from contextlib import ExitStack



def gnn_kernel(nc, x_in, src, dst, edge_type, noise,
               f_w1, f_b1, f_w2, f_b2, s1_w, s1_b, b1_w, b1_b, wq, bq, wk, bk, wv, bv, wo, bo,
               s2_w, s2_b, b2_w, b2_b, m_w1, m_b1, m_w2, m_b2,
               basis1, att1, gate_w1, root1, bias1, basis2, att2, gate_w2, root2, bias2, out,
               edge_table, x_lat, score_bias, adj_hi_dram, adj_lo_dram, rel_w, h_rgcn):
    fp32, f32r, bf16, f16 = mybir.dt.float32, mybir.dt.float32r, mybir.dt.bfloat16, mybir.dt.float16
    i32, i16 = mybir.dt.int32, mybir.dt.int16
    ALU, ACT, AX = mybir.AluOpType, mybir.ActivationFunctionType, mybir.AxisListType

    N, D = x_in.shape
    E = src.shape[0]
    T = 125
    NT = N // T
    W = 2 * T
    NP = N // W
    LAYERS = wq.shape[0]
    C = f_w2.shape[0]
    F2 = f_w1.shape[0]
    H = D // 128
    SW = 1254
    SB = SW // 3
    EPS = 1e-5
    SCALE = 128.0 ** -0.5
    NONE = -1e30
    MAGIC = 1.5 * 2 ** 23
    EC = -(-E // 128)
    NB = 2 * NT
    GE = 256
    NG = (EC * 128 + NB * (GE - 1)) // GE
    TC = NG * GE // 128
    R, B = att1.shape
    QL = 8
    Q = D // 4

    ctx = ExitStack()
    with ctx:
        def sb(name, shape, dt=fp32):
            return ctx.enter_context(nc.sbuf_tensor(name, shape, dt))

        ident = sb("ident", [128, 128])
        ones_r = sb("ones_r", [128, 128], f32r)
        neg_half = sb("neg_half", [128, 2])
        bn = sb("bn", [128, 2, 6])
        mv = sb("mv", [128, 2, 4])
        var_eps = sb("var_eps", [128, 2, 2])
        rstd = sb("rstd", [128, 2, 2])
        cols_all = sb("cols_all", [128, 4, LAYERS * H])
        rows_all = sb("rows_all", [4 * LAYERS * H, 128])
        bq_col = sb("bq_col", [128, H])
        bk_col = sb("bk_col", [128, H])
        b1_col = sb("b1_col", [128, H])
        row_max = sb("row_max", [128, 4])
        neg_max = sb("neg_max", [128, 4])
        den = sb("den", [128, 4])
        has_edge = sb("has_edge", [128, 4])
        inv_den = sb("inv_den", [128, 4])
        wait_slot = sb("wait_slot", [1, 1])
        pool_slot = sb("pool_slot", [1, 9])
        gate_sb = sb("gate_sb", [128, 2, R])

        BASE = (nc.sbuf_base + 63) // 64 * 64
        END = nc.sbuf_usable_end

        class Map:
            def __init__(self, at):
                self.at = at

            def __call__(self, name, shape, dt=fp32):
                size = 2 if dt in (bf16, f16, i16) else 4
                for n in shape[1:]:
                    size *= n
                t = nc.alloc_sbuf_tensor_at(name, shape, dt, offset=self.at)
                self.at += (size + 31) // 32 * 32
                assert self.at <= END, (name, self.at, END)
                return t

        m = Map(BASE)
        k_hi = m("k_hi", [128, H, SW], f32r)
        k_lo = m("k_lo", [128, H, SW], f32r)
        v_hi = m("v_hi", [T, NT, D], f32r)
        v_lo = m("v_lo", [T, NT, D], f32r)
        q_raw = m("q_raw", [128, H, N])
        SCRATCH0 = m.at
        cond3 = m("cond3", [96, N], f32r)
        SCRATCH = m.at

        m = Map(SCRATCH)
        wk_hi, wk_lo = m("wk_hi", [128, 4, D], f32r), m("wk_lo", [128, 4, D], f32r)
        wq_hi, wq_lo = m("wq_hi", [128, 4, D], f32r), m("wq_lo", [128, 4, D], f32r)
        wv_hi, wv_lo = m("wv_hi", [128, 4, D], f32r), m("wv_lo", [128, 4, D], f32r)
        w_raw = m("w_raw", [128, 4, D])
        mod3 = [m("scale3", [96, D], f32r), m("bias3", [96, D], f32r)]
        mod_raw = [m("scale_raw", [17, D]), m("bias_raw", [17, D])]
        bv3 = m("bv3", [128, D], f32r)
        bv_raw = m("bv_raw", [1, D])
        xt = [m(f"xt{i}", [T, 2, D]) for i in range(2)]
        yt = [m(f"yt{i}", [T, 2, D]) for i in range(2)]
        yT_hi = [m(f"yT_hi{i}", [128, 4, W], f32r) for i in range(2)]
        yT_lo = [m(f"yT_lo{i}", [128, 4, W], f32r) for i in range(2)]

        m = Map(SCRATCH)
        q_hi = m("q_hi", [128, H, W], f32r)
        q_lo = m("q_lo", [128, H, W], f32r)
        pT_hi = [m(f"pT_hi{i}", [T, NT, W], f32r) for i in range(2)]
        pT_lo = [m(f"pT_lo{i}", [T, NT, W], f32r) for i in range(2)]
        prob = [m(f"prob{i}", [T, SW]) for i in range(3)]
        sbias = [[m(f"sbias{i}{a}", [T, SW]) for a in range(2)] for i in range(2)]

        m = Map(BASE)
        wo_hi, wo_lo = m("wo_hi", [128, 4, D], f32r), m("wo_lo", [128, 4, D], f32r)
        w1_hi, w1_lo = m("w1_hi", [128, 4, D], f32r), m("w1_lo", [128, 4, D], f32r)
        w2_hi, w2_lo = m("w2_hi", [128, 4, D], f32r), m("w2_lo", [128, 4, D], f32r)
        bo3, b23 = m("bo3", [128, D], f32r), m("b23", [128, D], f32r)
        row_raw = m("row_raw", [1, 2, D])
        assert m.at <= SCRATCH0 - 20000
        m = Map(SCRATCH)
        w_raw3 = m("w_raw3", [128, 4, D])
        mod3b = [m("scale3b", [96, D], f32r), m("bias3b", [96, D], f32r)]
        mod_rawb = [m("scale_rawb", [17, D]), m("bias_rawb", [17, D])]
        oT_hi = [m(f"oT_hi{i}", [128, 4, W], f32r) for i in range(2)]
        oT_lo = [m(f"oT_lo{i}", [128, 4, W], f32r) for i in range(2)]
        xm = [m(f"xm{i}", [T, 2, D]) for i in range(2)]
        ym = [m(f"ym{i}", [T, 2, D]) for i in range(2)]
        zT_hi = m("zT_hi", [128, 4, W], f32r)
        zT_lo = m("zT_lo", [128, 4, W], f32r)
        hT = m("hT", [128, 4, W])
        hT_hi = m("hT_hi", [128, 4, W], f32r)
        hT_lo = m("hT_lo", [128, 4, W], f32r)

        m = Map(BASE)
        msg_hi = [m(f"msg_hi{r}", [T, NT, D], f32r) for r in range(R)]
        msg_lo = [m(f"msg_lo{r}", [T, NT, D], f32r) for r in range(R)]
        self_term = m("self_term", [T, NT, D])
        wr_hi = [m(f"wr_hi{i}", [128, 4, D], f32r) for i in range(3)]
        wr_lo = [m(f"wr_lo{i}", [128, 4, D], f32r) for i in range(3)]
        RG = m.at
        w_rawr = m("w_rawr", [128, 4, D])
        rb3 = m("rb3", [128, D], f32r)
        rb_raw = m("rb_raw", [1, D])
        gw_hl = m("gw_hl", [128, 4, 2 * R], f32r)
        xr = m("xr", [T, 2, D])
        lr = m("lr", [T, 2, D])
        yr = m("yr", [T, 2, D])
        rT_hi = m("rT_hi", [128, 4, W], f32r)
        rT_lo = m("rT_lo", [128, 4, W], f32r)
        m = Map(RG)
        adj_hi = [m(f"adj_hi{i}", [T, NB, T], f32r) for i in range(2)]
        adj_lo = [m(f"adj_lo{i}", [T, NB, T], f32r) for i in range(1)]
        res = [m(f"res{i}", [T, D]) for i in range(2)]
        xres = m("xres", [T, D])

        m = Map(BASE)
        src_i, dst_i, typ_i = m("src_i", [128, EC], i32), m("dst_i", [128, EC], i32), m("typ_i", [128, EC], i32)
        dst_f, typ_f, tile_f = m("dst_f", [128, EC]), m("typ_f", [128, EC]), m("tile_f", [128, EC])
        bucket = m("bucket", [128, EC])
        bucket_id = m("bucket_id", [128, NB])
        mask = m("mask", [128, NB, EC], bf16)
        lower = m("lower", [128, 128], bf16)
        ones_b = m("ones_b", [128, 128], bf16)
        rank = m("rank", [128, NB, EC])
        tot = m("tot", [128, NB, EC])
        pre = [m(f"pre{i}", [128, NB, EC]) for i in range(2)]
        grp = m("grp", [128, NB])
        gpre = [m(f"gpre{i}", [128, NB]) for i in range(2)]
        pos = m("pos", [128, EC])
        pos_hi = m("pos_hi", [128, EC])
        row_i = m("row_i", [128, EC], i32)
        payload = m("payload", [128, EC, 2])
        empty = m("empty", [128, TC * 2])
        group_no = m("group_no", [1, NG])
        group_ge = m("group_ge", [1, NG, NB])
        ph = m("ph", [F2, N])
        ph_int = m("ph_int", [F2, N])
        freq_off = m("freq_off", [F2, 2])
        freq_i = m("freq_i", [F2, 1])
        fw1 = m("fw1", [F2, C])
        fw2 = m("fw2", [C, C])
        fb = m("fb", [C, 4])
        z1 = m("z1", [C, N])
        z2 = m("z2", [C, N])
        assert m.at <= SCRATCH0
        m = Map(SCRATCH)
        group_tile = m("group_tile", [1, NG], i32)
        table = m("table", [128, TC, 2])
        basis_t = [m(f"basis_t{i}", [4 * B, QL, D]) for i in range(3)]
        att_z = [m(f"att_z{l}", [4 * B, 15 + 128]) for l in range(2)]
        w_out = [m(f"w_out{i}", [128, D]) for i in range(2)]
        x0 = [m(f"x0{i}", [T, 2, D]) for i in range(2)]
        y0 = [m(f"y0{i}", [T, 2, D]) for i in range(2)]
        m = Map(BASE)
        count = m("count", [T, NB, SW], i16)
        node_no = m("node_no", [128, SW], f16)
        src_hot = [m(f"src_hot{i}", [128, 2, SW], bf16) for i in range(2)]
        dst_hot = [m(f"dst_hot{i}", [128, 2, 128], bf16) for i in range(2)]
        csum = m("csum", [T, NT, T])
        cnt1 = m("cnt1", [T, SW])
        cnt0 = m("cnt0", [T, SW])
        c_hi = m("c_hi", [T, NB, T], f32r)
        c_lo = m("c_lo", [T, NB, T], f32r)
        assert m.at <= SCRATCH0

        PS = ctx.enter_context(nc.psum_tensor("PS", [128, 8, 512], fp32))

        class Signal:

            def __init__(self, name, setup=0, layer=0, unit=1):
                self.sem = ctx.enter_context(nc.semaphore(name))
                self.setup, self.layer, self.unit = setup, layer, unit

        def value(s, where, i):
            if isinstance(where, str):
                return ({"setup": 0, "final": s.setup + LAYERS * s.layer}[where] + i + 1) * s.unit
            return where * (s.layer * s.unit) + (s.setup + i + 1) * s.unit

        def wait(eng, s, where, i):
            eng.wait_ge(s.sem, value(s, where, i))

        pe_end = Signal("pe_end", 3, 3)
        act_end = Signal("act_end", 3, 3)
        dve_end = Signal("dve_end", 3, 3)
        pool_end = Signal("pool_end", 3, 3)
        ENDS = (pe_end, act_end, dve_end, pool_end)

        def phase_begins(eng, where, i):
            for s in ENDS:
                wait(eng, s, where, i)

        x_loaded = [Signal(f"x_loaded{i}", (3, 2)[i], (6, 4)[i], 16) for i in range(2)]
        var_ready = Signal("var_ready", 5, 10)
        rstd_ready = Signal("rstd_ready", 5, 10)
        x_used = Signal("x_used", 5, 10)
        chain = Signal("chain", 56, 91)
        const_ready = Signal("const_ready")
        mod_raw_in = Signal("mod_raw_in", 0, 2, 64)
        mod_ready = Signal("mod_ready", 0, 2)
        mod_ps = Signal("mod_ps", 0, 20)
        y_ready = Signal("y_ready", 0, 20)
        yT_ps = Signal("yT_ps", 0, 20)
        yT_hi_done = Signal("yT_hi_done", 0, 20)
        yT_lo_done = Signal("yT_lo_done", 0, 20)
        w_in = Signal("w_in", 0, 6, 16)
        w_hi_done = Signal("w_hi_done", 0, 6)
        w_lo_done = Signal("w_lo_done", 0, 6)
        cols_ready = Signal("cols_ready", 0, 1)
        rows_in = Signal("rows_in", 0, 3, 16)
        rows_ready_l = Signal("rows_ready_l", 0, 2)
        k_ps = Signal("k_ps", 0, 20)
        q_ps = Signal("q_ps", 0, 20)
        v_ps = Signal("v_ps", 0, 10)
        k_hi_done = Signal("k_hi_done", 0, 20)
        k_lo_done = Signal("k_lo_done", 0, 20)
        q_done = Signal("q_done", 0, 20)
        v_hi_done = Signal("v_hi_done", 0, 10)
        v_lo_done = Signal("v_lo_done", 0, 10)
        sbias_in = [Signal(f"sbias_in{i}{a}", 0, 3 - i, 16) for i in range(2) for a in range(2)]
        q_hi_done = Signal("q_hi_done", 0, 20)
        q_lo_done = Signal("q_lo_done", 0, 20)
        s_ps = Signal("s_ps", 0, 40)
        masked = Signal("masked", 0, 40)
        negmax_ready = Signal("negmax_ready", 0, 40)
        exp_done = Signal("exp_done", 0, 40)
        inv_ready = Signal("inv_ready", 0, 40)
        normed = Signal("normed", 0, 40)
        pT_ps = Signal("pT_ps", 0, 40)
        pT_hi_done = Signal("pT_hi_done", 0, 40)
        pT_lo_done = Signal("pT_lo_done", 0, 40)
        o_ps = Signal("o_ps", 0, 20)
        o_done = Signal("o_done", 0, 20)
        oT_hi_done = Signal("oT_hi_done", 0, 5)
        oT_lo_done = Signal("oT_lo_done", 0, 5)
        wo_ps = Signal("wo_ps", 0, 10)
        x_added = Signal("x_added", 0, 10)
        w1_ps = Signal("w1_ps", 0, 20)
        h_done = Signal("h_done", 0, 20)
        h_hi_done = Signal("h_hi_done", 0, 5)
        h_lo_done = Signal("h_lo_done", 0, 5)
        w2_ps = Signal("w2_ps", 0, 10)
        x_done = Signal("x_done", 0, 10)
        x_stored = [Signal(f"x_stored{i}", (3, 2)[i], (3, 2)[i], 16) for i in range(2)]

        def plain(name):
            return ctx.enter_context(nc.semaphore(name))

        (consts, edges_in, noise_in, fw_in, att_in, sp_passed, bias_cols_ps, table_filled, table_in, h0_ready, adj_stored,
         sbias_stored) = map(plain, (
             "consts", "edges_in", "noise_in", "fw_in", "att_in", "sp_passed", "bias_cols_ps", "table_filled", "table_in", "h0_ready",
             "adj_stored", "sbias_stored"))
        (edge_pads, empty_ready, mask_ready, rank_ps, rank_out, tot_out, rows_ready, scattered, freq_ready,
         phase_ready, sin_done, z1_ps, z1_exp, silu_done, z2_ps, cond_ready, basis_ps, basis_out,
         basis_used, att_zeroed) = map(plain, (
             "edge_pads", "empty_ready", "mask_ready", "rank_ps", "rank_out", "tot_out", "rows_ready",
             "scattered", "freq_ready", "phase_ready", "sin_done", "z1_ps", "z1_exp", "silu_done", "z2_ps",
             "cond_ready", "basis_ps", "basis_out", "basis_used", "att_zeroed"))
        basis_in = [plain(f"basis_in{i}") for i in range(3)]
        w_stored = [plain(f"w_stored{i}") for i in range(2)]
        (hot_ready, count_ps, count_added, node_no_ready, csum_ready, csumT_ps, cnt1_ready, ln_done, sbias_ready,
         adj_hi_done, adj_lo_done) = map(plain, (
             "hot_ready", "count_ps", "count_added", "node_no_ready", "csum_ready", "csumT_ps", "cnt1_ready", "ln_done",
             "sbias_ready", "adj_hi_done", "adj_lo_done"))
        (r_small_in, r_rows_ready, r_w_in, r_w_hi, r_w_lo, r_x_in, r_h_in, r_x1_ready, r_x1_stored, r_h_ready,
         r_hT_ps, r_hT_hi, r_hT_lo, r_gate_ps, r_gate_exp, r_gate, r_mm_ps, r_m_hi, r_m_lo, r_self_out,
         r_agg_ps, r_res_ready, r_xres_in, r_adj_lo_in) = map(plain, (
             "r_small_in", "r_rows_ready", "r_w_in", "r_w_hi", "r_w_lo", "r_x_in", "r_h_in", "r_x1_ready",
             "r_x1_stored", "r_h_ready", "r_hT_ps", "r_hT_hi", "r_hT_lo", "r_gate_ps", "r_gate_exp", "r_gate",
             "r_mm_ps", "r_m_hi", "r_m_lo", "r_self_out", "r_agg_ps", "r_res_ready", "r_xres_in",
             "r_adj_lo_in"))
        r_out_stored = [plain(f"r_out_stored{i}") for i in range(2)]
        r_adj_hi_in = [plain(f"r_adj_hi_in{i}") for i in range(2)]
        r_end = [plain(f"r_end_{e}") for e in ("pe", "act", "dve")]

        block = ctx.enter_context(nc.Block())

        QKV_GROUPS = []
        for p in range(NP):
            QKV_GROUPS += [(k_lo_done, 4 * p + c) for c in range(4)]
            QKV_GROUPS += [(q_done, 4 * p + c) for c in range(4)]
            QKV_GROUPS += [(v_lo_done, 2 * p + a) for a in range(2)]
        MLP_GROUPS = [(x_added, 0), (x_added, 1)]
        for p in range(NP):
            if p + 1 < NP:
                MLP_GROUPS += [(x_added, 2 * p + 2), (x_added, 2 * p + 3)]
            MLP_GROUPS += [(h_done, 4 * p + c) for c in range(4)]
            MLP_GROUPS += [(x_done, 2 * p), (x_done, 2 * p + 1)]

        def bank_of(groups, s, i):
            return 4 + groups.index((s, i)) % 4

        def bank_free(eng, groups, s, i, lay):
            n = groups.index((s, i))
            if n >= 4:
                wait(eng, groups[n - 4][0], lay, groups[n - 4][1])

        RC = 2 * EC
        NRC = NB * EC // RC
        CH = ((0, 418), (418, 416), (834, 416))
        NW = 2 * (Q // 16)
        NL = 2 * (Q // QL)

        def pair_rows(a, p):
            return a[W * p:W * (p + 1), :].rearrange("(a t) d -> t a d", t=T)

        @block.sync
        def _(sp):
            sp.wait_ge(edge_pads, 3)
            full = E // EC
            for t, a in ((src_i, src), (dst_i, dst), (typ_i, edge_type)):
                sp.dma_start(t[0:full, :], a[0:full * EC].rearrange("(p c) -> p c", c=EC)).then_inc(edges_in, 16)
                sp.dma_start(t[full:full + 1, 0:E - full * EC],
                             a[full * EC:E].rearrange("(p c) -> p c", p=1)).then_inc(edges_in, 16)
            sp.dma_start(ph[:], noise.rearrange("n a -> (a n)").partition_broadcast(F2)).then_inc(noise_in, 16)
            sp.dma_start(fw1[:], f_w1).then_inc(fw_in, 16)
            sp.dma_start(fw2[:], f_w2).then_inc(fw_in, 16)
            sp.dma_start(fb[:, 0:1], f_b1.rearrange("(p a) -> p a", a=1)).then_inc(fw_in, 16)
            sp.dma_start(fb[:, 1:2], f_b2.rearrange("(p a) -> p a", a=1)).then_inc(fw_in, 16)
            for b, a in enumerate((bk, bq, m_b1)):
                sp.dma_start(rows_all[LAYERS * H * b:LAYERS * H * (b + 1), :],
                             a.rearrange("l (c p) -> (l c) p", p=128)).then_inc(fw_in, 16)
            for l, a in enumerate((gate_w1, gate_w2)):
                r0 = 4 * LAYERS * H - 2 * R * 4 + R * 4 * l
                sp.dma_start(rows_all[r0:r0 + R * 4, :],
                             a.rearrange("r (c p) a -> (r c) (p a)", p=128)).then_inc(fw_in, 16)
            sp.wait_ge(att_zeroed, 2)
            for l, att in enumerate((att1, att2)):
                for r in range(R):
                    for ii in range(4):
                        col = 15 + 64 * r + 16 * ii
                        sp.dma_start(att_z[l][ii * B:(ii + 1) * B, col:col + 1],
                                     att[r, :].rearrange("(b a) -> b a", a=1)).then_inc(att_in, 16)
            sp.wait_ge(empty_ready, 1)
            sp.dma_start(edge_table.rearrange("(p c) k -> p (c k)", c=TC), empty[:]).then_inc(table_filled, 16)
            for n in range(NL):
                l, q0 = divmod(n * QL, Q)
                if n >= 3:
                    sp.wait_ge(basis_used, n - 2)
                rows = (basis1, basis2)[l].rearrange("b (i q) d -> i b q d", q=Q)
                for ii in range(4):
                    sp.dma_start(basis_t[n % 3][ii * B:(ii + 1) * B, :, :], rows[ii, :, q0:q0 + QL, :])\
                        .then_inc(basis_in[n % 3], 16)
            sp.wait_ge(scattered, 16 * EC)
            sp.dma_start(table[:].rearrange("p c k -> p (c k)"),
                         edge_table.rearrange("(p c) k -> p (c k)", c=TC)).then_inc(table_in, 16)
            for t in range(NT):
                sp.wait_ge(adj_hi_done, t + 1)
                sp.dma_start(adj_hi_dram[t, :, :, :], c_hi[:].bitcast(fp32)).then_inc(adj_stored, 16)
                sp.wait_ge(adj_lo_done, t + 1)
                sp.dma_start(adj_lo_dram[t, :, :, :], c_lo[:].bitcast(fp32)).then_inc(adj_stored, 16)
                sp.wait_ge(sbias_ready, t + 1)
                sp.dma_start(score_bias[t, :, :], cnt0[:]).then_inc(sbias_stored, 16)

            sp.wait_ge(sbias_stored, 16 * NT)

            with sp.Fori(0, LAYERS) as lay:
                def load_mods(tiles, pair):
                    for t, (w, b) in zip(tiles, pair):
                        sp.dma_start(t[0:C, :], w[bass.ds(lay, 1), :, :].rearrange("a p d -> (a p) d"))\
                            .then_inc(mod_raw_in.sem, 16)
                        sp.dma_start(t[C:C + 1, :], b[bass.ds(lay, 1), :]).then_inc(mod_raw_in.sem, 16)

                def load_w(tile, w, n):
                    if n % 3:
                        wait(sp, w_lo_done, lay, n - 1)
                        sp.sem_inc(sp_passed, 1)
                    sp.dma_start(tile[:], w[bass.ds(lay, 1), :, :].rearrange("a (c p) d -> p (a c) d", p=128))\
                        .then_inc(w_in.sem, 16)

                def load_x(tiles, p):
                    sp.dma_start(tiles[p % 2][:], pair_rows(x_lat, p)).then_inc(x_loaded[p % 2].sem, 16)

                phase_begins(sp, lay, -1)
                for p in range(2):
                    wait(sp, x_stored[p], lay, -1)
                    sp.sem_inc(sp_passed, 1)
                for p in range(2):
                    load_x(xt, p)
                load_mods(mod_raw, ((s1_w, s1_b), (b1_w, b1_b)))
                sp.dma_start(bv_raw[:], bv[bass.ds(lay, 1), :]).then_inc(rows_in.sem, 16)
                for n, w in enumerate((wk, wq, wv)):
                    load_w(w_raw, w, n)
                for p in range(2, NP):
                    wait(sp, x_used, lay, p - 2)
                    load_x(xt, p)

                phase_begins(sp, lay, 0)
                for p in range(NP):
                    for a in range(2):
                        if p >= 2:
                            wait(sp, masked, lay, 8 * (p - 2) + 6 + a)
                        sp.dma_start(sbias[p % 2][a][:], score_bias[2 * p + a, :, :])\
                            .then_inc(sbias_in[2 * (p % 2) + a].sem, 16)

                phase_begins(sp, lay, 1)
                sp.dma_start(row_raw[0:1, 0, :], bo[bass.ds(lay, 1), :]).then_inc(rows_in.sem, 16)
                sp.dma_start(row_raw[0:1, 1, :], m_b2[bass.ds(lay, 1), :]).then_inc(rows_in.sem, 16)
                load_w(w_raw3, wo, 3)
                load_x(xm, 0)
                load_x(xm, 1)
                load_mods(mod_rawb, ((s2_w, s2_b), (b2_w, b2_b)))
                load_w(w_raw3, m_w1, 4)
                load_w(w_raw3, m_w2, 5)
                for p in range(NP):
                    wait(sp, x_done, lay, 2 * p + 1)
                    sp.dma_start(pair_rows(x_lat, p), xm[p % 2][:]).then_inc(x_stored[p % 2].sem, 16)
                    if p + 2 < NP:
                        wait(sp, x_stored[p % 2], lay, p // 2)
                        load_x(xm, p + 2)

            phase_begins(sp, "final", -1)
            wait(sp, x_stored[0], "final", -1)
            wait(sp, x_stored[1], "final", -1)
            for l, (root, bias) in enumerate(((root1, bias1), (root2, bias2))):
                if l:
                    for s in r_end:
                        sp.wait_ge(s, 2)
                    for i in range(2):
                        sp.wait_ge(r_out_stored[i], 16 * NT // 2)
                sp.dma_start(rb_raw[:], bias.rearrange("(a n) -> a n", a=1)).then_inc(r_small_in, 16)
                for n, w in enumerate((rel_w[l, 0, :, :], rel_w[l, 1, :, :], root)):
                    if n:
                        sp.wait_ge(r_w_lo, 3 * l + n)
                    sp.dma_start(w_rawr[:], w.rearrange("(c p) d -> p c d", p=128)).then_inc(r_w_in, 16)
                for p in range(NP):
                    if l == 0:
                        if p:
                            sp.wait_ge(r_x1_stored, 16 * p)
                        sp.dma_start(xr[:], pair_rows(x_in, p)).then_inc(r_x_in, 16)
                        sp.dma_start(lr[:], pair_rows(x_lat, p)).then_inc(r_x_in, 16)
                        sp.wait_ge(r_x1_ready, p + 1)
                        if p:
                            sp.wait_ge(r_h_ready, p)
                        sp.dma_start(pair_rows(x_lat, p), xr[:]).then_inc(r_x1_stored, 16)
                        sp.wait_ge(r_h_ready, p + 1)
                    else:
                        if p:
                            sp.wait_ge(r_hT_ps, 2 * (NP + p))
                        sp.dma_start(yr[:], pair_rows(h_rgcn, p)).then_inc(r_h_in, 16)
                for s in r_end:
                    sp.wait_ge(s, 2 * l + 1)
                sp.wait_ge(adj_stored, 2 * 16 * NT)
                sp.wait_ge(r_x1_stored, 16 * NP)
                for t in range(NT):
                    n = NT * l + t
                    if t >= 2:
                        sp.wait_ge(r_agg_ps, n - 1)
                    sp.dma_start(adj_hi[t % 2][:].bitcast(fp32), adj_hi_dram[t, :, :, :]).then_inc(r_adj_hi_in[t % 2], 16)
                    if t >= 1:
                        sp.wait_ge(r_agg_ps, n)
                    sp.dma_start(adj_lo[0][:].bitcast(fp32), adj_lo_dram[t, :, :, :]).then_inc(r_adj_lo_in, 16)
                    if l:
                        if t >= 1:
                            sp.wait_ge(r_res_ready, n)
                        sp.dma_start(xres[:], x_lat[T * t:T * (t + 1), :]).then_inc(r_xres_in, 16)
                    if t >= 1:
                        sp.wait_ge(r_res_ready, n)
                        sp.dma_start((h_rgcn, out)[l][T * (t - 1):T * t, :], res[(t - 1) % 2][:]).then_inc(r_out_stored[(t - 1) % 2], 16)
                sp.wait_ge(r_res_ready, NT * (l + 1))
                sp.dma_start((h_rgcn, out)[l][T * (NT - 1):, :], res[(NT - 1) % 2][:]).then_inc(r_out_stored[(NT - 1) % 2], 16)
            for i in range(2):
                sp.wait_ge(r_out_stored[i], 16 * NT)

        @block.gpsimd
        def _(pool):
            pool.memset(src_i[:], -1).then_inc(edge_pads, 1)
            pool.memset(dst_i[:], 0).then_inc(edge_pads, 1)
            pool.memset(typ_i[:], 0).then_inc(edge_pads, 1)
            for l in range(2):
                pool.memset(att_z[l][:], 0.0).then_inc(att_zeroed, 1)
            pool.memset(pool_slot[:], 0.0)
            pool.memset(neg_half[:], -0.5).then_inc(consts, 1)
            pool.memset(empty[:], -1.0).then_inc(empty_ready, 1)
            pool.iota(freq_i[:].bitcast(i32), [[0, 1]], base=0, channel_multiplier=1).then_inc(freq_ready, 1)
            pool.memset(lower[:], 1.0).then_inc(consts, 1)
            pool.memset(ones_b[:], 1.0).then_inc(consts, 1)
            pool.memset(ident[:], 0.0).then_inc(consts, 1)
            pool.wait_ge(consts, 4)
            pool.affine_select(out=lower[:], in_=lower[:], compare_op=ALU.is_gt, fill=0.0, base=0,
                               pattern=[[1, 128]], channel_multiplier=-1).then_inc(consts, 1)
            pool.affine_select(out=ident[:], in_=ident[:], compare_op=ALU.not_equal, fill=1.0, base=0,
                               pattern=[[-1, 128]], channel_multiplier=1).then_inc(consts, 1)
            pool.iota(bucket_id[:], [[1, NB]], base=0, channel_multiplier=0,
                      allow_small_or_imprecise_dtypes=True).then_inc(consts, 1)
            pool.iota(group_no[:], [[1, NG]], base=0, channel_multiplier=0,
                      allow_small_or_imprecise_dtypes=True).then_inc(consts, 1)

            def inv_std(where, i):
                s = i % 2
                wait(pool, var_ready, where, i)
                pool.tensor_tensor(rstd[0:T, s, :], var_eps[0:T, s, :], neg_half[0:T, :], ALU.pow)\
                    .then_inc(rstd_ready.sem, 1)

            for p in range(NP):
                inv_std("setup", p)
            pool.wait_ge(rows_ready, 1)
            pool.wait_ge(table_filled, 16)
            for c in range(EC):
                pool.indirect_dma_start(edge_table, bass.IndirectOffsetOnAxis(ap=row_i[:, c:c + 1], axis=0),
                                        payload[:, c, :], None).then_inc(scattered, 16)
            pool.drain().then_inc(pool_end.sem, 1)
            phase_begins(pool, "setup", 0)
            pool.iota(node_no[:], [[1, SW]], base=0, channel_multiplier=0,
                      allow_small_or_imprecise_dtypes=True).then_inc(node_no_ready, 1)
            pool.drain().then_inc(pool_end.sem, 1)
            phase_begins(pool, "setup", 1)
            pool.drain().then_inc(pool_end.sem, 1)

            with pool.Fori(0, LAYERS) as lay:
                phase_begins(pool, lay, -1)
                for p in range(NP):
                    inv_std(lay, p)
                pool.drain().then_inc(pool_end.sem, 1)
                phase_begins(pool, lay, 0)
                for u in range(8 * NP):
                    wait(pool, inv_ready, lay, u)
                    pool.tensor_tensor(pool_slot[0:1, 1 + u % 8:2 + u % 8], pool_slot[0:1, 0:1], pool_slot[0:1, 0:1], ALU.mult)
                    pool.tensor_scalar(prob[u % 3][:], prob[u % 3][:], inv_den[0:T, u % 4:u % 4 + 1], None, ALU.mult)\
                        .then_inc(normed.sem, 1)
                pool.drain().then_inc(pool_end.sem, 1)
                phase_begins(pool, lay, 1)
                for p in range(NP):
                    inv_std(lay, NP + p)
                pool.drain().then_inc(pool_end.sem, 1)

            phase_begins(pool, "final", -1)
            for p in range(NP):
                inv_std("final", p)

        @block.tensor
        def _(pe):
            pe.wait_ge(consts, 6)
            pe.wait_ge(mask_ready, 1)
            mask_f = mask[:].rearrange("p k c -> p (k c)")
            for c in range(NRC):
                if c >= 2:
                    pe.wait_ge(rank_out, c - 1)
                    pe.wait_ge(tot_out, c - 1)
                cols = mask_f[:, c * RC:(c + 1) * RC]
                pe.matmul(PS[:, c % 2, 0:RC], lower[:], cols, start=True, stop=True)
                pe.matmul(PS[:, 2 + c % 2, 0:RC], ones_b[:], cols, start=True, stop=True).then_inc(rank_ps, 1)
            pe.wait_ge(fw_in, 16 * 9)
            pe.transpose(PS[:, 7, 0:4 * LAYERS * H], rows_all[:], ident[0:4 * LAYERS * H, 0:4 * LAYERS * H])\
                .then_inc(bias_cols_ps, 1)
            pe.wait_ge(sin_done, 1)
            for j, (c0, cn) in enumerate(CH):
                z = pe.matmul(PS[0:C, 4 + j, 0:cn], fw1[:], ph[:, c0:c0 + cn], start=True, stop=True)
            z.then_inc(z1_ps, 1)
            pe.wait_ge(silu_done, 1)
            for j, (c0, cn) in enumerate(CH):
                z = pe.matmul(PS[0:C, 4 + j, 0:cn], fw2[:], z1[:, c0:c0 + cn], start=True, stop=True)
            z.then_inc(z2_ps, 1)
            pe.wait_ge(att_in, 16 * 2 * R * 4)
            pe.wait_ge(cond_ready, 1)
            for n in range(NW):
                if n >= 2:
                    pe.wait_ge(basis_out, n - 1)
                for half in range(2):
                    load = 2 * n + half
                    pe.wait_ge(basis_in[load % 3], 64 * (load // 3 + 1))
                    for q in range(QL):
                        row = QL * half + q
                        g = pe.matmul(PS[:, 6 + n % 2, :], att_z[n // (NW // 2)][:, 15 - row:143 - row],
                                      basis_t[load % 3][:, q, :], start=(row == 0), stop=(row == 15))
                    g.then_inc(basis_used, 1)
            pe.drain().then_inc(pe_end.sem, 1)

            phase_begins(pe, "setup", 0)
            with pe.Fori(0, NG // 2) as it:
                for b in range(2):
                    pe.wait_ge(hot_ready, 2 * it + (b + 1))
                    for h in range(2):
                        for j in range(3):
                            g = pe.matmul(PS[0:T, 3 * b + j, 0:SB], dst_hot[b][:, h, 0:T],
                                          src_hot[b][:, h, SB * j:SB * (j + 1)], start=(h == 0), stop=(h == 1))
                    g.then_inc(count_ps, 1)
            pe.drain().then_inc(pe_end.sem, 1)

            phase_begins(pe, "setup", 1)
            for t in range(NT):
                pe.wait_ge(csum_ready, t + 1)
                if t:
                    pe.wait_ge(cnt1_ready, t)
                for k in range(NT):
                    g = pe.transpose(PS[0:T, k // 4, T * (k % 4):T * (k % 4 + 1)], csum[:, k, :], ident[0:T, 0:T])
                g.then_inc(csumT_ps, 1)
            pe.drain().then_inc(pe_end.sem, 1)

            def mods(lay, ph, p, a, mod):
                i = NP * 2 * ph + 2 * p + a
                if i % 10:
                    wait(pe, y_ready, lay, i - 1)
                else:
                    wait(pe, mod_ready, lay, ph)
                nodes = cond3[:, W * p + T * a:W * p + T * (a + 1)]
                for b in range(2):
                    g = pe.matmul(PS[0:T, b, :], nodes, mod[b][:], start=True, stop=True)
                g.then_inc(mod_ps.sem, 1)

            def transposed(lay, ph, p, a, y):
                i = NP * 2 * ph + 2 * p + a
                wait(pe, y_ready, lay, i)
                if i % 10 >= 2:
                    wait(pe, yT_lo_done, lay, i - 2)
                for c in range(4):
                    g = pe.transpose(PS[:, 2 + a, T * c:T * (c + 1)], y[:, a, 128 * c:128 * (c + 1)], ident[0:T, 0:T])
                g.then_inc(yT_ps.sem, 1)

            def columns(bank, c, w_hi, w_lo, x_hi, x_lo, x_lo_ready):
                o = PS[:, bank, 0:W]
                f = slice(128 * c, 128 * (c + 1))
                for k in range(4):
                    pe.matmul(o, w_hi[:, k, f], x_hi[:, k, :], start=(k == 0), stop=False)
                    pe.matmul(o, w_lo[:, k, f], x_hi[:, k, :], start=False, stop=False)
                x_lo_ready()
                for k in range(4):
                    g = pe.matmul(o, w_hi[:, k, f], x_lo[:, k, :], start=False, stop=(k == 3))
                return g

            def rows(bank, a, x_hi, x_lo, w_hi, w_lo, row3):
                o = PS[0:T, bank, :]
                n = slice(T * a, T * (a + 1))
                g = pe.matmul(o, ones_r[:, 0:T], row3[:], start=True, stop=False) if row3 is not None else None
                for k in range(4):
                    pe.matmul(o, x_hi[:, k, n], w_hi[:, k, :], start=(row3 is None and k == 0), stop=False)
                    pe.matmul(o, x_hi[:, k, n], w_lo[:, k, :], start=False, stop=False)
                    g = pe.matmul(o, x_lo[:, k, n], w_hi[:, k, :], start=False, stop=(k == 3))
                return g

            with pe.Fori(0, LAYERS) as lay:
                phase_begins(pe, lay, -1)
                for a in range(2):
                    mods(lay, 0, 0, a, mod3)
                for a in range(2):
                    transposed(lay, 0, 0, a, yt[0])
                for p in range(NP):
                    s = p % 2
                    if p + 1 < NP:
                        mods(lay, 0, p + 1, 0, mod3)
                    wait(pe, yT_hi_done, lay, 2 * p + 1)

                    def lo_ready():
                        wait(pe, yT_lo_done, lay, 2 * p + 1)

                    if p == 0:
                        wait(pe, w_lo_done, lay, 0)
                    for c in range(4):
                        bank_free(pe, QKV_GROUPS, k_lo_done, 4 * p + c, lay)
                        columns(bank_of(QKV_GROUPS, k_lo_done, 4 * p + c), c, wk_hi, wk_lo, yT_hi[s], yT_lo[s],
                                lo_ready).then_inc(k_ps.sem, 1)
                    if p + 1 < NP:
                        mods(lay, 0, p + 1, 1, mod3)
                    if p == 0:
                        wait(pe, w_lo_done, lay, 1)
                    for c in range(4):
                        bank_free(pe, QKV_GROUPS, q_done, 4 * p + c, lay)
                        columns(bank_of(QKV_GROUPS, q_done, 4 * p + c), c, wq_hi, wq_lo, yT_hi[s], yT_lo[s],
                                lo_ready).then_inc(q_ps.sem, 1)
                    if p + 1 < NP:
                        transposed(lay, 0, p + 1, 0, yt[(p + 1) % 2])
                    if p == 0:
                        wait(pe, w_lo_done, lay, 2)
                        wait(pe, rows_ready_l, lay, 0)
                    for a in range(2):
                        bank_free(pe, QKV_GROUPS, v_lo_done, 2 * p + a, lay)
                        rows(bank_of(QKV_GROUPS, v_lo_done, 2 * p + a), a, yT_hi[s], yT_lo[s], wv_hi, wv_lo,
                             bv3).then_inc(v_ps.sem, 1)
                    if p + 1 < NP:
                        transposed(lay, 0, p + 1, 1, yt[(p + 1) % 2])
                pe.drain().then_inc(pe_end.sem, 1)

                phase_begins(pe, lay, 0)

                def scores(i, a):
                    h = i % 4
                    wait(pe, q_lo_done, lay, i)
                    if 2 * i + a:
                        wait(pe, masked, lay, 2 * i + a - 1)
                    n = slice(T * a, T * (a + 1))
                    for x, (q_t, k_t) in enumerate(((q_hi, k_hi), (q_hi, k_lo), (q_lo, k_hi))):
                        for j in range(3):
                            g = pe.matmul(PS[0:T, j, 0:SB], q_t[:, h, n], k_t[:, h, SB * j:SB * (j + 1)],
                                          start=(x == 0), stop=(x == 2))
                    g.then_inc(s_ps.sem, 1)

                def turn(i, a):
                    u = 2 * i + a
                    wait(pe, normed, lay, u)
                    if u:
                        wait(pe, pT_lo_done, lay, u - 1)
                    for k in range(NT):
                        g = pe.transpose(PS[0:T, 3 + k // 4, T * (k % 4):T * (k % 4 + 1)],
                                         prob[u % 3][:, T * k:T * (k + 1)], ident[0:T, 0:T])
                    g.then_inc(pT_ps.sem, 1)

                def values(i, half):
                    h, s = i % 4, i % 2
                    if half == 0:
                        wait(pe, pT_lo_done, lay, 2 * i + 1)
                        if i >= 2:
                            wait(pe, o_done, lay, i - 2)
                    f = slice(128 * h, 128 * (h + 1))
                    for k in range(5 * half, 5 * half + 5):
                        for x, (v_t, p_t) in enumerate(((v_hi, pT_hi[s]), (v_hi, pT_lo[s]), (v_lo, pT_hi[s]))):
                            g = pe.matmul(PS[:, 6 + s, 0:W], v_t[:, k, f], p_t[:, k, :],
                                          start=(k == 0 and x == 0), stop=(k == NT - 1 and x == 2))
                    if half:
                        g.then_inc(o_ps.sem, 1)

                for i in range(4 * NP + 2):
                    for a in range(2):
                        if i < 4 * NP:
                            scores(i, a)
                        if 1 <= i <= 4 * NP:
                            turn(i - 1, a)
                        if i >= 2:
                            values(i - 2, a)
                pe.drain().then_inc(pe_end.sem, 1)

                phase_begins(pe, lay, 1)

                def out_proj(p):
                    wait(pe, oT_lo_done, lay, p)
                    for a in range(2):
                        bank_free(pe, MLP_GROUPS, x_added, 2 * p + a, lay)
                        rows(bank_of(MLP_GROUPS, x_added, 2 * p + a), a, oT_hi[p % 2], oT_lo[p % 2], wo_hi, wo_lo,
                             bo3).then_inc(wo_ps.sem, 1)

                wait(pe, w_lo_done, lay, 3)
                wait(pe, rows_ready_l, lay, 1)
                out_proj(0)
                for a in range(2):
                    mods(lay, 1, 0, a, mod3b)
                for a in range(2):
                    transposed(lay, 1, 0, a, ym[0])
                for p in range(NP):
                    if p + 1 < NP:
                        out_proj(p + 1)
                    wait(pe, yT_hi_done, lay, 2 * NP + 2 * p + 1)
                    if p == 0:
                        wait(pe, w_lo_done, lay, 4)
                    for c in range(4):
                        bank_free(pe, MLP_GROUPS, h_done, 4 * p + c, lay)
                        columns(bank_of(MLP_GROUPS, h_done, 4 * p + c), c, w1_hi, w1_lo, zT_hi, zT_lo,
                                lambda: wait(pe, yT_lo_done, lay, 2 * NP + 2 * p + 1)).then_inc(w1_ps.sem, 1)
                    if p + 1 < NP:
                        mods(lay, 1, p + 1, 0, mod3b)
                    if p == 0:
                        wait(pe, w_lo_done, lay, 5)
                    wait(pe, h_lo_done, lay, p)
                    for a in range(2):
                        bank_free(pe, MLP_GROUPS, x_done, 2 * p + a, lay)
                        rows(bank_of(MLP_GROUPS, x_done, 2 * p + a), a, hT_hi, hT_lo, w2_hi, w2_lo,
                             b23).then_inc(w2_ps.sem, 1)
                        if a == 0 and p + 1 < NP:
                            mods(lay, 1, p + 1, 1, mod3b)
                    if p + 1 < NP:
                        for a in range(2):
                            transposed(lay, 1, p + 1, a, ym[(p + 1) % 2])
                pe.drain().then_inc(pe_end.sem, 1)

            phase_begins(pe, "final", -1)
            for l in range(2):
                if l:
                    pe.wait_ge(r_end[2], 2)
                    pe.wait_ge(r_end[1], 2)
                pe.wait_ge(r_w_lo, 3 * (l + 1))
                pe.wait_ge(r_rows_ready, l + 1)
                for p in range(NP):
                    n = NP * l + p
                    for a in range(2):
                        if l == 0:
                            pe.wait_ge(r_h_ready, n + 1)
                        else:
                            pe.wait_ge(r_h_in, 16 * (p + 1))
                        if n:
                            pe.wait_ge(r_hT_lo, 2 * n - 1 + a)
                        for c in range(4):
                            g = pe.transpose(PS[:, a, T * c:T * (c + 1)], yr[:, a, 128 * c:128 * (c + 1)], ident[0:T, 0:T])
                        g.then_inc(r_hT_ps, 1)
                    for a in range(2):
                        i = 2 * n + a
                        pe.wait_ge(r_hT_lo, i + 1)
                        nodes = slice(T * a, T * (a + 1))
                        if i:
                            pe.wait_ge(r_gate, i)
                        for k in range(4):
                            pe.matmul(PS[0:T, 2, 0:2 * R], rT_hi[:, k, nodes], gw_hl[:, k, :], start=(k == 0), stop=(k == 3))
                        for k in range(4):
                            g = pe.matmul(PS[0:T, 3, 0:2 * R], rT_lo[:, k, nodes], gw_hl[:, k, :], start=(k == 0), stop=(k == 3))
                        g.then_inc(r_gate_ps, 1)
                        for w in range(3):
                            if i:
                                if w < 2:
                                    pe.wait_ge(r_m_lo, 2 * (i - 1) + w + 1)
                                else:
                                    pe.wait_ge(r_self_out, i)
                            rows(4 + w, a, rT_hi, rT_lo, wr_hi[w], wr_lo[w], rb3 if w == 2 else None)\
                                .then_inc(r_mm_ps, 1)
                pe.drain().then_inc(r_end[0], 1)
                for s in r_end[1:]:
                    pe.wait_ge(s, 2 * l + 1)
                for t in range(NT):
                    n = NT * l + t
                    pe.wait_ge(r_adj_hi_in[t % 2], 16 * (NT // 2 * l + t // 2 + 1))
                    pe.wait_ge(r_adj_lo_in, 16 * (n + 1))
                    if n >= 2:
                        pe.wait_ge(r_res_ready, n - 1)
                    for k in range(NB):
                        r, tile = divmod(k, NT)
                        for x, (c_t, m_t) in enumerate(((adj_hi[t % 2], msg_hi), (adj_hi[t % 2], msg_lo), (adj_lo[0], msg_hi))):
                            g = pe.matmul(PS[0:T, t % 2, :], c_t[:, k, :], m_t[r][:, tile, :],
                                          start=(k == 0 and x == 0), stop=(k == NB - 1 and x == 2))
                    g.then_inc(r_agg_ps, 1)
                pe.drain().then_inc(r_end[0], 1)

        @block.scalar
        def _(act):
            def store_x0(p):
                act.wait_ge(h0_ready, p + 1)
                act.dma_start(pair_rows(x_lat, p), y0[p % 2][:]).then_inc(x_stored[p % 2].sem, 16)

            for p in range(2):
                act.dma_start(x0[p][:], pair_rows(x_in, p)).then_inc(x_loaded[p].sem, 16)
            for p in range(2, NP):
                wait(act, x_used, "setup", p - 2)
                act.dma_start(x0[p % 2][:], pair_rows(x_in, p)).then_inc(x_loaded[p % 2].sem, 16)
                store_x0(p - 2)
            store_x0(NP - 2)
            store_x0(NP - 1)
            for c in range(NRC):
                act.wait_ge(rank_ps, c + 1)
                act.activation(tot[:].rearrange("p k c -> p (k c)")[:, c * RC:(c + 1) * RC],
                               PS[:, 2 + c % 2, 0:RC], ACT.Copy).then_inc(tot_out, 1)
            act.wait_ge(phase_ready, 1)
            act.activation(ph[:], ph[:], ACT.Sin, scale=2.0 * math.pi).then_inc(sin_done, 1)
            act.wait_ge(z1_ps, 1)
            for j, (c0, cn) in enumerate(CH):
                z = act.activation(z2[:, c0:c0 + cn], PS[0:C, 4 + j, 0:cn], ACT.Exp, bias=fb[:, 2:3], scale=-1.0)
            z.then_inc(z1_exp, 1)
            for n in range(NW):
                l, q0 = divmod(16 * n, Q)
                act.wait_ge(basis_used, 2 * n + 2)
                if n >= 2:
                    act.wait_ge(w_stored[n % 2], 32 * (n // 2))
                act.activation(w_out[n % 2][:], PS[:, 6 + n % 2, :], ACT.Copy).then_inc(basis_out, 1)
                act.wait_ge(basis_out, n + 1)
                for r in range(R):
                    act.dma_start(rel_w[l, r, :, :].rearrange("(i q) d -> i q d", q=Q)[:, q0:q0 + 16, :],
                                  w_out[n % 2][64 * r:64 * (r + 1), :]).then_inc(w_stored[n % 2], 16)
            act.drain().then_inc(act_end.sem, 1)
            phase_begins(act, "setup", 0)
            for i in range(2):
                act.wait_ge(w_stored[i], 16 * NW)
            act.drain().then_inc(act_end.sem, 1)
            phase_begins(act, "setup", 1)
            for t in range(NT):
                if t:
                    act.wait_ge(adj_stored, 32 * t)
                    act.wait_ge(adj_lo_done, t)
                act.activation(c_hi[:], count[:, :, T * t:T * (t + 1)], ACT.Copy).then_inc(adj_hi_done, 1)
                act.wait_ge(cnt1_ready, t + 1)
                act.activation(cnt1[:, 0:N], cnt1[:, 0:N], ACT.Ln).then_inc(ln_done, 1)
            act.drain().then_inc(act_end.sem, 1)

            def yT_high(lay, i, a, dst_t, before=None):
                wait(act, yT_ps, lay, i)
                if before:
                    before()
                act.activation(dst_t[:, :, T * a:T * (a + 1)],
                               PS[:, 2 + a, 0:4 * T].rearrange("p (c t) -> p c t", c=4), ACT.Copy)\
                    .then_inc(yT_hi_done.sem, 1)

            with act.Fori(0, LAYERS) as lay:
                def w_high(hi, raw, n):
                    wait(act, w_in, lay, n)
                    act.activation(hi[:], raw[:], ACT.Copy).then_inc(w_hi_done.sem, 1)

                phase_begins(act, lay, -1)
                w_high(wk_hi, w_raw, 0)
                yT_high(lay, 0, 0, yT_hi[0])
                yT_high(lay, 1, 1, yT_hi[0])
                w_high(wq_hi, w_raw, 1)
                w_high(wv_hi, w_raw, 2)
                wait(act, cols_ready, lay, 0)
                for p in range(NP):
                    cols = slice(W * p, W * (p + 1))
                    for c in range(4):
                        wait(act, k_ps, lay, 4 * p + c)
                        act.activation(k_hi[:, c, cols], PS[:, bank_of(QKV_GROUPS, k_lo_done, 4 * p + c), 0:W],
                                       ACT.Identity, bias=bk_col[:, c:c + 1]).then_inc(k_hi_done.sem, 1)
                    for c in range(4):
                        wait(act, q_ps, lay, 4 * p + c)
                        act.activation(q_raw[:, c, cols], PS[:, bank_of(QKV_GROUPS, q_done, 4 * p + c), 0:W],
                                       ACT.Identity, bias=bq_col[:, c:c + 1]).then_inc(q_done.sem, 1)
                    for a in range(2):
                        if p + 1 < NP and a == 0:
                            if p >= 1:
                                wait(act, v_ps, lay, 2 * p - 1)
                            yT_high(lay, 2 * p + 2, 0, yT_hi[(p + 1) % 2])
                        wait(act, v_ps, lay, 2 * p + a)
                        act.activation(v_hi[:, 2 * p + a, :], PS[0:T, bank_of(QKV_GROUPS, v_lo_done, 2 * p + a), :],
                                       ACT.Copy).then_inc(v_hi_done.sem, 1)
                    if p + 1 < NP:
                        yT_high(lay, 2 * p + 3, 1, yT_hi[(p + 1) % 2])
                act.drain().then_inc(act_end.sem, 1)

                phase_begins(act, lay, 0)

                def q_high(i):
                    if i >= 4:
                        wait(act, s_ps, lay, 2 * (i - 4) + 1)
                    p, h = divmod(i, 4)
                    act.activation(q_hi[:, h, :], q_raw[:, h, W * p:W * (p + 1)], ACT.Copy).then_inc(q_hi_done.sem, 1)

                def exponentials(i, a):
                    u = 2 * i + a
                    wait(act, negmax_ready, lay, u)
                    act.activation(prob[u % 3][:], prob[u % 3][:], ACT.Exp, bias=neg_max[0:T, u % 4:u % 4 + 1],
                                   scale=SCALE, accum_out=den[0:T, u % 4:u % 4 + 1]).then_inc(exp_done.sem, 1)

                def pT_high(i, a):
                    u = 2 * i + a
                    wait(act, pT_ps, lay, u)
                    if i >= 2 and a == 0:
                        wait(act, o_ps, lay, i - 2)
                    n = slice(T * a, T * (a + 1))
                    act.activation(pT_hi[i % 2][:, 0:8, n].rearrange("p (b c) t -> p b c t", b=2),
                                   PS[0:T, 3:5, 0:4 * T].rearrange("p b (c t) -> p b c t", c=4), ACT.Copy)
                    act.activation(pT_hi[i % 2][:, 8:10, n],
                                   PS[0:T, 5, 0:2 * T].rearrange("p (c t) -> p c t", c=2), ACT.Copy)\
                        .then_inc(pT_hi_done.sem, 1)

                def head_out(i):
                    p, h = divmod(i, 4)
                    wait(act, o_ps, lay, i)
                    act.activation(q_raw[:, h, W * p:W * (p + 1)], PS[:, 6 + i % 2, 0:W], ACT.Copy)\
                        .then_inc(o_done.sem, 1)

                q_high(0)
                q_high(1)
                for i in range(4 * NP + 2):
                    for a in range(2):
                        if i < 4 * NP:
                            exponentials(i, a)
                        if 1 <= i <= 4 * NP:
                            pT_high(i - 1, a)
                        if a == 0 and 2 <= i + 1 < 4 * NP:
                            q_high(i + 1)
                    if i >= 2:
                        head_out(i - 2)
                act.drain().then_inc(act_end.sem, 1)

                phase_begins(act, lay, 1)

                def o_high(p):
                    if p >= 2:
                        wait(act, wo_ps, lay, 2 * (p - 2) + 1)
                    act.activation(oT_hi[p % 2][:], q_raw[:, :, W * p:W * (p + 1)], ACT.Copy)\
                        .then_inc(oT_hi_done.sem, 1)

                o_high(0)
                w_high(wo_hi, w_raw3, 3)
                o_high(1)
                w_high(w1_hi, w_raw3, 4)
                for a in range(2):
                    yT_high(lay, 2 * NP + a, a, zT_hi)
                w_high(w2_hi, w_raw3, 5)
                for p in range(NP):
                    for c in range(4):
                        wait(act, w1_ps, lay, 4 * p + c)
                        if p and c == 0:
                            wait(act, h_lo_done, lay, p - 1)
                        act.activation(hT[:, c, :], PS[:, bank_of(MLP_GROUPS, h_done, 4 * p + c), 0:W],
                                       ACT.Relu, bias=b1_col[:, c:c + 1]).then_inc(h_done.sem, 1)
                    wait(act, h_done, lay, 4 * p + 3)
                    if p:
                        wait(act, w2_ps, lay, 2 * p - 1)
                    act.activation(hT_hi[:], hT[:], ACT.Copy).then_inc(h_hi_done.sem, 1)
                    if p + 2 < NP:
                        o_high(p + 2)
                    if p + 1 < NP:
                        for a in range(2):
                            yT_high(lay, 2 * NP + 2 * p + 2 + a, a, zT_hi)
                act.drain().then_inc(act_end.sem, 1)

            phase_begins(act, "final", -1)
            for l in range(2):
                if l:
                    act.wait_ge(r_end[0], 2)
                    act.wait_ge(r_end[2], 2)
                for n in range(3):
                    act.wait_ge(r_w_in, 16 * (3 * l + n + 1))
                    act.activation(wr_hi[n][:], w_rawr[:], ACT.Copy).then_inc(r_w_hi, 1)
                for p in range(NP):
                    for a in range(2):
                        i = 2 * (NP * l + p) + a
                        act.wait_ge(r_hT_ps, i + 1)
                        if i >= 2:
                            act.wait_ge(r_mm_ps, 3 * 2 * (NP * l + p))
                        act.activation(rT_hi[:, :, T * a:T * (a + 1)],
                                       PS[:, a, 0:4 * T].rearrange("p (c t) -> p c t", c=4), ACT.Copy)\
                            .then_inc(r_hT_hi, 1)
                    for a in range(2):
                        i = 2 * (NP * l + p) + a
                        tile = 2 * p + a
                        act.wait_ge(r_gate_exp, 2 * i + 1)
                        act.activation(gate_sb[0:T, 1, :], gate_sb[0:T, 0, :], ACT.Exp, scale=-1.0).then_inc(r_gate_exp, 1)
                        act.wait_ge(r_gate, i + 1)
                        for r in range(R):
                            act.wait_ge(r_mm_ps, 3 * i + r + 1)
                            act.activation(msg_hi[r][:, tile, :], PS[0:T, 4 + r, :], ACT.Copy,
                                           scale=gate_sb[0:T, 0, r:r + 1]).then_inc(r_m_hi, 1)
                        act.wait_ge(r_mm_ps, 3 * i + 3)
                        act.activation(self_term[:, tile, :], PS[0:T, 6, :], ACT.Copy).then_inc(r_self_out, 1)
                act.drain().then_inc(r_end[1], 1)
                act.drain().then_inc(r_end[1], 1)

        @block.vector
        def _(v):
            links = {"setup": 0, "layer": 0, "final": 0}

            def link(ins, where):
                kind = where if isinstance(where, str) else "layer"
                ins.then_inc(chain.sem, 1)
                wait(v, chain, where, links[kind])
                links[kind] += 1

            def norm_stats(where, i, x):
                s = i % 2
                for a in range(2):
                    last = v.bn_stats(bn[0:T, a, :], x[:, a, :])
                link(last, where)
                v.memset(wait_slot[0:1, 0:1], 0.0)
                for a in range(2):
                    last = v.bn_aggr(mv[0:T, s, 2 * a:2 * a + 2], bn[0:T, a, :])
                link(last, where)
                v.tensor_scalar(var_eps[0:T, s, :], mv[0:T, s, 1:4:2], EPS, None, ALU.add).then_inc(var_ready.sem, 1)

            def norm_apply(where, i, x, y):
                s = i % 2
                wait(v, rstd_ready, where, i)
                for a in range(2):
                    last = v.tensor_scalar(y[:, a, :], x[:, a, :], mv[0:T, s, 2 * a:2 * a + 1], rstd[0:T, s, a:a + 1],
                                           ALU.subtract, ALU.mult)
                last.then_inc(x_used.sem, 1)
                wait(v, x_used, where, i)

            v.memset(cond3[:].bitcast(fp32), 1.0)
            v.memset(ones_r[:].bitcast(fp32), 1.0)
            for p in range(NP):
                wait(v, x_loaded[p % 2], "setup", p // 2)
                norm_stats("setup", p, x0[p % 2])
                if p >= 2:
                    wait(v, x_stored[p % 2], "setup", p // 2 - 1)
                norm_apply("setup", p, x0[p % 2], y0[p % 2])
                v.tensor_scalar(y0[p % 2][:], y0[p % 2][:], 0.0, None, ALU.max).then_inc(h0_ready, 1)

            v.wait_ge(edges_in, 96)
            v.wait_ge(consts, 8)
            v.tensor_copy(dst_f[:], dst_i[:])
            v.tensor_copy(payload[:, :, 0], src_i[:])
            link(v.tensor_copy(typ_f[:], typ_i[:]), "setup")
            link(v.tensor_scalar(tile_f[:], dst_f[:], 1.0 / T, 0.5 / T - 0.5, ALU.mult, ALU.add), "setup")
            link(v.tensor_scalar(tile_f[:], tile_f[:], MAGIC, None, ALU.add), "setup")
            link(v.tensor_scalar(tile_f[:], tile_f[:], MAGIC, None, ALU.subtract), "setup")
            v.scalar_tensor_tensor(payload[:, :, 1], tile_f[:], -float(T), dst_f[:], ALU.mult, ALU.add)
            link(v.tensor_scalar(typ_f[:], typ_f[:], 0.0, float(NT), ALU.not_equal, ALU.mult), "setup")
            link(v.tensor_tensor(bucket[:], typ_f[:], tile_f[:], ALU.add), "setup")
            v.tensor_tensor(mask[:], bucket[:].unsqueeze(1).to_broadcast([128, NB, EC]),
                            bucket_id[:].unsqueeze(2).to_broadcast([128, NB, EC]), ALU.is_equal).then_inc(mask_ready, 1)

            v.wait_ge(freq_ready, 1)
            v.wait_ge(noise_in, 16)
            v.wait_ge(fw_in, 16 * 9)
            link(v.tensor_copy(freq_off[:, 0:1], freq_i[:].bitcast(i32)), "setup")
            link(v.tensor_scalar(freq_off[:, 1:2], freq_off[:, 0:1], F2 / 2 - 0.5, 0.25, ALU.is_gt, ALU.mult), "setup")
            link(v.scalar_tensor_tensor(freq_off[:, 0:1], freq_off[:, 1:2], -2.0 * F2, freq_off[:, 0:1],
                                        ALU.mult, ALU.add), "setup")
            link(v.tensor_scalar(freq_off[:, 0:1], freq_off[:, 0:1], 1.0, 1.0 / 16, ALU.add, ALU.mult), "setup")
            link(v.tensor_scalar(ph[:], ph[:], freq_off[:, 0:1], freq_off[:, 1:2], ALU.mult, ALU.add), "setup")
            link(v.tensor_scalar(ph_int[:], ph[:], MAGIC, None, ALU.add), "setup")
            link(v.tensor_scalar(ph_int[:], ph_int[:], MAGIC, None, ALU.subtract), "setup")
            link(v.tensor_tensor(ph[:], ph[:], ph_int[:], ALU.subtract), "setup")
            v.tensor_scalar(fb[:, 2:3], fb[:, 0:1], -1.0, None, ALU.mult)
            v.tensor_scalar(ph[:], ph[:], 0.4999999, -0.4999999, ALU.min, ALU.max).then_inc(phase_ready, 1)

            for c in range(NRC):
                v.wait_ge(rank_ps, c + 1)
                last = v.tensor_copy(rank[:].rearrange("p k c -> p (k c)")[:, c * RC:(c + 1) * RC], PS[:, c % 2, 0:RC])
                last.then_inc(rank_out, 1)
            v.wait_ge(tot_out, NRC)
            v.wait_ge(rank_out, NRC)
            a_t, n = tot, 0
            step = 1
            while step < EC:
                b_t = pre[n % 2]
                v.tensor_tensor(b_t[:, :, step:], a_t[:, :, step:], a_t[:, :, 0:EC - step], ALU.add)
                link(v.tensor_copy(b_t[:, :, 0:step], a_t[:, :, 0:step]), "setup")
                a_t, n, step = b_t, n + 1, 2 * step
            incl = a_t
            other = pre[n % 2]
            link(v.tensor_tensor(other[:], incl[:], tot[:], ALU.subtract), "setup")
            link(v.tensor_scalar(grp[:], incl[:, :, EC - 1], GE - 1.0, 1.0 / GE, ALU.add, ALU.mult), "setup")
            link(v.tensor_scalar(grp[:], grp[:], 0.5 / GE - 0.5, MAGIC, ALU.add, ALU.add), "setup")
            link(v.tensor_scalar(grp[:], grp[:], MAGIC, None, ALU.subtract), "setup")
            g_t, n, step = grp, 0, 1
            while step < NB:
                b_t = gpre[n % 2]
                v.tensor_tensor(b_t[:, step:], g_t[:, step:], g_t[:, 0:NB - step], ALU.add)
                link(v.tensor_copy(b_t[:, 0:step], g_t[:, 0:step]), "setup")
                g_t, n, step = b_t, n + 1, 2 * step
            ends = g_t
            link(v.tensor_tensor(group_ge[:], group_no[:].unsqueeze(2).to_broadcast([1, NG, NB]),
                                 ends[0:1, :].unsqueeze(1).to_broadcast([1, NG, NB]), ALU.is_ge), "setup")
            link(v.tensor_reduce(group_no[:], group_ge[:], AX.X, ALU.add), "setup")
            v.tensor_scalar(group_tile[:], group_no[:], NB - 1.0, None, ALU.min)
            link(v.tensor_tensor(grp[:], ends[:], grp[:], ALU.subtract), "setup")
            link(v.tensor_scalar(grp[:], grp[:], float(GE), None, ALU.mult), "setup")
            link(v.tensor_tensor(rank[:], rank[:], other[:], ALU.add), "setup")
            link(v.tensor_tensor(rank[:], rank[:], grp[:].unsqueeze(2).to_broadcast([128, NB, EC]), ALU.add), "setup")
            link(v.tensor_tensor(rank[:], rank[:], mask[:], ALU.mult), "setup")
            link(v.tensor_reduce(pos[:], rank[:].rearrange("p k c -> p c k"), AX.X, ALU.add), "setup")
            link(v.tensor_scalar(pos_hi[:], pos[:], 1.0 / 128, 1.0 / 256 - 0.5, ALU.mult, ALU.add), "setup")
            link(v.tensor_scalar(pos_hi[:], pos_hi[:], MAGIC, None, ALU.add), "setup")
            link(v.tensor_scalar(pos_hi[:], pos_hi[:], MAGIC, -(128.0 * TC - 1), ALU.subtract, ALU.mult), "setup")
            link(v.scalar_tensor_tensor(pos[:], pos[:], float(TC), pos_hi[:], ALU.mult, ALU.add), "setup")
            v.tensor_copy(row_i[:], pos[:]).then_inc(rows_ready, 1)

            v.wait_ge(z1_exp, 1)
            link(v.tensor_scalar(z2[:], z2[:], 1.0, None, ALU.add), "setup")
            link(v.reciprocal(z2[:], z2[:]), "setup")
            for j, (c0, cn) in enumerate(CH):
                last = v.scalar_tensor_tensor(z1[:, c0:c0 + cn], PS[0:C, 4 + j, 0:cn], fb[:, 0:1], z2[:, c0:c0 + cn],
                                              ALU.add, ALU.mult)
            last.then_inc(silu_done, 1)
            v.wait_ge(bias_cols_ps, 1)
            v.tensor_copy(cols_all[:].rearrange("p b c -> p (b c)"), PS[:, 7, 0:4 * LAYERS * H])
            v.wait_ge(z2_ps, 1)
            for j, (c0, cn) in enumerate(CH):
                v.tensor_scalar(cond3[0:C, c0:c0 + cn], PS[0:C, 4 + j, 0:cn], fb[:, 1:2], None, ALU.add)
                last = v.tensor_scalar(cond3[64:64 + C, c0:c0 + cn], PS[0:C, 4 + j, 0:cn], fb[:, 1:2], None, ALU.add)
            link(last, "setup")
            for j, (c0, cn) in enumerate(CH):
                last = v.scalar_tensor_tensor(cond3[32:32 + C, c0:c0 + cn], PS[0:C, 4 + j, 0:cn], fb[:, 1:2],
                                              cond3[0:C, c0:c0 + cn].bitcast(fp32), ALU.add, ALU.subtract)
            last.then_inc(cond_ready, 1)
            v.drain().then_inc(dve_end.sem, 1)

            phase_begins(v, "setup", 0)
            v.wait_ge(table_in, 16)
            v.wait_ge(node_no_ready, 1)
            v.memset(count[:], 0).then_inc(count_added, 1)
            with v.Fori(0, NG // 2) as it:
                for b in range(2):
                    for h in range(2):
                        col = 4 * it + (2 * b + h)
                        v.tensor_scalar(dst_hot[b][:, h, :], node_no[:, 0:128],
                                        table[:, bass.ds(col, 1), 1:2].rearrange("p a k -> p (a k)"), None, ALU.is_equal)
                        last = v.tensor_scalar(src_hot[b][:, h, :], node_no[:],
                                               table[:, bass.ds(col, 1), 0:1].rearrange("p a k -> p (a k)"), None, ALU.is_equal)
                    last.then_inc(hot_ready, 1)
                for b in range(2):
                    k = v.value_load(group_tile[0:1, bass.ds(2 * it + b, 1)], min_val=0, max_val=NB - 1)
                    tile = count[:, bass.ds(k, 1), :].rearrange("p a (j s) -> p (a j) s", j=3)
                    v.wait_ge(count_ps, 2 * it + (b + 1))
                    v.wait_ge(count_added, 2 * it + (b + 1))
                    v.tensor_tensor(tile, tile, PS[0:T, 3 * b:3 * b + 3, 0:SB], ALU.add).then_inc(count_added, 1)
            v.drain().then_inc(dve_end.sem, 1)

            phase_begins(v, "setup", 1)
            v.memset(cnt0[:, N:SW], NONE)
            for t in range(NT):
                n = slice(T * t, T * (t + 1))
                if t:
                    v.wait_ge(csumT_ps, t)
                v.tensor_tensor(csum[:], count[:, 0:NT, n], count[:, NT:NB, n], ALU.add).then_inc(csum_ready, 1)
                v.wait_ge(adj_hi_done, t + 1)
                if t:
                    v.wait_ge(adj_stored, 32 * t)
                v.tensor_tensor(c_lo[:], count[:, :, n], c_hi[:].bitcast(fp32), ALU.subtract).then_inc(adj_lo_done, 1)
                v.wait_ge(csumT_ps, t + 1)
                if t:
                    v.wait_ge(sbias_stored, 16 * t)
                for ps, c0, c1 in ((PS[0:T, 0:2, 0:4 * T], 0, 8 * T), (PS[0:T, 2, 0:2 * T], 8 * T, N)):
                    def part(x):
                        return x[:, c0:c1].rearrange("p (b s) -> p b s", b=2) if c0 == 0 else x[:, c0:c1]
                    v.tensor_scalar(part(cnt0), ps, 0.0, NONE, ALU.is_equal, ALU.mult)
                    last = v.tensor_scalar(part(cnt1), ps, 1.0, None, ALU.max)
                last.then_inc(cnt1_ready, 1)
                v.wait_ge(ln_done, t + 1)
                v.scalar_tensor_tensor(cnt0[:, 0:N], cnt1[:, 0:N], 1.0 / SCALE, cnt0[:, 0:N], ALU.mult, ALU.add)\
                    .then_inc(sbias_ready, 1)
                v.wait_ge(sbias_ready, t + 1)
            v.drain().then_inc(dve_end.sem, 1)

            def split_mods(lay, ph, mod, raw):
                for b in range(2):
                    last = v.memset(mod[b][:].bitcast(fp32), 0.0)
                link(last, lay)
                wait(v, mod_raw_in, lay, ph)
                for b in range(2):
                    v.tensor_copy(mod[b][32:32 + C, :], raw[b][0:C, :])
                    last = v.tensor_copy(mod[b][0:C + 1, :], raw[b][:])
                link(last, lay)
                for b in range(2):
                    last = v.tensor_tensor(mod[b][64:64 + C + 1, :], raw[b][:], mod[b][0:C + 1, :].bitcast(fp32), ALU.subtract)
                last.then_inc(mod_ready.sem, 1)

            def split_row(where, row3, raw):
                link(v.memset(row3[:].bitcast(fp32), 0.0), where)
                link(v.tensor_copy(row3[0:1, :], raw), where)
                return v.tensor_tensor(row3[32:33, :], raw, row3[0:1, :].bitcast(fp32), ALU.subtract)

            def w_low(lay, lo, hi, raw, n):
                wait(v, w_hi_done, lay, n)
                v.tensor_tensor(lo[:], raw[:], hi[:].bitcast(fp32), ALU.subtract).then_inc(w_lo_done.sem, 1)

            def modulate(lay, i, a, y):
                wait(v, mod_ps, lay, i)
                link(v.scalar_tensor_tensor(y[:, a, :], PS[0:T, 0, :], 1.0, y[:, a, :], ALU.add, ALU.mult), lay)
                v.tensor_tensor(y[:, a, :], PS[0:T, 1, :], y[:, a, :], ALU.add).then_inc(y_ready.sem, 1)

            def yT_low(lay, i, a, hi, lo):
                wait(v, yT_hi_done, lay, i)
                n = slice(T * a, T * (a + 1))
                v.tensor_tensor(lo[:, :, n], PS[:, 2 + a, 0:4 * T].rearrange("p (c t) -> p c t", c=4),
                                hi[:, :, n].bitcast(fp32), ALU.subtract).then_inc(yT_lo_done.sem, 1)

            with v.Fori(0, LAYERS) as lay:
                phase_begins(v, lay, -1)
                for c in (k_hi, k_lo):
                    v.memset(c[:, :, N:SW].bitcast(fp32), 0.0)
                for b, col in enumerate((bk_col, bq_col, b1_col)):
                    last = v.tensor_copy(col[:], cols_all[:, b, bass.ds(H * lay, H)])
                last.then_inc(cols_ready.sem, 1)
                wait(v, x_loaded[0], lay, 0)
                norm_stats(lay, 0, xt[0])
                split_mods(lay, 0, mod3, mod_raw)
                norm_apply(lay, 0, xt[0], yt[0])
                for a in range(2):
                    modulate(lay, a, a, yt[0])
                w_low(lay, wk_lo, wk_hi, w_raw, 0)
                for a in range(2):
                    yT_low(lay, a, a, yT_hi[0], yT_lo[0])
                wait(v, rows_in, lay, 0)
                split_row(lay, bv3, bv_raw[:]).then_inc(rows_ready_l.sem, 1)
                w_low(lay, wq_lo, wq_hi, w_raw, 1)
                w_low(lay, wv_lo, wv_hi, w_raw, 2)
                wait(v, cols_ready, lay, 0)
                for p in range(NP):
                    cols = slice(W * p, W * (p + 1))
                    nxt = (p + 1) % 2
                    if p + 1 < NP:
                        wait(v, x_loaded[nxt], lay, (p + 1) // 2)
                        norm_stats(lay, p + 1, xt[nxt])
                        norm_apply(lay, p + 1, xt[nxt], yt[nxt])
                        modulate(lay, 2 * p + 2, 0, yt[nxt])
                    for c in range(4):
                        wait(v, k_hi_done, lay, 4 * p + c)
                        v.scalar_tensor_tensor(k_lo[:, c, cols], PS[:, bank_of(QKV_GROUPS, k_lo_done, 4 * p + c), 0:W],
                                               bk_col[:, c:c + 1], k_hi[:, c, cols].bitcast(fp32), ALU.add, ALU.subtract)\
                            .then_inc(k_lo_done.sem, 1)
                    if p + 1 < NP:
                        modulate(lay, 2 * p + 3, 1, yt[nxt])
                        if p >= 1:
                            wait(v, v_ps, lay, 2 * p - 1)
                        yT_low(lay, 2 * p + 2, 0, yT_hi[nxt], yT_lo[nxt])
                    for a in range(2):
                        wait(v, v_hi_done, lay, 2 * p + a)
                        v.tensor_tensor(v_lo[:, 2 * p + a, :], PS[0:T, bank_of(QKV_GROUPS, v_lo_done, 2 * p + a), :],
                                        v_hi[:, 2 * p + a, :].bitcast(fp32), ALU.subtract).then_inc(v_lo_done.sem, 1)
                    if p + 1 < NP:
                        yT_low(lay, 2 * p + 3, 1, yT_hi[nxt], yT_lo[nxt])
                v.drain().then_inc(dve_end.sem, 1)

                phase_begins(v, lay, 0)

                def q_low(i):
                    wait(v, q_hi_done, lay, i)
                    p, h = divmod(i, 4)
                    v.tensor_tensor(q_lo[:, h, :], q_raw[:, h, W * p:W * (p + 1)], q_hi[:, h, :].bitcast(fp32),
                                    ALU.subtract).then_inc(q_lo_done.sem, 1)

                def masking(i, a):
                    p, u = i // 4, 2 * i + a
                    wait(v, s_ps, lay, u)
                    if i % 4 == 0:
                        wait(v, sbias_in[2 * (p % 2) + a], lay, p // 2)
                    if u >= 3:
                        wait(v, pT_ps, lay, u - 3)
                    s = slice(u % 4, u % 4 + 1)
                    v.memset(wait_slot[0:1, 0:1], 0.0)
                    v.tensor_tensor_reduce(prob[u % 3][:].rearrange("p (j s) -> p j s", j=3), PS[0:T, 0:3, 0:SB],
                                           sbias[p % 2][a][:].rearrange("p (j s) -> p j s", j=3),
                                           1.0, -3e38, ALU.add, ALU.max, row_max[0:T, s]).then_inc(masked.sem, 1)
                    wait(v, masked, lay, u)
                    v.tensor_scalar(has_edge[0:T, s], row_max[0:T, s], 0.5 * NONE, None, ALU.is_gt)
                    v.tensor_scalar(neg_max[0:T, s], row_max[0:T, s], -SCALE, None, ALU.mult).then_inc(negmax_ready.sem, 1)

                def inverse(i, a):
                    u = 2 * i + a
                    s = slice(u % 4, u % 4 + 1)
                    wait(v, exp_done, lay, u)
                    link(v.reciprocal(inv_den[0:T, s], den[0:T, s]), lay)
                    v.tensor_tensor(inv_den[0:T, s], inv_den[0:T, s], has_edge[0:T, s], ALU.mult).then_inc(inv_ready.sem, 1)

                def pT_low(i, a):
                    u = 2 * i + a
                    wait(v, pT_hi_done, lay, u)
                    n = slice(T * a, T * (a + 1))
                    v.tensor_tensor(pT_lo[i % 2][:, 0:8, n].rearrange("p (b c) t -> p b c t", b=2),
                                    PS[0:T, 3:5, 0:4 * T].rearrange("p b (c t) -> p b c t", c=4),
                                    pT_hi[i % 2][:, 0:8, n].rearrange("p (b c) t -> p b c t", b=2).bitcast(fp32), ALU.subtract)
                    v.tensor_tensor(pT_lo[i % 2][:, 8:10, n], PS[0:T, 5, 0:2 * T].rearrange("p (c t) -> p c t", c=2),
                                    pT_hi[i % 2][:, 8:10, n].bitcast(fp32), ALU.subtract).then_inc(pT_lo_done.sem, 1)

                q_low(0)
                q_low(1)
                for i in range(4 * NP + 1):
                    for a in range(2):
                        if i < 4 * NP:
                            masking(i, a)
                        if 2 * i + a >= 1 and 2 * i + a <= 8 * NP:
                            inverse(*divmod(2 * i + a - 1, 2))
                        if i >= 1:
                            pT_low(i - 1, a)
                        if a == 0 and 2 <= i + 1 < 4 * NP:
                            q_low(i + 1)
                v.drain().then_inc(dve_end.sem, 1)

                phase_begins(v, lay, 1)

                def o_low(p):
                    wait(v, oT_hi_done, lay, p)
                    v.tensor_tensor(oT_lo[p % 2][:], q_raw[:, :, W * p:W * (p + 1)], oT_hi[p % 2][:].bitcast(fp32),
                                    ALU.subtract).then_inc(oT_lo_done.sem, 1)

                def add_attention(p):
                    x = xm[p % 2]
                    wait(v, x_loaded[p % 2], lay, (3, 2)[p % 2] + p // 2)
                    for a in range(2):
                        wait(v, wo_ps, lay, 2 * p + a)
                        v.tensor_tensor(x[:, a, :], PS[0:T, bank_of(MLP_GROUPS, x_added, 2 * p + a), :], x[:, a, :],
                                        ALU.add).then_inc(x_added.sem, 1)
                    wait(v, x_added, lay, 2 * p + 1)
                    norm_stats(lay, NP + p, x)
                    norm_apply(lay, NP + p, x, ym[p % 2])

                o_low(0)
                w_low(lay, wo_lo, wo_hi, w_raw3, 3)
                wait(v, rows_in, lay, 2)
                link(split_row(lay, bo3, row_raw[0:1, 0, :]), lay)
                split_row(lay, b23, row_raw[0:1, 1, :]).then_inc(rows_ready_l.sem, 1)
                o_low(1)
                split_mods(lay, 1, mod3b, mod_rawb)
                add_attention(0)
                for a in range(2):
                    modulate(lay, 2 * NP + a, a, ym[0])
                w_low(lay, w1_lo, w1_hi, w_raw3, 4)
                for a in range(2):
                    yT_low(lay, 2 * NP + a, a, zT_hi, zT_lo)
                w_low(lay, w2_lo, w2_hi, w_raw3, 5)
                for p in range(NP):
                    if p + 1 < NP:
                        add_attention(p + 1)
                    wait(v, h_hi_done, lay, p)
                    v.tensor_tensor(hT_lo[:], hT[:], hT_hi[:].bitcast(fp32), ALU.subtract).then_inc(h_lo_done.sem, 1)
                    if p + 2 < NP:
                        o_low(p + 2)
                    if p + 1 < NP:
                        modulate(lay, 2 * NP + 2 * p + 2, 0, ym[(p + 1) % 2])
                    for a in range(2):
                        wait(v, w2_ps, lay, 2 * p + a)
                        x = xm[p % 2]
                        v.tensor_tensor(x[:, a, :], PS[0:T, bank_of(MLP_GROUPS, x_done, 2 * p + a), :], x[:, a, :],
                                        ALU.add).then_inc(x_done.sem, 1)
                        if a == 0 and p + 1 < NP:
                            modulate(lay, 2 * NP + 2 * p + 3, 1, ym[(p + 1) % 2])
                    if p + 1 < NP:
                        for a in range(2):
                            yT_low(lay, 2 * NP + 2 * p + 2 + a, a, zT_hi, zT_lo)
                v.drain().then_inc(dve_end.sem, 1)

            phase_begins(v, "final", -1)
            for l in range(2):
                if l:
                    v.wait_ge(r_end[0], 2)
                    v.wait_ge(r_end[1], 2)
                v.wait_ge(r_small_in, 16 * (l + 1))
                gw = cols_all[:, 3, R * 4 * l:R * 4 * (l + 1)].rearrange("p (r c) -> p c r", c=4)
                link(split_row("final", rb3, rb_raw[:]), "final")
                link(v.tensor_copy(gw_hl[:, :, 0:R], gw), "final")
                v.tensor_tensor(gw_hl[:, :, R:2 * R], gw, gw_hl[:, :, 0:R].bitcast(fp32), ALU.subtract)\
                    .then_inc(r_rows_ready, 1)
                for n in range(3):
                    v.wait_ge(r_w_hi, 3 * l + n + 1)
                    v.tensor_tensor(wr_lo[n][:], w_rawr[:], wr_hi[n][:].bitcast(fp32), ALU.subtract).then_inc(r_w_lo, 1)
                for p in range(NP):
                    if l == 0:
                        v.wait_ge(r_x_in, 32 * (p + 1))
                        v.tensor_tensor(xr[:], xr[:], lr[:], ALU.add).then_inc(r_x1_ready, 1)
                        v.wait_ge(r_x1_ready, p + 1)
                        norm_stats("final", p, xr)
                        if p:
                            v.wait_ge(r_hT_ps, 2 * p)
                        norm_apply("final", p, xr, yr)
                        v.tensor_scalar(yr[:], yr[:], 0.0, None, ALU.max).then_inc(r_h_ready, 1)
                    for a in range(2):
                        i = 2 * (NP * l + p) + a
                        v.wait_ge(r_hT_hi, i + 1)
                        n = slice(T * a, T * (a + 1))
                        v.tensor_tensor(rT_lo[:, :, n], PS[:, a, 0:4 * T].rearrange("p (c t) -> p c t", c=4),
                                        rT_hi[:, :, n].bitcast(fp32), ALU.subtract).then_inc(r_hT_lo, 1)
                    for a in range(2):
                        i = 2 * (NP * l + p) + a
                        v.wait_ge(r_gate_ps, i + 1)
                        if i:
                            v.wait_ge(r_m_hi, 2 * i)
                            v.wait_ge(r_m_lo, 2 * i)
                        g = gate_sb[0:T, 0, :]
                        link(v.tensor_copy(g, PS[0:T, 2, 0:R]), "final")
                        link(v.tensor_tensor(g, PS[0:T, 2, R:2 * R], g, ALU.add), "final")
                        v.tensor_tensor(g, PS[0:T, 3, 0:R], g, ALU.add).then_inc(r_gate_exp, 1)
                        v.wait_ge(r_gate_exp, 2 * i + 2)
                        link(v.tensor_scalar(gate_sb[0:T, 1, :], gate_sb[0:T, 1, :], 1.0, None, ALU.add), "final")
                        v.reciprocal(g, gate_sb[0:T, 1, :]).then_inc(r_gate, 1)
                        v.wait_ge(r_gate, i + 1)
                        for r in range(R):
                            v.wait_ge(r_m_hi, 2 * i + r + 1)
                            v.scalar_tensor_tensor(msg_lo[r][:, 2 * p + a, :], PS[0:T, 4 + r, :], gate_sb[0:T, 0, r:r + 1],
                                                   msg_hi[r][:, 2 * p + a, :].bitcast(fp32), ALU.mult, ALU.subtract)\
                                .then_inc(r_m_lo, 1)
                v.drain().then_inc(r_end[2], 1)
                v.wait_ge(r_end[0], 2 * l + 1)
                v.wait_ge(r_end[1], 2 * l + 1)
                for t in range(NT):
                    n = NT * l + t
                    v.wait_ge(r_agg_ps, n + 1)
                    if t >= 2:
                        v.wait_ge(r_out_stored[t % 2], 16 * (n // 2))
                    link(v.tensor_tensor(res[t % 2][:], PS[0:T, t % 2, :], self_term[:, t, :], ALU.add), "final")
                    if l == 0:
                        v.tensor_scalar(res[t % 2][:], res[t % 2][:], 0.0, None, ALU.max).then_inc(r_res_ready, 1)
                    else:
                        v.wait_ge(r_xres_in, 16 * (t + 1))
                        v.tensor_tensor(res[t % 2][:], res[t % 2][:], xres[:], ALU.add).then_inc(r_res_ready, 1)
                v.drain().then_inc(r_end[2], 1)
            assert (links["setup"], links["layer"]) == (chain.setup, chain.layer), links


_INS = ['x', 'src', 'dst', 'edge_type_2', 'node_vec1',
        'L0_gnn_f_w1', 'L0_gnn_f_b1', 'L0_gnn_f_w2', 'L0_gnn_f_b2', 'L0_gnn_s1_w', 'L0_gnn_s1_b', 'L0_gnn_b1_w',
        'L0_gnn_b1_b', 'L0_gnn_wq', 'L0_gnn_bq', 'L0_gnn_wk', 'L0_gnn_bk', 'L0_gnn_wv', 'L0_gnn_bv', 'L0_gnn_wo',
        'L0_gnn_bo', 'L0_gnn_s2_w', 'L0_gnn_s2_b', 'L0_gnn_b2_w', 'L0_gnn_b2_b', 'L0_gnn_m_w1', 'L0_gnn_m_b1',
        'L0_gnn_m_w2', 'L0_gnn_m_b2',
        'L1_gnn_basis1', 'L1_gnn_att1', 'L1_gnn_gate_w1', 'L1_gnn_root1', 'L1_gnn_bias1',
        'L1_gnn_basis2', 'L1_gnn_att2', 'L1_gnn_gate_w2', 'L1_gnn_root2', 'L1_gnn_bias2']
_OUTS = [((1250, 512), 'float32')]
_SCRATCH = [("edge_table", (25088, 2)), ("x_lat", (1250, 512)), ("score_bias", (10, 125, 1254)),
            ("adj_hi", (10, 125, 20, 125)), ("adj_lo", (10, 125, 20, 125)), ("rel_w", (2, 2, 512, 512)),
            ("h_rgcn", (1250, 512))]


def kernel(**inputs):
    import numpy as _np
    import concourse.bacc as _bacc
    from concourse import mybir as _mybir
    from concourse.bass_utils import run_bass_kernel_spmd as _run

    nc = _bacc.Bacc("TRN2", target_bir_lowering=False, num_devices=1)
    arrays, args = {}, []
    for name in _INS:
        a = _np.ascontiguousarray(inputs[name])
        arrays[f"in_{name}_dram"] = a
        args.append(nc.dram_tensor(f"in_{name}_dram", a.shape, _mybir.dt.from_np(a.dtype), kind="ExternalInput").ap())
    for i, (shape, dtype) in enumerate(_OUTS):
        dt = _mybir.dt.from_np(_np.dtype(dtype))
        args.append(nc.dram_tensor(f"out_{i}_dram", shape, dt, kind="ExternalOutput").ap())
    for name, shape in _SCRATCH:
        args.append(nc.dram_tensor(name, shape, _mybir.dt.float32, kind="Internal").ap())
    gnn_kernel(nc, *args)
    r = _run(nc, [arrays], core_ids=[0])
    return r.results[0]["out_0_dram"]
```

```python
import math
import concourse.bass as bass
from concourse import mybir
from contextlib import ExitStack



def gnn_kernel(nc, x_in, src, dst, edge_type, noise,
               f_w1, f_b1, f_w2, f_b2, s1_w, s1_b, b1_w, b1_b, wq, bq, wk, bk, wv, bv, wo, bo,
               s2_w, s2_b, b2_w, b2_b, m_w1, m_b1, m_w2, m_b2,
               basis1, att1, gate_w1, root1, bias1, basis2, att2, gate_w2, root2, bias2, out,
               edge_table, x_lat, score_bias, adj, rel_w, h_rgcn):
    fp32, f32r, bf16, f16 = mybir.dt.float32, mybir.dt.float32r, mybir.dt.bfloat16, mybir.dt.float16
    i32, i16 = mybir.dt.int32, mybir.dt.int16
    ALU, ACT, AX = mybir.AluOpType, mybir.ActivationFunctionType, mybir.AxisListType

    N, D = x_in.shape
    E = src.shape[0]
    T = 125
    NT = N // T
    W = 2 * T
    NP = N // W
    LAYERS = wq.shape[0]
    C = f_w2.shape[0]
    F2 = f_w1.shape[0]
    H = D // 128
    SW = 1254
    SB = SW // 3
    SPLIT = 8 * T
    EPS = 1e-5
    SCALE = 128.0 ** -0.5
    NONE = -1e30
    MAGIC = 1.5 * 2 ** 23
    EC = -(-E // 128)
    NB = 2 * NT
    GE = 256
    NG = (EC * 128 + NB * (GE - 1)) // GE
    TC = NG * GE // 128
    R, B = att1.shape
    QL = 8
    Q = D // 4

    ctx = ExitStack()
    with ctx:
        def sb(name, shape, dt=fp32):
            return ctx.enter_context(nc.sbuf_tensor(name, shape, dt))

        ident = sb("ident", [128, 128])
        ones_r = sb("ones_r", [128, 128], f32r)
        neg_half = sb("neg_half", [128, 2])
        bn = sb("bn", [128, 2, 6])
        mv = sb("mv", [128, 2, 4])
        var_eps = sb("var_eps", [128, 2, 2])
        rstd = sb("rstd", [128, 2, 2])
        cols_all = sb("cols_all", [128, 4, LAYERS * H])
        rows_all = sb("rows_all", [4 * LAYERS * H, 128])
        bq_col = sb("bq_col", [128, H])
        bk_col = sb("bk_col", [128, H])
        b1_col = sb("b1_col", [128, H])
        row_max = sb("row_max", [128, 4])
        neg_max = sb("neg_max", [128, 4])
        den = sb("den", [128, 4])
        has_edge = sb("has_edge", [128, 4])
        inv_den = sb("inv_den", [128, 4])
        wait_slot = sb("wait_slot", [1, 1])
        pool_slot = sb("pool_slot", [1, 9])
        gate_sb = sb("gate_sb", [128, 2, R])
        large = sb("large", [1, 1])
        large_flag = sb("large_flag", [1, 1], i32)

        BASE = (nc.sbuf_base + 63) // 64 * 64
        END = nc.sbuf_usable_end

        class Map:
            def __init__(self, at):
                self.at = at

            def __call__(self, name, shape, dt=fp32):
                size = 2 if dt in (bf16, f16, i16) else 4
                for n in shape[1:]:
                    size *= n
                t = nc.alloc_sbuf_tensor_at(name, shape, dt, offset=self.at)
                self.at += (size + 31) // 32 * 32
                assert self.at <= END, (name, self.at, END)
                return t

        m = Map(BASE)
        k_hi = m("k_hi", [128, H, SW], f32r)
        k_lo = m("k_lo", [128, H, SW], f32r)
        v_hi = m("v_hi", [T, NT, D], f32r)
        v_lo = m("v_lo", [T, NT, D], f32r)
        q_raw = m("q_raw", [128, H, N])
        SCRATCH0 = m.at
        cond3 = m("cond3", [96, N], f32r)
        SCRATCH = m.at

        TOP = END // 64 * 64 - 5 * 4 * D * 2
        m = Map(TOP)
        w_raw = m("w_raw", [128, 4, D])
        mod3 = [m("scale3", [96, D], f32r), m("bias3", [96, D], f32r)]
        mod_raw = [m("scale_raw", [17, D]), m("bias_raw", [17, D])]
        x_first = m("x_first", [T, 2, D])

        AHEAD = TOP - 2 * 4 * 4 * D - 3 * 4 * 2 * D
        m = Map(AHEAD)
        x_slot = [x_first, m("x_second", [T, 2, D])]
        yt = [m(f"yt{i}", [T, 2, D]) for i in range(2)]
        wk_hi, wk_lo = m("wk_hi", [128, 4, D], f32r), m("wk_lo", [128, 4, D], f32r)
        m = Map(SCRATCH)
        wq_hi, wq_lo = m("wq_hi", [128, 4, D], f32r), m("wq_lo", [128, 4, D], f32r)
        wv_hi, wv_lo = m("wv_hi", [128, 4, D], f32r), m("wv_lo", [128, 4, D], f32r)
        bv3 = m("bv3", [128, D], f32r)
        bv_raw = m("bv_raw", [1, D])
        yT_hi = [m(f"yT_hi{i}", [128, 4, W], f32r) for i in range(2)]
        yT_lo = [m(f"yT_lo{i}", [128, 4, W], f32r) for i in range(2)]
        assert m.at <= AHEAD

        m = Map(SCRATCH)
        q_hi = m("q_hi", [128, H, W], f32r)
        q_lo = m("q_lo", [128, H, W], f32r)
        pT_hi = [m(f"pT_hi{i}", [T, NT, W], f32r) for i in range(2)]
        pT_lo = [m(f"pT_lo{i}", [T, NT, W], f32r) for i in range(2)]
        prob = [m(f"prob{i}", [T, SW]) for i in range(3)]
        sbias = [[m(f"sbias{i}{a}", [T, SW]) for a in range(2)] for i in range(2)]
        assert m.at <= TOP

        m = Map(BASE)
        wo_hi, wo_lo = m("wo_hi", [128, 4, D], f32r), m("wo_lo", [128, 4, D], f32r)
        w1_hi, w1_lo = m("w1_hi", [128, 4, D], f32r), m("w1_lo", [128, 4, D], f32r)
        w2_hi, w2_lo = m("w2_hi", [128, 4, D], f32r), m("w2_lo", [128, 4, D], f32r)
        bo3, b23 = m("bo3", [128, D], f32r), m("b23", [128, D], f32r)
        row_raw = m("row_raw", [1, 2, D])
        assert m.at <= SCRATCH0 - 20000
        m = Map(SCRATCH)
        oT_hi = [m(f"oT_hi{i}", [128, 4, W], f32r) for i in range(2)]
        oT_lo = [m(f"oT_lo{i}", [128, 4, W], f32r) for i in range(2)]
        ym = [m(f"ym{i}", [T, 2, D]) for i in range(2)]
        zT_hi = m("zT_hi", [128, 4, W], f32r)
        zT_lo = m("zT_lo", [128, 4, W], f32r)
        hT = m("hT", [128, 4, W])
        hT_hi = m("hT_hi", [128, 4, W], f32r)
        hT_lo = m("hT_lo", [128, 4, W], f32r)
        assert m.at <= AHEAD

        m = Map(BASE)
        msg_hi = [m(f"msg_hi{r}", [T, NT, D], f32r) for r in range(R)]
        msg_lo = [m(f"msg_lo{r}", [T, NT, D], f32r) for r in range(R)]
        self_term = m("self_term", [T, NT, D])
        wr_hi = [m(f"wr_hi{i}", [128, 4, D], f32r) for i in range(3)]
        wr_lo = [m(f"wr_lo{i}", [128, 4, D], f32r) for i in range(3)]
        w_rawr = m("w_rawr", [128, 4, D])
        rb3 = m("rb3", [128, D], f32r)
        gw_hl = m("gw_hl", [128, 4, 2 * R], f32r)
        RG = m.at
        rb_raw = m("rb_raw", [1, D])
        xr = [m(f"xr{i}", [T, 2, D]) for i in range(2)]
        lr = [m(f"lr{i}", [T, 2, D]) for i in range(2)]
        yr = [m(f"yr{i}", [T, 2, D]) for i in range(2)]
        rT_hi = [m(f"rT_hi{i}", [128, 4, W], f32r) for i in range(2)]
        rT_lo = [m(f"rT_lo{i}", [128, 4, W], f32r) for i in range(2)]
        m = Map(RG)
        adj16 = [m(f"adj16{i}", [T, NB, T], i16) for i in range(2)]
        adj_hi = [m(f"adj_hi{i}", [T, NB, T], f32r) for i in range(2)]
        adj_lo = m("adj_lo", [T, NB, T], f32r)
        res = [m(f"res{i}", [T, D]) for i in range(2)]
        xres = [m(f"xres{i}", [T, D]) for i in range(2)]

        m = Map(BASE)
        src_i, dst_i, typ_i = m("src_i", [128, EC], i32), m("dst_i", [128, EC], i32), m("typ_i", [128, EC], i32)
        dst_f, typ_f, tile_f = m("dst_f", [128, EC]), m("typ_f", [128, EC]), m("tile_f", [128, EC])
        bucket = m("bucket", [128, EC])
        bucket_id = m("bucket_id", [128, NB])
        mask = m("mask", [128, NB, EC], bf16)
        lower = m("lower", [128, 128], bf16)
        ones_b = m("ones_b", [128, 128], bf16)
        rank = m("rank", [128, NB, EC])
        tot = m("tot", [128, NB, EC])
        upto = m("upto", [128, NB, EC])
        begin = m("begin", [128, NB])
        grp = m("grp", [128, NB])
        gpre = [m(f"gpre{i}", [128, NB]) for i in range(2)]
        pos = m("pos", [128, EC])
        pos_hi = m("pos_hi", [128, EC])
        row_i = m("row_i", [128, EC], i32)
        payload = m("payload", [128, EC, 2])
        empty = m("empty", [128, TC * 2])
        group_no = m("group_no", [1, NG])
        group_ge = m("group_ge", [1, NG, NB])
        ph = m("ph", [F2, N])
        ph_int = m("ph_int", [F2, N])
        freq_off = m("freq_off", [F2, 2])
        freq_i = m("freq_i", [F2, 1])
        fw1 = m("fw1", [F2, C])
        fw2 = m("fw2", [C, C])
        fb = m("fb", [C, 4])
        z1 = m("z1", [C, N])
        z2 = m("z2", [C, N])
        assert m.at <= SCRATCH0
        W_OUT = SCRATCH0 // 64 * 64 - 2 * 4 * D
        assert m.at <= W_OUT
        m = Map(W_OUT)
        w_out = [m(f"w_out{i}", [128, D]) for i in range(2)]
        m = Map(SCRATCH)
        group_tile = m("group_tile", [1, NG], i32)
        table = m("table", [128, TC, 2])
        basis_t = [m(f"basis_t{i}", [4 * B, QL, D]) for i in range(3)]
        att_z = [m(f"att_z{l}", [4 * B, 15 + 128]) for l in range(2)]
        x0 = [m(f"x0{i}", [T, 2, D]) for i in range(NP)]
        m = Map(BASE)
        count = m("count", [T, NB, SW], i16)
        COUNT_END = m.at
        count_add = [m(f"count_add{i}", [T, SW], i16) for i in range(2)]
        node_no = m("node_no", [128, SW], f16)
        src_hot = [m(f"src_hot{i}", [128, 2, SW], bf16) for i in range(2)]
        dst_hot = [m(f"dst_hot{i}", [128, 2, 128], bf16) for i in range(2)]
        assert m.at <= SCRATCH0
        m = Map(COUNT_END)
        csum = [m(f"csum{i}", [T, NT, T]) for i in range(2)]
        cnt1 = [m(f"cnt1{i}", [T, SW]) for i in range(2)]
        cnt0 = [m(f"cnt0{i}", [T, SW]) for i in range(2)]
        count_t = [m(f"count_t{i}", [T, NB, T], i16) for i in range(2)]
        assert m.at <= W_OUT

        PS = ctx.enter_context(nc.psum_tensor("PS", [128, 8, 512], fp32))

        class Signal:

            def __init__(self, name, setup=0, layer=0, unit=1):
                self.sem = ctx.enter_context(nc.semaphore(name))
                self.setup, self.layer, self.unit = setup, layer, unit

        def value(s, where, i):
            if isinstance(where, str):
                return ({"setup": 0, "final": s.setup + LAYERS * s.layer}[where] + i + 1) * s.unit
            return where * (s.layer * s.unit) + (s.setup + i + 1) * s.unit

        def wait(eng, s, where, i):
            eng.wait_ge(s.sem, value(s, where, i))

        pe_end = Signal("pe_end", 3, 3)
        act_end = Signal("act_end", 3, 3)
        dve_end = Signal("dve_end", 3, 3)
        pool_end = Signal("pool_end", 3, 3)
        ENDS = (pe_end, act_end, dve_end, pool_end)

        def phase_begins(eng, where, i):
            for s in ENDS:
                wait(eng, s, where, i)

        x_loaded = [Signal(f"x_loaded{i}", (4, 3)[i], (5, 3)[i], 16) for i in range(2)]
        var_ready = Signal("var_ready", 7, 10)
        rstd_ready = Signal("rstd_ready", 7, 10)
        x_used = Signal("x_used", 7, 10)
        MLP_NORM = (3, 4, 6, 8, 9)
        NEXT_NORM = (5, 7)
        chain = Signal("chain", 56, 89)
        const_ready = Signal("const_ready")
        mod_raw_in = Signal("mod_raw_in", 1, 2, 64)
        mod_ready = Signal("mod_ready", 1, 2)
        mod_ps = Signal("mod_ps", 0, 20)
        y_ready = Signal("y_ready", 0, 20)
        yT_ps = Signal("yT_ps", 0, 20)
        yT_hi_done = Signal("yT_hi_done", 0, 20)
        yT_lo_done = Signal("yT_lo_done", 0, 20)
        w_in = Signal("w_in", 2, 6, 16)
        w_hi_done = Signal("w_hi_done", 1, 6)
        w_lo_done = Signal("w_lo_done", 1, 6)
        cols_ready = Signal("cols_ready", 0, 1)
        rows_in = Signal("rows_in", 0, 3, 16)
        rows_ready_l = Signal("rows_ready_l", 0, 2)
        k_ps = Signal("k_ps", 0, 20)
        q_ps = Signal("q_ps", 0, 20)
        v_ps = Signal("v_ps", 0, 10)
        k_hi_done = Signal("k_hi_done", 0, 20)
        k_lo_done = Signal("k_lo_done", 0, 20)
        q_done = Signal("q_done", 0, 20)
        v_hi_done = Signal("v_hi_done", 0, 10)
        v_lo_done = Signal("v_lo_done", 0, 10)
        sbias_in = [Signal(f"sbias_in{i}{a}", 0, 3 - i, 16) for i in range(2) for a in range(2)]
        q_hi_done = Signal("q_hi_done", 0, 20)
        q_lo_done = Signal("q_lo_done", 0, 20)
        s_ps = Signal("s_ps", 0, 40)
        masked = Signal("masked", 0, 40)
        negmax_ready = Signal("negmax_ready", 0, 40)
        exp_done = Signal("exp_done", 0, 40)
        inv_ready = Signal("inv_ready", 0, 40)
        normed = Signal("normed", 0, 40)
        rest_normed = Signal("rest_normed", 0, 40)
        pT_ps = Signal("pT_ps", 0, 40)
        pT_hi_done = Signal("pT_hi_done", 0, 40)
        pT_lo_done = Signal("pT_lo_done", 0, 40)
        o_ps = Signal("o_ps", 0, 20)
        o_done = Signal("o_done", 0, 20)
        oT_hi_done = Signal("oT_hi_done", 0, 5)
        oT_lo_done = Signal("oT_lo_done", 0, 5)
        wo_ps = Signal("wo_ps", 0, 10)
        x_added = Signal("x_added", 0, 10)
        w1_ps = Signal("w1_ps", 0, 20)
        h_done = Signal("h_done", 0, 20)
        h_lo_done = Signal("h_lo_done", 0, 20)
        w2_ps = Signal("w2_ps", 0, 10)
        x_done = Signal("x_done", 0, 10)
        x_stored = [Signal(f"x_stored{i}", (3, 2)[i], (3, 2)[i], 16) for i in range(2)]

        def plain(name):
            return ctx.enter_context(nc.semaphore(name))

        (consts, edges_in, noise_in, fw_in, att_in, sp_passed, bias_cols_ps, table_filled, table_in, h0_ready) = map(plain, (
             "consts", "edges_in", "noise_in", "fw_in", "att_in", "sp_passed", "bias_cols_ps", "table_filled", "table_in", "h0_ready"))
        (edge_pads, empty_ready, mask_ready, rank_ps, rank_out, tot_out, rows_ready, scattered, freq_ready,
         phase_ready, sin_done, z1_ps, z1_exp, silu_done, z2_ps, cond_ready, basis_ps, basis_out,
         basis_used, att_zeroed) = map(plain, (
             "edge_pads", "empty_ready", "mask_ready", "rank_ps", "rank_out", "tot_out", "rows_ready",
             "scattered", "freq_ready", "phase_ready", "sin_done", "z1_ps", "z1_exp", "silu_done", "z2_ps",
             "cond_ready", "basis_ps", "basis_out", "basis_used", "att_zeroed"))
        basis_in = [plain(f"basis_in{i}") for i in range(3)]
        w_stored = [plain(f"w_stored{i}") for i in range(2)]
        (hot_ready, group_out, count_ps, count_added, node_no_ready, csum_ready, csumT_ps, cnt1_ready, ln_done, sbias_ready,
         count_t_done) = map(plain, (
             "hot_ready", "group_out", "count_ps", "count_added", "node_no_ready", "csum_ready", "csumT_ps", "cnt1_ready", "ln_done",
             "sbias_ready", "count_t_done"))
        adj_stored = [plain(f"adj_stored{i}") for i in range(2)]
        sbias_stored = [plain(f"sbias_stored{i}") for i in range(2)]
        (r_small_in, r_rows_ready, r_w_in, r_w_hi, r_w_lo, r_x1_ready, r_h_ready,
         r_hT_ps, r_hT_hi, r_hT_lo, r_gate_ps, r_gate_exp, r_gate, r_mm_ps, r_m_hi, r_m_lo, r_self_out,
         r_agg_ps, r_res_ready, r_adj_hi, r_adj_lo) = map(plain, (
             "r_small_in", "r_rows_ready", "r_w_in", "r_w_hi", "r_w_lo", "r_x1_ready",
             "r_h_ready", "r_hT_ps", "r_hT_hi", "r_hT_lo", "r_gate_ps", "r_gate_exp", "r_gate",
             "r_mm_ps", "r_m_hi", "r_m_lo", "r_self_out", "r_agg_ps", "r_res_ready",
             "r_adj_hi", "r_adj_lo"))
        r_out_stored = [plain(f"r_out_stored{i}") for i in range(2)]
        r_x_in = [plain(f"r_x_in{i}") for i in range(2)]
        r_h_in = [plain(f"r_h_in{i}") for i in range(2)]
        r_x1_stored = [plain(f"r_x1_stored{i}") for i in range(2)]
        r_xres_in = [plain(f"r_xres_in{i}") for i in range(2)]
        r_adj_in = [plain(f"r_adj_in{i}") for i in range(2)]
        r_end = [plain(f"r_end_{e}") for e in ("pe", "act", "dve")]

        block = ctx.enter_context(nc.Block())

        QKV_GROUPS = []
        for p in range(NP):
            QKV_GROUPS += [(k_lo_done, 4 * p + c) for c in range(4)]
            QKV_GROUPS += [(q_done, 4 * p + c) for c in range(4)]
            QKV_GROUPS += [(v_lo_done, 2 * p + a) for a in range(2)]
        MLP_GROUPS = [(x_added, 0), (x_added, 1)]
        for p in range(NP):
            if p + 1 < NP:
                MLP_GROUPS += [(x_added, 2 * p + 2), (x_added, 2 * p + 3)]
            MLP_GROUPS += [(h_done, 4 * p + c) for c in range(4)]
            MLP_GROUPS += [(x_done, 2 * p), (x_done, 2 * p + 1)]

        def bank_of(groups, s, i):
            return 4 + groups.index((s, i)) % 4

        def bank_free(eng, groups, s, i, lay):
            n = groups.index((s, i))
            if n >= 4:
                wait(eng, groups[n - 4][0], lay, groups[n - 4][1])

        RC = 2 * EC
        NRC = NB * EC // RC
        CH = ((0, 418), (418, 416), (834, 416))
        NW = 2 * (Q // 16)
        NL = 2 * (Q // QL)
        LOAD_AT, SPLIT_AT = (1, 5, 9), (3, 7, 9)
        NLA = NL - 6

        def pair_rows(a, p):
            return a[W * p:W * (p + 1), :].rearrange("(a t) d -> t a d", t=T)

        @block.sync
        def _(sp):
            def load_mods(where, index, pair):
                for t, (w, b) in zip(mod_raw, pair):
                    sp.dma_start(t[0:C, :], w[bass.ds(index, 1), :, :].rearrange("a p d -> (a p) d"))\
                        .then_inc(mod_raw_in.sem, 16)
                    sp.dma_start(t[C:C + 1, :], b[bass.ds(index, 1), :]).then_inc(mod_raw_in.sem, 16)

            def load_w(where, index, w, n):
                if n or not isinstance(where, str):
                    wait(sp, w_lo_done, where, n - (1 if isinstance(where, str) else 2))
                    sp.sem_inc(sp_passed, 1)
                sp.dma_start(w_raw[:], w[bass.ds(index, 1), :, :].rearrange("a (c p) d -> p (a c) d", p=128))\
                    .then_inc(w_in.sem, 16)

            sp.wait_ge(edge_pads, 3)
            full = E // EC
            for t, a in ((src_i, src), (dst_i, dst), (typ_i, edge_type)):
                sp.dma_start(t[0:full, :], a[0:full * EC].rearrange("(p c) -> p c", c=EC)).then_inc(edges_in, 16)
                sp.dma_start(t[full:full + 1, 0:E - full * EC],
                             a[full * EC:E].rearrange("(p c) -> p c", p=1)).then_inc(edges_in, 16)
            sp.dma_start(ph[:], noise.rearrange("n a -> (a n)").partition_broadcast(F2)).then_inc(noise_in, 16)
            sp.dma_start(fw1[:], f_w1).then_inc(fw_in, 16)
            sp.dma_start(fw2[:], f_w2).then_inc(fw_in, 16)
            sp.dma_start(fb[:, 0:1], f_b1.rearrange("(p a) -> p a", a=1)).then_inc(fw_in, 16)
            sp.dma_start(fb[:, 1:2], f_b2.rearrange("(p a) -> p a", a=1)).then_inc(fw_in, 16)
            for b, a in enumerate((bk, bq, m_b1)):
                sp.dma_start(rows_all[LAYERS * H * b:LAYERS * H * (b + 1), :],
                             a.rearrange("l (c p) -> (l c) p", p=128)).then_inc(fw_in, 16)
            for l, a in enumerate((gate_w1, gate_w2)):
                r0 = 4 * LAYERS * H - 2 * R * 4 + R * 4 * l
                sp.dma_start(rows_all[r0:r0 + R * 4, :],
                             a.rearrange("r (c p) a -> (r c) (p a)", p=128)).then_inc(fw_in, 16)
            sp.wait_ge(att_zeroed, 2)
            for l, att in enumerate((att1, att2)):
                for r in range(R):
                    for ii in range(4):
                        col = 15 + 64 * r + 16 * ii
                        sp.dma_start(att_z[l][ii * B:(ii + 1) * B, col:col + 1],
                                     att[r, :].rearrange("(b a) -> b a", a=1)).then_inc(att_in, 16)
            sp.wait_ge(empty_ready, 1)
            sp.dma_start(edge_table.rearrange("(p c) k -> p (c k)", c=TC), empty[:]).then_inc(table_filled, 16)

            def load_bases(n):
                l, q0 = divmod(n * QL, Q)
                if n >= 3:
                    sp.wait_ge(basis_used, n - 2)
                rows = (basis1, basis2)[l].rearrange("b (i q) d -> i b q d", q=Q)
                for ii in range(4):
                    sp.dma_start(basis_t[n % 3][ii * B:(ii + 1) * B, :, :], rows[ii, :, q0:q0 + QL, :])\
                        .then_inc(basis_in[n % 3], 16)

            for n in range(NLA + 3):
                load_bases(n)
            load_mods("setup", 0, ((s1_w, s1_b), (b1_w, b1_b)))
            load_w("setup", 0, wk, 0)
            sp.wait_ge(scattered, 16 * EC)
            sp.dma_start(table[:].rearrange("p c k -> p (c k)"),
                         edge_table.rearrange("(p c) k -> p (c k)", c=TC)).then_inc(table_in, 16)
            for t in range(NT):
                sp.wait_ge(count_t_done, t + 1)
                if t == 0:
                    for p in range(2):
                        wait(sp, x_stored[p], "setup", (3, 2)[p] - 1)
                        sp.dma_start(x_slot[p][:], pair_rows(x_lat, p)).then_inc(x_loaded[p].sem, 16)
                sp.dma_start(adj[t, :, :, :], count_t[t % 2][:]).then_inc(adj_stored[t % 2], 16)
                if NLA + 3 + t < NL:
                    load_bases(NLA + 3 + t)
                sp.wait_ge(sbias_ready, t + 1)
                sp.dma_start(score_bias[t, :, :], cnt0[t % 2][:]).then_inc(sbias_stored[t % 2], 16)
            load_w("setup", 0, wq, 1)
            for i in range(2):
                sp.wait_ge(sbias_stored[i], 16 * NT // 2)

            with sp.Fori(0, LAYERS) as lay:
                def load_x(p):
                    sp.dma_start(x_slot[p % 2][:], pair_rows(x_lat, p)).then_inc(x_loaded[p % 2].sem, 16)

                phase_begins(sp, lay, -1)
                for p in range(2):
                    wait(sp, x_stored[p], lay, -1)
                    sp.sem_inc(sp_passed, 1)
                for p in range(2, 4):
                    load_x(p)
                sp.dma_start(bv_raw[:], bv[bass.ds(lay, 1), :]).then_inc(rows_in.sem, 16)
                load_w(lay, lay, wv, 2)
                for p in range(4, NP):
                    wait(sp, x_used, lay, p - 4)
                    load_x(p)

                phase_begins(sp, lay, 0)
                for p in range(NP):
                    for a in range(2):
                        if p >= 2:
                            wait(sp, masked, lay, 8 * (p - 2) + 6 + a)
                        sp.dma_start(sbias[p % 2][a][:], score_bias[2 * p + a, :, :])\
                            .then_inc(sbias_in[2 * (p % 2) + a].sem, 16)
                    if p == 1:
                        load_x(0)
                        wait(sp, mod_ready, lay, -1)
                        sp.sem_inc(sp_passed, 1)
                        load_mods(lay, lay, ((s2_w, s2_b), (b2_w, b2_b)))
                        load_w(lay, lay, wo, 3)

                phase_begins(sp, lay, 1)
                sp.dma_start(row_raw[0:1, 0, :], bo[bass.ds(lay, 1), :]).then_inc(rows_in.sem, 16)
                sp.dma_start(row_raw[0:1, 1, :], m_b2[bass.ds(lay, 1), :]).then_inc(rows_in.sem, 16)
                load_x(1)
                load_w(lay, lay, m_w1, 4)
                load_w(lay, lay, m_w2, 5)
                following = (lay + 1) % LAYERS
                wait(sp, mod_ready, lay, 0)
                sp.sem_inc(sp_passed, 1)
                load_mods(lay, following, ((s1_w, s1_b), (b1_w, b1_b)))
                load_w(lay, following, wk, 6)
                for p in range(NP):
                    wait(sp, x_done, lay, 2 * p + 1)
                    sp.dma_start(pair_rows(x_lat, p), x_slot[p % 2][:]).then_inc(x_stored[p % 2].sem, 16)
                    if p + 2 < NP:
                        wait(sp, x_stored[p % 2], lay, p // 2)
                        if p < 2:
                            sp.sem_inc(sp_passed, 1)
                            wait(sp, x_used, lay, NEXT_NORM[p])
                        load_x(p + 2)
                load_w(lay, following, wq, 7)

            phase_begins(sp, "final", -1)
            wait(sp, x_stored[0], "final", -1)
            wait(sp, x_stored[1], "final", -1)
            weights = [(rel_w[l, 0, :, :], rel_w[l, 1, :, :], root) for l, root in enumerate((root1, root2))]

            def load_r(l, n):
                if 3 * l + n:
                    sp.wait_ge(r_w_lo, 3 * l + n)
                sp.dma_start(w_rawr[:], weights[l][n].rearrange("(c p) d -> p c d", p=128)).then_inc(r_w_in, 16)

            def load_sum(p):
                sp.dma_start(xr[p % 2][:], pair_rows(x_in, p)).then_inc(r_x_in[p % 2], 16)
                sp.dma_start(lr[p % 2][:], pair_rows(x_lat, p)).then_inc(r_x_in[p % 2], 16)

            for l, bias in enumerate((bias1, bias2)):
                if l:
                    for s in r_end:
                        sp.wait_ge(s, 2)
                    for i in range(2):
                        sp.wait_ge(r_out_stored[i], 16 * NT // 2)
                    for p in range(NP):
                        if p >= 2:
                            sp.wait_ge(r_hT_ps, 2 * (NP + p - 1))
                        sp.dma_start(yr[p % 2][:], pair_rows(h_rgcn, p)).then_inc(r_h_in[p % 2], 16)
                        if p == 1:
                            sp.dma_start(rb_raw[:], bias.rearrange("(a n) -> a n", a=1)).then_inc(r_small_in, 16)
                else:
                    load_sum(0)
                    load_r(0, 0)
                    load_sum(1)
                    sp.dma_start(rb_raw[:], bias.rearrange("(a n) -> a n", a=1)).then_inc(r_small_in, 16)
                    load_r(0, 1)
                    load_r(0, 2)
                    for p in range(NP):
                        sp.wait_ge(r_x1_ready, p + 1)
                        sp.dma_start(pair_rows(x_lat, p), xr[p % 2][:]).then_inc(r_x1_stored[p % 2], 16)
                        if p + 2 < NP:
                            sp.wait_ge(r_h_ready, p + 1)
                            sp.wait_ge(r_x1_stored[p % 2], 16 * (p // 2 + 1))
                            load_sum(p + 2)
                for s in r_end:
                    sp.wait_ge(s, 2 * l + 1)
                for i in range(2):
                    sp.wait_ge(adj_stored[i], 16 * NT // 2)
                    sp.wait_ge(r_x1_stored[i], 16 * ((NP + 1 - i) // 2))

                def store_result(t):
                    sp.wait_ge(r_res_ready, NT * l + t + 1)
                    sp.dma_start((h_rgcn, out)[l][T * t:T * (t + 1), :], res[t % 2][:]).then_inc(r_out_stored[t % 2], 16)

                for t in range(NT):
                    n = NT * l + t
                    if t >= 2:
                        sp.wait_ge(r_adj_lo, n - 1)
                    sp.dma_start(adj16[t % 2][:], adj[t, :, :, :]).then_inc(r_adj_in[t % 2], 16)
                    if t >= 2:
                        store_result(t - 2)
                    if l:
                        sp.dma_start(xres[t % 2][:], x_lat[T * t:T * (t + 1), :]).then_inc(r_xres_in[t % 2], 16)
                    elif t in LOAD_AT:
                        load_r(1, LOAD_AT.index(t))
                store_result(NT - 2)
                store_result(NT - 1)
            for i in range(2):
                sp.wait_ge(r_out_stored[i], 16 * NT)

        @block.gpsimd
        def _(pool):
            pool.memset(src_i[:], -1).then_inc(edge_pads, 1)
            pool.memset(dst_i[:], 0).then_inc(edge_pads, 1)
            pool.memset(typ_i[:], 0).then_inc(edge_pads, 1)
            for l in range(2):
                pool.memset(att_z[l][:], 0.0).then_inc(att_zeroed, 1)
            pool.memset(pool_slot[:], 0.0)
            pool.memset(neg_half[:], -0.5).then_inc(consts, 1)
            pool.memset(empty[:], -1.0).then_inc(empty_ready, 1)
            pool.iota(freq_i[:].bitcast(i32), [[0, 1]], base=0, channel_multiplier=1).then_inc(freq_ready, 1)
            pool.memset(lower[:], 1.0).then_inc(consts, 1)
            pool.memset(ones_b[:], 1.0).then_inc(consts, 1)
            pool.memset(ident[:], 0.0).then_inc(consts, 1)
            pool.wait_ge(consts, 4)
            pool.affine_select(out=lower[:], in_=lower[:], compare_op=ALU.is_gt, fill=0.0, base=0,
                               pattern=[[1, 128]], channel_multiplier=-1).then_inc(consts, 1)
            pool.affine_select(out=ident[:], in_=ident[:], compare_op=ALU.not_equal, fill=1.0, base=0,
                               pattern=[[-1, 128]], channel_multiplier=1).then_inc(consts, 1)
            pool.iota(bucket_id[:], [[1, NB]], base=0, channel_multiplier=0,
                      allow_small_or_imprecise_dtypes=True).then_inc(consts, 1)
            pool.iota(group_no[:], [[1, NG]], base=0, channel_multiplier=0,
                      allow_small_or_imprecise_dtypes=True).then_inc(consts, 1)

            def inv_std(where, i):
                s = i % 2
                wait(pool, var_ready, where, i)
                pool.tensor_tensor(rstd[0:T, s, :], var_eps[0:T, s, :], neg_half[0:T, :], ALU.pow)\
                    .then_inc(rstd_ready.sem, 1)

            pool.wait_ge(rows_ready, 1)
            pool.wait_ge(table_filled, 16)
            for c in range(EC):
                pool.indirect_dma_start(edge_table, bass.IndirectOffsetOnAxis(ap=row_i[:, c:c + 1], axis=0),
                                        payload[:, c, :], None).then_inc(scattered, 16)
                if c % 12 == 11 and c // 12 < NP:
                    inv_std("setup", c // 12)
            pool.iota(node_no[:], [[1, SW]], base=0, channel_multiplier=0,
                      allow_small_or_imprecise_dtypes=True).then_inc(node_no_ready, 1)
            pool.drain().then_inc(pool_end.sem, 1)
            phase_begins(pool, "setup", 0)
            pool.drain().then_inc(pool_end.sem, 1)
            phase_begins(pool, "setup", 1)
            for p in range(2):
                inv_std("setup", NP + p)
            pool.drain().then_inc(pool_end.sem, 1)

            with pool.Fori(0, LAYERS) as lay:
                phase_begins(pool, lay, -1)
                for i in range(3):
                    inv_std(lay, i)
                pool.drain().then_inc(pool_end.sem, 1)
                phase_begins(pool, lay, 0)
                for u in range(8 * NP):
                    wait(pool, inv_ready, lay, u)
                    pool.tensor_tensor(pool_slot[0:1, 1 + u % 8:2 + u % 8], pool_slot[0:1, 0:1], pool_slot[0:1, 0:1], ALU.mult)
                    pool.tensor_scalar(prob[u % 3][:, 0:SPLIT], prob[u % 3][:, 0:SPLIT], inv_den[0:T, u % 4:u % 4 + 1], None, ALU.mult)\
                        .then_inc(normed.sem, 1)
                pool.drain().then_inc(pool_end.sem, 1)
                phase_begins(pool, lay, 1)
                for i in range(3, 10):
                    inv_std(lay, i)
                pool.drain().then_inc(pool_end.sem, 1)

            phase_begins(pool, "final", -1)
            for p in range(NP):
                inv_std("final", p)

        @block.tensor
        def _(pe):
            pe.wait_ge(consts, 6)
            pe.wait_ge(mask_ready, 1)
            mask_f = mask[:].rearrange("p k c -> p (k c)")
            for c in range(NRC):
                if c >= 2:
                    pe.wait_ge(rank_out, c - 1)
                    pe.wait_ge(tot_out, c - 1)
                cols = mask_f[:, c * RC:(c + 1) * RC]
                pe.matmul(PS[:, c % 2, 0:RC], lower[:], cols, start=True, stop=True)
                pe.matmul(PS[:, 2 + c % 2, 0:RC], ones_b[:], cols, start=True, stop=True).then_inc(rank_ps, 1)
            pe.wait_ge(fw_in, 16 * 9)
            pe.transpose(PS[:, 7, 0:4 * LAYERS * H], rows_all[:], ident[0:4 * LAYERS * H, 0:4 * LAYERS * H])\
                .then_inc(bias_cols_ps, 1)
            pe.wait_ge(sin_done, 1)
            for j, (c0, cn) in enumerate(CH):
                z = pe.matmul(PS[0:C, 4 + j, 0:cn], fw1[:], ph[:, c0:c0 + cn], start=True, stop=True)
            z.then_inc(z1_ps, 1)
            pe.wait_ge(att_in, 16 * 2 * R * 4)
            pe.wait_ge(rank_out, NRC)

            def relation_weights(load, bank):
                n = load // 2
                if load % 2 == 0 and n >= 2:
                    pe.wait_ge(basis_out, n - 1)
                pe.wait_ge(basis_in[load % 3], 64 * (load // 3 + 1))
                for q in range(QL):
                    row = QL * (load % 2) + q
                    g = pe.matmul(PS[:, bank, :], att_z[n // (NW // 2)][:, 15 - row:143 - row],
                                  basis_t[load % 3][:, q, :], start=(row == 0), stop=(row == 15))
                g.then_inc(basis_used, 1)

            for load in range(NLA):
                if load == 8:
                    pe.wait_ge(silu_done, 1)
                    for j, (c0, cn) in enumerate(CH):
                        z = pe.matmul(PS[0:C, 4 + j, 0:cn], fw2[:], z1[:, c0:c0 + cn], start=True, stop=True)
                    z.then_inc(z2_ps, 1)
                relation_weights(load, load // 2 % 2)
            pe.drain().then_inc(pe_end.sem, 1)

            phase_begins(pe, "setup", 0)

            def group_counts(it, b, first):
                pe.wait_ge(hot_ready, 2 * it + (b + 1))
                if not first:
                    pe.wait_ge(group_out, 2 * it + (b - 1))
                for h in range(2):
                    for j in range(3):
                        g = pe.matmul(PS[0:T, 3 * b + j, 0:SB], dst_hot[b][:, h, 0:T],
                                      src_hot[b][:, h, SB * j:SB * (j + 1)], start=(h == 0), stop=(h == 1))
                g.then_inc(count_ps, 1)

            for b in range(2):
                group_counts(0, b, True)
            with pe.Fori(1, NG // 2) as it:
                for b in range(2):
                    group_counts(it, b, False)
            pe.drain().then_inc(pe_end.sem, 1)

            phase_begins(pe, "setup", 1)
            for t in range(NT):
                pe.wait_ge(csum_ready, t + 1)
                if t >= 2:
                    pe.wait_ge(cnt1_ready, t - 1)
                for k in range(NT):
                    g = pe.transpose(PS[0:T, 3 * (t % 2) + k // 4, T * (k % 4):T * (k % 4 + 1)],
                                     csum[t % 2][:, k, :], ident[0:T, 0:T])
                g.then_inc(csumT_ps, 1)
                if NLA + t < NL:
                    relation_weights(NLA + t, 6 + (NLA + t) // 2 % 2)
            pe.drain().then_inc(pe_end.sem, 1)

            def mods(lay, ph, p, a, mod):
                i = NP * 2 * ph + 2 * p + a
                if i % 10:
                    wait(pe, y_ready, lay, i - 1)
                else:
                    wait(pe, mod_ready, lay, ph - 1)
                nodes = cond3[:, W * p + T * a:W * p + T * (a + 1)]
                for b in range(2):
                    g = pe.matmul(PS[0:T, b, :], nodes, mod[b][:], start=True, stop=True)
                g.then_inc(mod_ps.sem, 1)

            def transposed(lay, ph, p, a, y):
                i = NP * 2 * ph + 2 * p + a
                wait(pe, y_ready, lay, i)
                if i % 10 >= 2:
                    wait(pe, yT_lo_done, lay, i - 2)
                for c in range(4):
                    g = pe.transpose(PS[:, 2 + a, T * c:T * (c + 1)], y[:, a, 128 * c:128 * (c + 1)], ident[0:T, 0:T])
                g.then_inc(yT_ps.sem, 1)

            def columns(bank, c, w_hi, w_lo, x_hi, x_lo, x_lo_ready):
                o = PS[:, bank, 0:W]
                f = slice(128 * c, 128 * (c + 1))
                for k in range(4):
                    pe.matmul(o, w_hi[:, k, f], x_hi[:, k, :], start=(k == 0), stop=False)
                    pe.matmul(o, w_lo[:, k, f], x_hi[:, k, :], start=False, stop=False)
                x_lo_ready()
                for k in range(4):
                    g = pe.matmul(o, w_hi[:, k, f], x_lo[:, k, :], start=False, stop=(k == 3))
                return g

            def rows(bank, a, x_hi, x_lo, w_hi, w_lo, row3, before=None):
                o = PS[0:T, bank, :]
                n = slice(T * a, T * (a + 1))
                for k in range(4):
                    if before:
                        before(k)
                    pe.matmul(o, x_hi[:, k, n], w_hi[:, k, :], start=(k == 0), stop=False)
                    pe.matmul(o, x_hi[:, k, n], w_lo[:, k, :], start=False, stop=False)
                    g = pe.matmul(o, x_lo[:, k, n], w_hi[:, k, :], start=False, stop=(row3 is None and k == 3))
                if row3 is not None:
                    if before:
                        before(4)
                    g = pe.matmul(o, ones_r[:, 0:T], row3[:], start=False, stop=True)
                return g

            with pe.Fori(0, LAYERS) as lay:
                phase_begins(pe, lay, -1)
                for a in range(2):
                    mods(lay, 0, 0, a, mod3)
                for a in range(2):
                    transposed(lay, 0, 0, a, yt[0])
                for p in range(NP):
                    s = p % 2
                    if p + 1 < NP:
                        mods(lay, 0, p + 1, 0, mod3)
                    wait(pe, yT_hi_done, lay, 2 * p + 1)

                    def lo_ready():
                        wait(pe, yT_lo_done, lay, 2 * p + 1)

                    if p == 0:
                        wait(pe, w_lo_done, lay, 0 - 1)
                    for c in range(4):
                        bank_free(pe, QKV_GROUPS, k_lo_done, 4 * p + c, lay)
                        columns(bank_of(QKV_GROUPS, k_lo_done, 4 * p + c), c, wk_hi, wk_lo, yT_hi[s], yT_lo[s],
                                lo_ready).then_inc(k_ps.sem, 1)
                    if p + 1 < NP:
                        mods(lay, 0, p + 1, 1, mod3)
                    if p == 0:
                        wait(pe, w_lo_done, lay, 1 - 1)
                    for c in range(4):
                        bank_free(pe, QKV_GROUPS, q_done, 4 * p + c, lay)
                        columns(bank_of(QKV_GROUPS, q_done, 4 * p + c), c, wq_hi, wq_lo, yT_hi[s], yT_lo[s],
                                lo_ready).then_inc(q_ps.sem, 1)
                    if p + 1 < NP:
                        transposed(lay, 0, p + 1, 0, yt[(p + 1) % 2])
                    if p == 0:
                        wait(pe, w_lo_done, lay, 2 - 1)
                        wait(pe, rows_ready_l, lay, 0)
                    for a in range(2):
                        bank_free(pe, QKV_GROUPS, v_lo_done, 2 * p + a, lay)
                        rows(bank_of(QKV_GROUPS, v_lo_done, 2 * p + a), a, yT_hi[s], yT_lo[s], wv_hi, wv_lo,
                             bv3).then_inc(v_ps.sem, 1)
                    if p + 1 < NP:
                        transposed(lay, 0, p + 1, 1, yt[(p + 1) % 2])
                pe.drain().then_inc(pe_end.sem, 1)

                phase_begins(pe, lay, 0)

                def scores(i, a):
                    h = i % 4
                    wait(pe, q_lo_done, lay, i)
                    if 2 * i + a:
                        wait(pe, masked, lay, 2 * i + a - 1)
                    n = slice(T * a, T * (a + 1))
                    for x, (q_t, k_t) in enumerate(((q_hi, k_hi), (q_hi, k_lo), (q_lo, k_hi))):
                        for j in range(3):
                            g = pe.matmul(PS[0:T, j, 0:SB], q_t[:, h, n], k_t[:, h, SB * j:SB * (j + 1)],
                                          start=(x == 0), stop=(x == 2))
                    g.then_inc(s_ps.sem, 1)

                def turn(i, a):
                    u = 2 * i + a
                    wait(pe, normed, lay, u)
                    wait(pe, rest_normed, lay, u)
                    if u:
                        wait(pe, pT_lo_done, lay, u - 1)
                    for k in range(NT):
                        g = pe.transpose(PS[0:T, 3 + k // 4, T * (k % 4):T * (k % 4 + 1)],
                                         prob[u % 3][:, T * k:T * (k + 1)], ident[0:T, 0:T])
                    g.then_inc(pT_ps.sem, 1)

                def values(i, half):
                    h, s = i % 4, i % 2
                    if half == 0:
                        wait(pe, pT_lo_done, lay, 2 * i + 1)
                        if i >= 2:
                            wait(pe, o_done, lay, i - 2)
                    f = slice(128 * h, 128 * (h + 1))
                    for k in range(5 * half, 5 * half + 5):
                        for x, (v_t, p_t) in enumerate(((v_hi, pT_hi[s]), (v_hi, pT_lo[s]), (v_lo, pT_hi[s]))):
                            g = pe.matmul(PS[:, 6 + s, 0:W], v_t[:, k, f], p_t[:, k, :],
                                          start=(k == 0 and x == 0), stop=(k == NT - 1 and x == 2))
                    if half:
                        g.then_inc(o_ps.sem, 1)

                for i in range(4 * NP + 2):
                    for a in range(2):
                        if i < 4 * NP:
                            scores(i, a)
                        if 1 <= i <= 4 * NP:
                            turn(i - 1, a)
                        if i >= 2:
                            values(i - 2, a)
                pe.drain().then_inc(pe_end.sem, 1)

                phase_begins(pe, lay, 1)

                def out_proj(p):
                    wait(pe, oT_lo_done, lay, p)
                    for a in range(2):
                        bank_free(pe, MLP_GROUPS, x_added, 2 * p + a, lay)
                        rows(bank_of(MLP_GROUPS, x_added, 2 * p + a), a, oT_hi[p % 2], oT_lo[p % 2], wo_hi, wo_lo,
                             bo3, lambda k: wait(pe, rows_ready_l, lay, 1) if p == a == 0 and k == 4 else None)\
                            .then_inc(wo_ps.sem, 1)

                wait(pe, w_lo_done, lay, 3 - 1)
                out_proj(0)
                for a in range(2):
                    mods(lay, 1, 0, a, mod3)
                for a in range(2):
                    transposed(lay, 1, 0, a, ym[0])
                for p in range(NP):
                    if p + 1 < NP:
                        out_proj(p + 1)
                    wait(pe, yT_hi_done, lay, 2 * NP + 2 * p + 1)
                    if p == 0:
                        wait(pe, w_lo_done, lay, 4 - 1)
                    for c in range(4):
                        bank_free(pe, MLP_GROUPS, h_done, 4 * p + c, lay)
                        columns(bank_of(MLP_GROUPS, h_done, 4 * p + c), c, w1_hi, w1_lo, zT_hi, zT_lo,
                                lambda: wait(pe, yT_lo_done, lay, 2 * NP + 2 * p + 1)).then_inc(w1_ps.sem, 1)
                    if p + 1 < NP:
                        mods(lay, 1, p + 1, 0, mod3)
                    if p == 0:
                        wait(pe, w_lo_done, lay, 5 - 1)
                    for a in range(2):
                        bank_free(pe, MLP_GROUPS, x_done, 2 * p + a, lay)
                        rows(bank_of(MLP_GROUPS, x_done, 2 * p + a), a, hT_hi, hT_lo, w2_hi, w2_lo, b23,
                             lambda k: wait(pe, h_lo_done, lay, 4 * p + k) if a == 0 and k < 4 else None)\
                            .then_inc(w2_ps.sem, 1)
                        if a == 0 and p + 1 < NP:
                            mods(lay, 1, p + 1, 1, mod3)
                    if p + 1 < NP:
                        for a in range(2):
                            transposed(lay, 1, p + 1, a, ym[(p + 1) % 2])
                pe.drain().then_inc(pe_end.sem, 1)

            phase_begins(pe, "final", -1)
            counts_large = pe.value_load(large_flag[0:1, 0:1], min_val=0, max_val=1)
            for l in range(2):
                if l:
                    pe.wait_ge(r_end[2], 2)
                    pe.wait_ge(r_end[1], 2)

                def turn_nodes(p):
                    n = NP * l + p
                    for a in range(2):
                        if l == 0:
                            pe.wait_ge(r_h_ready, n + 1)
                        else:
                            pe.wait_ge(r_h_in[p % 2], 16 * (p // 2 + 1))
                        if n:
                            pe.wait_ge(r_hT_lo, 2 * n - 1 + a)
                        for c in range(4):
                            g = pe.transpose(PS[:, a, T * c:T * (c + 1)], yr[p % 2][:, a, 128 * c:128 * (c + 1)],
                                             ident[0:T, 0:T])
                        g.then_inc(r_hT_ps, 1)

                turn_nodes(0)
                for p in range(NP):
                    n = NP * l + p
                    for a in range(2):
                        i = 2 * n + a
                        pe.wait_ge(r_hT_lo, i + 1)
                        if i % (2 * NP) == 0:
                            pe.wait_ge(r_rows_ready, l + 1)
                        nodes = slice(T * a, T * (a + 1))
                        if i:
                            pe.wait_ge(r_gate, i)
                        for k in range(4):
                            pe.matmul(PS[0:T, 2, 0:2 * R], rT_hi[n % 2][:, k, nodes], gw_hl[:, k, :],
                                      start=(k == 0), stop=(k == 3))
                        for k in range(4):
                            g = pe.matmul(PS[0:T, 3, 0:2 * R], rT_lo[n % 2][:, k, nodes], gw_hl[:, k, :],
                                          start=(k == 0), stop=(k == 3))
                        g.then_inc(r_gate_ps, 1)
                        for w in range(3):
                            if i % (2 * NP) == 0:
                                pe.wait_ge(r_w_lo, 3 * l + w + 1)
                            if i:
                                if w < 2:
                                    pe.wait_ge(r_m_lo, 2 * (i - 1) + w + 1)
                                else:
                                    pe.wait_ge(r_self_out, i)
                            rows(4 + w, a, rT_hi[n % 2], rT_lo[n % 2], wr_hi[w], wr_lo[w], rb3 if w == 2 else None)\
                                .then_inc(r_mm_ps, 1)
                        if a == 0 and p + 1 < NP:
                            turn_nodes(p + 1)
                pe.drain().then_inc(r_end[0], 1)
                for s in r_end[1:]:
                    pe.wait_ge(s, 2 * l + 1)
                for t in range(NT):
                    n = NT * l + t
                    pe.wait_ge(r_adj_hi, n + 1)
                    if n >= 2:
                        pe.wait_ge(r_res_ready, n - 1)
                    for r in range(R):
                        for k in range(NT):
                            pe.matmul(PS[0:T, t % 2, :], adj_hi[t % 2][:, NT * r + k, :], msg_hi[r][:, k, :],
                                      start=(r == 0 and k == 0), stop=False)
                    pe.wait_ge(r_adj_lo, n + 1)
                    with pe.If(counts_large):
                        for r in range(R):
                            for k in range(NT):
                                pe.matmul(PS[0:T, t % 2, :], adj_lo[:, NT * r + k, :], msg_hi[r][:, k, :],
                                          start=False, stop=False)
                    for r in range(R):
                        for k in range(NT):
                            g = pe.matmul(PS[0:T, t % 2, :], adj_hi[t % 2][:, NT * r + k, :], msg_lo[r][:, k, :],
                                          start=False, stop=(r == R - 1 and k == NT - 1))
                    g.then_inc(r_agg_ps, 1)
                pe.drain().then_inc(r_end[0], 1)

        @block.scalar
        def _(act):
            def w_high(where, hi, n):
                wait(act, w_in, where, n - (0 if isinstance(where, str) else 2))
                act.activation(hi[:], w_raw[:], ACT.Copy).then_inc(w_hi_done.sem, 1)

            for p in range(NP):
                act.dma_start(x0[p][:], pair_rows(x_in, p)).then_inc(x_loaded[p % 2].sem, 16)
            for c in range(NRC):
                act.wait_ge(rank_ps, c + 1)
                act.activation(tot[:].rearrange("p k c -> p (k c)")[:, c * RC:(c + 1) * RC],
                               PS[:, 2 + c % 2, 0:RC], ACT.Copy).then_inc(tot_out, 1)
            act.wait_ge(phase_ready, 1)
            act.activation(ph[:], ph[:], ACT.Sin, scale=2.0 * math.pi).then_inc(sin_done, 1)
            act.wait_ge(z1_ps, 1)
            for j, (c0, cn) in enumerate(CH):
                z = act.activation(z2[:, c0:c0 + cn], PS[0:C, 4 + j, 0:cn], ACT.Exp, bias=fb[:, 2:3], scale=-1.0)
            z.then_inc(z1_exp, 1)
            def store_weights(n, bank):
                l, q0 = divmod(16 * n, Q)
                act.wait_ge(basis_used, 2 * n + 2)
                if n >= 2:
                    act.wait_ge(w_stored[n % 2], 32 * (n // 2))
                act.activation(w_out[n % 2][:], PS[:, bank, :], ACT.Copy).then_inc(basis_out, 1)
                act.wait_ge(basis_out, n + 1)
                for r in range(R):
                    act.dma_start(rel_w[l, r, :, :].rearrange("(i q) d -> i q d", q=Q)[:, q0:q0 + 16, :],
                                  w_out[n % 2][64 * r:64 * (r + 1), :]).then_inc(w_stored[n % 2], 16)

            for n in range(NLA // 2):
                if n == 8:
                    for p in range(NP):
                        act.wait_ge(h0_ready, p + 1)
                        act.dma_start(pair_rows(x_lat, p), x0[p][:]).then_inc(x_stored[p % 2].sem, 16)
                store_weights(n, n % 2)
            wait(act, x_stored[0], "setup", (NP + 1) // 2 - 1)
            wait(act, x_stored[1], "setup", NP // 2 - 1)
            act.drain().then_inc(act_end.sem, 1)
            phase_begins(act, "setup", 0)

            def group_to_int(it, b, first):
                act.wait_ge(count_ps, 2 * it + (b + 1))
                if not first:
                    act.wait_ge(count_added, 2 * it + b)
                act.activation(count_add[b][:].rearrange("p (j s) -> p j s", j=3), PS[0:T, 3 * b:3 * b + 3, 0:SB], ACT.Copy)\
                    .then_inc(group_out, 1)

            for b in range(2):
                group_to_int(0, b, True)
            with act.Fori(1, NG // 2) as it:
                for b in range(2):
                    group_to_int(it, b, False)
            act.drain().then_inc(act_end.sem, 1)
            phase_begins(act, "setup", 1)
            for t in range(NT):
                if t >= 2:
                    act.wait_ge(adj_stored[t % 2], 16 * (t // 2))
                act.activation(count_t[t % 2][:], count[:, :, T * t:T * (t + 1)], ACT.Copy).then_inc(count_t_done, 1)
                act.wait_ge(cnt1_ready, t + 1)
                act.activation(cnt1[t % 2][:, 0:N], cnt1[t % 2][:, 0:N], ACT.Ln).then_inc(ln_done, 1)
                if t == 3:
                    w_high("setup", wk_hi, 0)
                if t % 2 == 0 and t and NLA + t <= NL:
                    n = (NLA + t) // 2 - 1
                    store_weights(n, 6 + n % 2)
            for i in range(2):
                act.wait_ge(w_stored[i], 16 * NW)
                act.wait_ge(adj_stored[i], 16 * NT // 2)
            act.drain().then_inc(act_end.sem, 1)

            def yT_high(lay, i, a, dst_t, before=None):
                wait(act, yT_ps, lay, i)
                if before:
                    before()
                act.activation(dst_t[:, :, T * a:T * (a + 1)],
                               PS[:, 2 + a, 0:4 * T].rearrange("p (c t) -> p c t", c=4), ACT.Copy)\
                    .then_inc(yT_hi_done.sem, 1)

            with act.Fori(0, LAYERS) as lay:

                phase_begins(act, lay, -1)
                yT_high(lay, 0, 0, yT_hi[0])
                yT_high(lay, 1, 1, yT_hi[0])
                w_high(lay, wq_hi, 1)
                wait(act, cols_ready, lay, 0)
                for p in range(NP):
                    cols = slice(W * p, W * (p + 1))
                    for c in range(4):
                        wait(act, k_ps, lay, 4 * p + c)
                        act.activation(k_hi[:, c, cols], PS[:, bank_of(QKV_GROUPS, k_lo_done, 4 * p + c), 0:W],
                                       ACT.Identity, bias=bk_col[:, c:c + 1]).then_inc(k_hi_done.sem, 1)
                    if p == 0:
                        w_high(lay, wv_hi, 2)
                    for c in range(4):
                        wait(act, q_ps, lay, 4 * p + c)
                        act.activation(q_raw[:, c, cols], PS[:, bank_of(QKV_GROUPS, q_done, 4 * p + c), 0:W],
                                       ACT.Identity, bias=bq_col[:, c:c + 1]).then_inc(q_done.sem, 1)
                    for a in range(2):
                        if p + 1 < NP and a == 0:
                            if p >= 1:
                                wait(act, v_ps, lay, 2 * p - 1)
                            yT_high(lay, 2 * p + 2, 0, yT_hi[(p + 1) % 2])
                        wait(act, v_ps, lay, 2 * p + a)
                        act.activation(v_hi[:, 2 * p + a, :], PS[0:T, bank_of(QKV_GROUPS, v_lo_done, 2 * p + a), :],
                                       ACT.Copy).then_inc(v_hi_done.sem, 1)
                    if p + 1 < NP:
                        yT_high(lay, 2 * p + 3, 1, yT_hi[(p + 1) % 2])
                act.drain().then_inc(act_end.sem, 1)

                phase_begins(act, lay, 0)

                def q_high(i):
                    if i >= 4:
                        wait(act, s_ps, lay, 2 * (i - 4) + 1)
                    p, h = divmod(i, 4)
                    act.activation(q_hi[:, h, :], q_raw[:, h, W * p:W * (p + 1)], ACT.Copy).then_inc(q_hi_done.sem, 1)

                def exponentials(i, a):
                    u = 2 * i + a
                    wait(act, negmax_ready, lay, u)
                    act.activation(prob[u % 3][:], prob[u % 3][:], ACT.Exp, bias=neg_max[0:T, u % 4:u % 4 + 1],
                                   scale=SCALE, accum_out=den[0:T, u % 4:u % 4 + 1]).then_inc(exp_done.sem, 1)

                def normalise_rest(i, a):
                    u = 2 * i + a
                    wait(act, inv_ready, lay, u)
                    act.activation(prob[u % 3][:, SPLIT:N], prob[u % 3][:, SPLIT:N], ACT.Copy,
                                   scale=inv_den[0:T, u % 4:u % 4 + 1]).then_inc(rest_normed.sem, 1)

                def pT_high(i, a):
                    u = 2 * i + a
                    wait(act, pT_ps, lay, u)
                    if i >= 2 and a == 0:
                        wait(act, o_ps, lay, i - 2)
                    n = slice(T * a, T * (a + 1))
                    act.activation(pT_hi[i % 2][:, 0:8, n].rearrange("p (b c) t -> p b c t", b=2),
                                   PS[0:T, 3:5, 0:4 * T].rearrange("p b (c t) -> p b c t", c=4), ACT.Copy)
                    act.activation(pT_hi[i % 2][:, 8:10, n],
                                   PS[0:T, 5, 0:2 * T].rearrange("p (c t) -> p c t", c=2), ACT.Copy)\
                        .then_inc(pT_hi_done.sem, 1)

                def head_out(i):
                    p, h = divmod(i, 4)
                    wait(act, o_ps, lay, i)
                    act.activation(q_raw[:, h, W * p:W * (p + 1)], PS[:, 6 + i % 2, 0:W], ACT.Copy)\
                        .then_inc(o_done.sem, 1)

                q_high(0)
                q_high(1)
                for i in range(4 * NP + 2):
                    for a in range(2):
                        if 1 <= i <= 4 * NP:
                            pT_high(i - 1, a)
                        if i < 4 * NP:
                            exponentials(i, a)
                            normalise_rest(i, a)
                        if a == 0 and 2 <= i + 1 < 4 * NP:
                            q_high(i + 1)
                    if i >= 2:
                        head_out(i - 2)
                act.drain().then_inc(act_end.sem, 1)

                phase_begins(act, lay, 1)

                def o_high(p):
                    if p >= 2:
                        wait(act, wo_ps, lay, 2 * (p - 2) + 1)
                    act.activation(oT_hi[p % 2][:], q_raw[:, :, W * p:W * (p + 1)], ACT.Copy)\
                        .then_inc(oT_hi_done.sem, 1)

                o_high(0)
                w_high(lay, wo_hi, 3)
                o_high(1)
                w_high(lay, w1_hi, 4)
                for a in range(2):
                    yT_high(lay, 2 * NP + a, a, zT_hi)
                w_high(lay, w2_hi, 5)
                for p in range(NP):
                    for c in range(4):
                        wait(act, w1_ps, lay, 4 * p + c)
                        if p:
                            wait(act, h_lo_done, lay, 4 * (p - 1) + c)
                            if c == 0:
                                wait(act, w2_ps, lay, 2 * p - 1)
                        h = PS[:, bank_of(MLP_GROUPS, h_done, 4 * p + c), 0:W]
                        act.activation(hT[:, c, :], h, ACT.Relu, bias=b1_col[:, c:c + 1])
                        act.activation(hT_hi[:, c, :], h, ACT.Relu, bias=b1_col[:, c:c + 1]).then_inc(h_done.sem, 1)
                    if p == 2:
                        w_high(lay, wk_hi, 6)
                    if p + 2 < NP:
                        o_high(p + 2)
                    if p + 1 < NP:
                        for a in range(2):
                            yT_high(lay, 2 * NP + 2 * p + 2 + a, a, zT_hi)
                act.drain().then_inc(act_end.sem, 1)

            phase_begins(act, "final", -1)
            for l in range(2):
                if l:
                    act.wait_ge(r_end[0], 2)
                    act.wait_ge(r_end[2], 2)

                def nodes_high(p):
                    n = NP * l + p
                    for a in range(2):
                        act.wait_ge(r_hT_ps, 2 * n + a + 1)
                        if n >= 2:
                            act.wait_ge(r_mm_ps, 6 * (n - 1))
                        act.activation(rT_hi[n % 2][:, :, T * a:T * (a + 1)],
                                       PS[:, a, 0:4 * T].rearrange("p (c t) -> p c t", c=4), ACT.Copy)\
                            .then_inc(r_hT_hi, 1)

                def weights_high(l, n):
                    act.wait_ge(r_w_in, 16 * (3 * l + n + 1))
                    act.activation(wr_hi[n][:], w_rawr[:], ACT.Copy).then_inc(r_w_hi, 1)

                if l == 0:
                    weights_high(0, 0)
                nodes_high(0)
                if l == 0:
                    weights_high(0, 1)
                    weights_high(0, 2)
                for p in range(NP):
                    for a in range(2):
                        i = 2 * (NP * l + p) + a
                        tile = 2 * p + a
                        act.wait_ge(r_gate_exp, 2 * i + 1)
                        act.activation(gate_sb[0:T, 1, :], gate_sb[0:T, 0, :], ACT.Exp, scale=-1.0).then_inc(r_gate_exp, 1)
                        act.wait_ge(r_gate, i + 1)
                        for r in range(R):
                            act.wait_ge(r_mm_ps, 3 * i + r + 1)
                            act.activation(msg_hi[r][:, tile, :], PS[0:T, 4 + r, :], ACT.Copy,
                                           scale=gate_sb[0:T, 0, r:r + 1]).then_inc(r_m_hi, 1)
                        act.wait_ge(r_mm_ps, 3 * i + 3)
                        act.activation(self_term[:, tile, :], PS[0:T, 6, :], ACT.Copy).then_inc(r_self_out, 1)
                        if a == 0 and p + 1 < NP:
                            nodes_high(p + 1)
                act.drain().then_inc(r_end[1], 1)
                for e in (r_end[0], r_end[2]):
                    act.wait_ge(e, 2 * l + 1)
                for t in range(NT):
                    n = NT * l + t
                    act.wait_ge(r_adj_in[t % 2], 16 * (n // 2 + 1))
                    if t >= 2:
                        act.wait_ge(r_agg_ps, n - 1)
                    act.activation(adj_hi[t % 2][:], adj16[t % 2][:], ACT.Copy).then_inc(r_adj_hi, 1)
                    if l == 0 and t in SPLIT_AT:
                        weights_high(1, SPLIT_AT.index(t))
                act.drain().then_inc(r_end[1], 1)

        @block.vector
        def _(v):
            links = {"setup": 0, "layer": 0, "final": 0}

            def link(ins, where):
                kind = where if isinstance(where, str) else "layer"
                ins.then_inc(chain.sem, 1)
                wait(v, chain, where, links[kind])
                links[kind] += 1

            def norm_stats(where, i, x):
                s = i % 2
                for a in range(2):
                    last = v.bn_stats(bn[0:T, a, :], x[:, a, :])
                link(last, where)
                v.memset(wait_slot[0:1, 0:1], 0.0)
                for a in range(2):
                    last = v.bn_aggr(mv[0:T, s, 2 * a:2 * a + 2], bn[0:T, a, :])
                link(last, where)
                v.tensor_scalar(var_eps[0:T, s, :], mv[0:T, s, 1:4:2], EPS, None, ALU.add).then_inc(var_ready.sem, 1)

            def norm_apply(where, i, x, y):
                s = i % 2
                wait(v, rstd_ready, where, i)
                for a in range(2):
                    last = v.tensor_scalar(y[:, a, :], x[:, a, :], mv[0:T, s, 2 * a:2 * a + 1], rstd[0:T, s, a:a + 1],
                                           ALU.subtract, ALU.mult)
                last.then_inc(x_used.sem, 1)
                wait(v, x_used, where, i)

            v.memset(cond3[:].bitcast(fp32), 1.0)
            v.memset(ones_r[:].bitcast(fp32), 1.0)
            for b in range(2):
                v.memset(mod3[b][:].bitcast(fp32), 0.0)
            v.wait_ge(edges_in, 96)
            v.wait_ge(consts, 8)
            v.tensor_copy(dst_f[:], dst_i[:])
            v.tensor_copy(payload[:, :, 0], src_i[:])
            link(v.tensor_copy(typ_f[:], typ_i[:]), "setup")
            link(v.tensor_scalar(tile_f[:], dst_f[:], 1.0 / T, 0.5 / T - 0.5, ALU.mult, ALU.add), "setup")
            link(v.tensor_scalar(tile_f[:], tile_f[:], MAGIC, None, ALU.add), "setup")
            link(v.tensor_scalar(tile_f[:], tile_f[:], MAGIC, None, ALU.subtract), "setup")
            v.scalar_tensor_tensor(payload[:, :, 1], tile_f[:], -float(T), dst_f[:], ALU.mult, ALU.add)
            link(v.tensor_scalar(typ_f[:], typ_f[:], 0.0, float(NT), ALU.not_equal, ALU.mult), "setup")
            link(v.tensor_tensor(bucket[:], typ_f[:], tile_f[:], ALU.add), "setup")
            v.tensor_tensor(mask[:], bucket[:].unsqueeze(1).to_broadcast([128, NB, EC]),
                            bucket_id[:].unsqueeze(2).to_broadcast([128, NB, EC]), ALU.is_equal).then_inc(mask_ready, 1)

            v.wait_ge(freq_ready, 1)
            v.wait_ge(noise_in, 16)
            v.wait_ge(fw_in, 16 * 9)
            link(v.tensor_copy(freq_off[:, 0:1], freq_i[:].bitcast(i32)), "setup")
            link(v.tensor_scalar(freq_off[:, 1:2], freq_off[:, 0:1], F2 / 2 - 0.5, 0.25, ALU.is_gt, ALU.mult), "setup")
            link(v.scalar_tensor_tensor(freq_off[:, 0:1], freq_off[:, 1:2], -2.0 * F2, freq_off[:, 0:1],
                                        ALU.mult, ALU.add), "setup")
            link(v.tensor_scalar(freq_off[:, 0:1], freq_off[:, 0:1], 1.0, 1.0 / 16, ALU.add, ALU.mult), "setup")
            link(v.tensor_scalar(ph[:], ph[:], freq_off[:, 0:1], freq_off[:, 1:2], ALU.mult, ALU.add), "setup")
            link(v.tensor_scalar(ph_int[:], ph[:], MAGIC, None, ALU.add), "setup")
            link(v.tensor_scalar(ph_int[:], ph_int[:], MAGIC, None, ALU.subtract), "setup")
            link(v.tensor_tensor(ph[:], ph[:], ph_int[:], ALU.subtract), "setup")
            v.tensor_scalar(fb[:, 2:3], fb[:, 0:1], -1.0, None, ALU.mult)
            v.tensor_scalar(ph[:], ph[:], 0.4999999, -0.4999999, ALU.min, ALU.max).then_inc(phase_ready, 1)

            for c in range(NRC):
                v.wait_ge(tot_out, c + 1)
                v.tensor_tensor(rank[:].rearrange("p k c -> p (k c)")[:, c * RC:(c + 1) * RC], PS[:, c % 2, 0:RC],
                                tot[:].rearrange("p k c -> p (k c)")[:, c * RC:(c + 1) * RC], ALU.subtract)\
                    .then_inc(rank_out, 1)
            v.wait_ge(tot_out, NRC)
            v.wait_ge(rank_out, NRC)
            tot_f = tot[:].rearrange("p k c -> p (k c)")
            link(v.tensor_tensor_scan(upto[:].rearrange("p k c -> p (k c)"), tot_f, tot_f, 0.0, ALU.add, ALU.max), "setup")
            v.memset(begin[:, 0:1], 0.0)
            link(v.tensor_copy(begin[:, 1:NB], upto[:, 0:NB - 1, EC - 1]), "setup")
            link(v.tensor_tensor(grp[:], upto[:, :, EC - 1], begin[:], ALU.subtract), "setup")
            link(v.tensor_scalar(grp[:], grp[:], GE - 1.0, 1.0 / GE, ALU.add, ALU.mult), "setup")
            link(v.tensor_scalar(grp[:], grp[:], 0.5 / GE - 0.5, MAGIC, ALU.add, ALU.add), "setup")
            link(v.tensor_scalar(grp[:], grp[:], MAGIC, None, ALU.subtract), "setup")
            link(v.tensor_reduce(large[:], grp[0:1, :], AX.X, ALU.max), "setup")
            v.tensor_scalar(large_flag[:], large[:], 4096.0 / GE, None, ALU.is_gt)
            g_t, n, step = grp, 0, 1
            while step < NB:
                b_t = gpre[n % 2]
                v.tensor_tensor(b_t[:, step:], g_t[:, step:], g_t[:, 0:NB - step], ALU.add)
                link(v.tensor_copy(b_t[:, 0:step], g_t[:, 0:step]), "setup")
                g_t, n, step = b_t, n + 1, 2 * step
            ends = g_t
            link(v.tensor_tensor(grp[:], ends[:], grp[:], ALU.subtract), "setup")
            link(v.scalar_tensor_tensor(begin[:], grp[:], float(GE), begin[:], ALU.mult, ALU.subtract), "setup")
            link(v.tensor_tensor(rank[:], rank[:], upto[:], ALU.add), "setup")
            link(v.tensor_tensor(rank[:], rank[:], begin[:].unsqueeze(2).to_broadcast([128, NB, EC]), ALU.add), "setup")
            link(v.tensor_tensor(rank[:], rank[:], mask[:], ALU.mult), "setup")
            link(v.tensor_reduce(pos[:], rank[:].rearrange("p k c -> p c k"), AX.X, ALU.add), "setup")
            link(v.tensor_scalar(pos_hi[:], pos[:], 1.0 / 128, 1.0 / 256 - 0.5, ALU.mult, ALU.add), "setup")
            link(v.tensor_scalar(pos_hi[:], pos_hi[:], MAGIC, None, ALU.add), "setup")
            link(v.tensor_scalar(pos_hi[:], pos_hi[:], MAGIC, -(128.0 * TC - 1), ALU.subtract, ALU.mult), "setup")
            link(v.scalar_tensor_tensor(pos[:], pos[:], float(TC), pos_hi[:], ALU.mult, ALU.add), "setup")
            v.tensor_copy(row_i[:], pos[:]).then_inc(rows_ready, 1)
            link(v.tensor_tensor(group_ge[:], group_no[:].unsqueeze(2).to_broadcast([1, NG, NB]),
                                 ends[0:1, :].unsqueeze(1).to_broadcast([1, NG, NB]), ALU.is_ge), "setup")
            link(v.tensor_reduce(group_no[:], group_ge[:], AX.X, ALU.add), "setup")
            v.tensor_scalar(group_tile[:], group_no[:], NB - 1.0, None, ALU.min)

            v.wait_ge(z1_exp, 1)
            link(v.tensor_scalar(z2[:], z2[:], 1.0, None, ALU.add), "setup")
            link(v.reciprocal(z2[:], z2[:]), "setup")
            for j, (c0, cn) in enumerate(CH):
                last = v.scalar_tensor_tensor(z1[:, c0:c0 + cn], PS[0:C, 4 + j, 0:cn], fb[:, 0:1], z2[:, c0:c0 + cn],
                                              ALU.add, ALU.mult)
            last.then_inc(silu_done, 1)
            wait(v, x_loaded[0], "setup", (NP + 1) // 2 - 1)
            wait(v, x_loaded[1], "setup", NP // 2 - 1)
            for p in range(NP):
                norm_stats("setup", p, x0[p])
                norm_apply("setup", p, x0[p], x0[p])
                v.tensor_scalar(x0[p][:], x0[p][:], 0.0, None, ALU.max).then_inc(h0_ready, 1)

            v.wait_ge(bias_cols_ps, 1)
            v.tensor_copy(cols_all[:].rearrange("p b c -> p (b c)"), PS[:, 7, 0:4 * LAYERS * H])
            v.wait_ge(z2_ps, 1)
            for j, (c0, cn) in enumerate(CH):
                v.tensor_scalar(cond3[0:C, c0:c0 + cn], PS[0:C, 4 + j, 0:cn], fb[:, 1:2], None, ALU.add)
                last = v.tensor_scalar(cond3[64:64 + C, c0:c0 + cn], PS[0:C, 4 + j, 0:cn], fb[:, 1:2], None, ALU.add)
            link(last, "setup")
            for j, (c0, cn) in enumerate(CH):
                last = v.scalar_tensor_tensor(cond3[32:32 + C, c0:c0 + cn], PS[0:C, 4 + j, 0:cn], fb[:, 1:2],
                                              cond3[0:C, c0:c0 + cn].bitcast(fp32), ALU.add, ALU.subtract)
            last.then_inc(cond_ready, 1)
            v.memset(count[:].bitcast(fp32), 0.0).then_inc(count_added, 1)
            v.drain().then_inc(dve_end.sem, 1)

            phase_begins(v, "setup", 0)
            v.wait_ge(table_in, 16)
            v.wait_ge(node_no_ready, 1)
            def one_hot(it, b, first):
                if not first:
                    v.wait_ge(count_ps, 2 * it + (b - 1))
                for h in range(2):
                    v.tensor_scalar(dst_hot[b][:, h, :], node_no[:, 0:128],
                                    table[:, bass.ds(4 * it + (2 * b + h), 1), 1:2].rearrange("p a k -> p (a k)"),
                                    None, ALU.is_equal)
                    last = v.tensor_scalar(src_hot[b][:, h, :], node_no[:],
                                           table[:, bass.ds(4 * it + (2 * b + h), 1), 0:1].rearrange("p a k -> p (a k)"),
                                           None, ALU.is_equal)
                last.then_inc(hot_ready, 1)

            def add_group(it, b):
                k = v.value_load(group_tile[0:1, bass.ds(2 * it + b, 1)], min_val=0, max_val=NB - 1)
                tile = count[:, bass.ds(k, 1), :].rearrange("p a s -> p (a s)")
                v.wait_ge(group_out, 2 * it + (b + 1))
                v.wait_ge(count_added, 2 * it + (b + 1))
                v.tensor_tensor(tile, tile, count_add[b][:], ALU.add).then_inc(count_added, 1)

            for b in range(2):
                one_hot(0, b, True)
            with v.Fori(1, NG // 2) as it:
                for b in range(2):
                    one_hot(it, b, False)
                    add_group(it - 1, b)
            for b in range(2):
                add_group(NG // 2 - 1, b)
            v.drain().then_inc(dve_end.sem, 1)

            def split_mods(lay, ph, mod=mod3, raw=mod_raw):
                wait(v, mod_raw_in, lay, ph)
                for b in range(2):
                    v.tensor_copy(mod[b][32:32 + C, :], raw[b][0:C, :])
                    last = v.tensor_copy(mod[b][0:C + 1, :], raw[b][:])
                link(last, lay)
                for b in range(2):
                    last = v.tensor_tensor(mod[b][64:64 + C + 1, :], raw[b][:], mod[b][0:C + 1, :].bitcast(fp32), ALU.subtract)
                last.then_inc(mod_ready.sem, 1)

            def w_low(where, lo, hi, n):
                wait(v, w_hi_done, where, n - (0 if isinstance(where, str) else 1))
                v.tensor_tensor(lo[:], w_raw[:], hi[:].bitcast(fp32), ALU.subtract).then_inc(w_lo_done.sem, 1)

            phase_begins(v, "setup", 1)
            for i in range(2):
                v.memset(cnt0[i][:, N:SW], NONE)

            def add_log(t):
                v.wait_ge(ln_done, t + 1)
                v.scalar_tensor_tensor(cnt0[t % 2][:, 0:N], cnt1[t % 2][:, 0:N], 1.0 / SCALE, cnt0[t % 2][:, 0:N],
                                       ALU.mult, ALU.add).then_inc(sbias_ready, 1)

            def both_relations(t):
                if t >= 2:
                    v.wait_ge(csumT_ps, t - 1)
                n = slice(T * t, T * (t + 1))
                v.tensor_tensor(csum[t % 2][:], count[:, 0:NT, n], count[:, NT:NB, n], ALU.add).then_inc(csum_ready, 1)

            both_relations(0)
            for t in range(NT):
                if t + 1 < NT:
                    both_relations(t + 1)
                v.wait_ge(csumT_ps, t + 1)
                if t >= 2:
                    v.wait_ge(sbias_stored[t % 2], 16 * (t // 2))
                    v.wait_ge(sbias_ready, t - 1)
                k0 = 3 * (t % 2)
                for ps, c0, c1 in ((PS[0:T, k0:k0 + 2, 0:4 * T], 0, 8 * T), (PS[0:T, k0 + 2, 0:2 * T], 8 * T, N)):
                    def part(x):
                        return x[:, c0:c1].rearrange("p (b s) -> p b s", b=2) if c0 == 0 else x[:, c0:c1]
                    v.tensor_scalar(part(cnt0[t % 2]), ps, 0.0, NONE, ALU.is_equal, ALU.mult)
                    last = v.tensor_scalar(part(cnt1[t % 2]), ps, 1.0, None, ALU.max)
                last.then_inc(cnt1_ready, 1)
                if t:
                    add_log(t - 1)
                if t in (2, 3):
                    p = t - 2
                    wait(v, x_loaded[p], "setup", (3, 2)[p])
                    norm_stats("setup", NP + p, x_slot[p])
                    norm_apply("setup", NP + p, x_slot[p], yt[p])
                if t == 4:
                    w_low("setup", wk_lo, wk_hi, 0)
                if t == 6:
                    split_mods("setup", 0)
            add_log(NT - 1)
            v.drain().then_inc(dve_end.sem, 1)

            def split_row(where, row3, raw):
                link(v.memset(row3[:].bitcast(fp32), 0.0), where)
                link(v.tensor_copy(row3[0:1, :], raw), where)
                return v.tensor_tensor(row3[32:33, :], raw, row3[0:1, :].bitcast(fp32), ALU.subtract)

            def modulate(lay, i, a, y):
                wait(v, mod_ps, lay, i)
                link(v.scalar_tensor_tensor(y[:, a, :], PS[0:T, 0, :], 1.0, y[:, a, :], ALU.add, ALU.mult), lay)
                v.tensor_tensor(y[:, a, :], PS[0:T, 1, :], y[:, a, :], ALU.add).then_inc(y_ready.sem, 1)

            def yT_low(lay, i, a, hi, lo):
                wait(v, yT_hi_done, lay, i)
                n = slice(T * a, T * (a + 1))
                v.tensor_tensor(lo[:, :, n], PS[:, 2 + a, 0:4 * T].rearrange("p (c t) -> p c t", c=4),
                                hi[:, :, n].bitcast(fp32), ALU.subtract).then_inc(yT_lo_done.sem, 1)

            with v.Fori(0, LAYERS) as lay:
                phase_begins(v, lay, -1)
                for c in (k_hi, k_lo):
                    v.memset(c[:, :, N:SW].bitcast(fp32), 0.0)
                for b, col in enumerate((bk_col, bq_col, b1_col)):
                    last = v.tensor_copy(col[:], cols_all[:, b, bass.ds(H * lay, H)])
                last.then_inc(cols_ready.sem, 1)
                for a in range(2):
                    modulate(lay, a, a, yt[0])
                for a in range(2):
                    yT_low(lay, a, a, yT_hi[0], yT_lo[0])
                wait(v, rows_in, lay, 0)
                split_row(lay, bv3, bv_raw[:]).then_inc(rows_ready_l.sem, 1)
                w_low(lay, wq_lo, wq_hi, 1)
                wait(v, cols_ready, lay, 0)
                for p in range(NP):
                    cols = slice(W * p, W * (p + 1))
                    nxt = (p + 1) % 2
                    if p + 1 < NP:
                        if p:
                            wait(v, x_loaded[nxt], lay, (p + 1) // 2 - 1)
                            norm_stats(lay, p - 1, x_slot[nxt])
                            norm_apply(lay, p - 1, x_slot[nxt], yt[nxt])
                        modulate(lay, 2 * p + 2, 0, yt[nxt])
                    for c in range(4):
                        wait(v, k_hi_done, lay, 4 * p + c)
                        v.scalar_tensor_tensor(k_lo[:, c, cols], PS[:, bank_of(QKV_GROUPS, k_lo_done, 4 * p + c), 0:W],
                                               bk_col[:, c:c + 1], k_hi[:, c, cols].bitcast(fp32), ALU.add, ALU.subtract)\
                            .then_inc(k_lo_done.sem, 1)
                    if p + 1 < NP:
                        modulate(lay, 2 * p + 3, 1, yt[nxt])
                        if p == 0:
                            w_low(lay, wv_lo, wv_hi, 2)
                        if p >= 1:
                            wait(v, v_ps, lay, 2 * p - 1)
                        yT_low(lay, 2 * p + 2, 0, yT_hi[nxt], yT_lo[nxt])
                    for a in range(2):
                        wait(v, v_hi_done, lay, 2 * p + a)
                        v.tensor_tensor(v_lo[:, 2 * p + a, :], PS[0:T, bank_of(QKV_GROUPS, v_lo_done, 2 * p + a), :],
                                        v_hi[:, 2 * p + a, :].bitcast(fp32), ALU.subtract).then_inc(v_lo_done.sem, 1)
                    if p + 1 < NP:
                        yT_low(lay, 2 * p + 3, 1, yT_hi[nxt], yT_lo[nxt])
                v.drain().then_inc(dve_end.sem, 1)

                phase_begins(v, lay, 0)

                def q_low(i):
                    wait(v, q_hi_done, lay, i)
                    p, h = divmod(i, 4)
                    v.tensor_tensor(q_lo[:, h, :], q_raw[:, h, W * p:W * (p + 1)], q_hi[:, h, :].bitcast(fp32),
                                    ALU.subtract).then_inc(q_lo_done.sem, 1)

                def masking(i, a):
                    p, u = i // 4, 2 * i + a
                    wait(v, s_ps, lay, u)
                    if i % 4 == 0:
                        wait(v, sbias_in[2 * (p % 2) + a], lay, p // 2)
                    if u >= 3:
                        wait(v, pT_ps, lay, u - 3)
                    s = slice(u % 4, u % 4 + 1)
                    v.memset(wait_slot[0:1, 0:1], 0.0)
                    v.tensor_tensor_reduce(prob[u % 3][:].rearrange("p (j s) -> p j s", j=3), PS[0:T, 0:3, 0:SB],
                                           sbias[p % 2][a][:].rearrange("p (j s) -> p j s", j=3),
                                           1.0, -3e38, ALU.add, ALU.max, row_max[0:T, s]).then_inc(masked.sem, 1)
                    wait(v, masked, lay, u)
                    v.tensor_scalar(has_edge[0:T, s], row_max[0:T, s], 0.5 * NONE, None, ALU.is_gt)
                    v.tensor_scalar(neg_max[0:T, s], row_max[0:T, s], -SCALE, None, ALU.mult).then_inc(negmax_ready.sem, 1)

                def inverse(i, a):
                    u = 2 * i + a
                    s = slice(u % 4, u % 4 + 1)
                    wait(v, exp_done, lay, u)
                    link(v.reciprocal(inv_den[0:T, s], den[0:T, s]), lay)
                    v.tensor_tensor(inv_den[0:T, s], inv_den[0:T, s], has_edge[0:T, s], ALU.mult).then_inc(inv_ready.sem, 1)

                def pT_low(i, a):
                    u = 2 * i + a
                    wait(v, pT_hi_done, lay, u)
                    n = slice(T * a, T * (a + 1))
                    v.tensor_tensor(pT_lo[i % 2][:, 0:8, n].rearrange("p (b c) t -> p b c t", b=2),
                                    PS[0:T, 3:5, 0:4 * T].rearrange("p b (c t) -> p b c t", c=4),
                                    pT_hi[i % 2][:, 0:8, n].rearrange("p (b c) t -> p b c t", b=2).bitcast(fp32), ALU.subtract)
                    v.tensor_tensor(pT_lo[i % 2][:, 8:10, n], PS[0:T, 5, 0:2 * T].rearrange("p (c t) -> p c t", c=2),
                                    pT_hi[i % 2][:, 8:10, n].bitcast(fp32), ALU.subtract).then_inc(pT_lo_done.sem, 1)

                q_low(0)
                q_low(1)
                for i in range(4 * NP + 1):
                    for a in range(2):
                        if i < 4 * NP:
                            masking(i, a)
                        if i >= 1:
                            pT_low(i - 1, a)
                        if i < 4 * NP:
                            inverse(i, a)
                        if a == 0 and 2 <= i + 1 < 4 * NP:
                            q_low(i + 1)
                    if i == 4:
                        split_mods(lay, 0)
                v.drain().then_inc(dve_end.sem, 1)

                phase_begins(v, lay, 1)

                def o_low(p):
                    wait(v, oT_hi_done, lay, p)
                    v.tensor_tensor(oT_lo[p % 2][:], q_raw[:, :, W * p:W * (p + 1)], oT_hi[p % 2][:].bitcast(fp32),
                                    ALU.subtract).then_inc(oT_lo_done.sem, 1)

                def add_attention(p):
                    x = x_slot[p % 2]
                    wait(v, x_loaded[p % 2], lay, (2, 1)[p % 2] + p // 2)
                    for a in range(2):
                        wait(v, wo_ps, lay, 2 * p + a)
                        v.tensor_tensor(x[:, a, :], PS[0:T, bank_of(MLP_GROUPS, x_added, 2 * p + a), :], x[:, a, :],
                                        ALU.add).then_inc(x_added.sem, 1)
                    wait(v, x_added, lay, 2 * p + 1)
                    norm_stats(lay, MLP_NORM[p], x)
                    norm_apply(lay, MLP_NORM[p], x, ym[p % 2])

                o_low(0)
                w_low(lay, wo_lo, wo_hi, 3)
                wait(v, rows_in, lay, 2)
                link(split_row(lay, bo3, row_raw[0:1, 0, :]), lay)
                split_row(lay, b23, row_raw[0:1, 1, :]).then_inc(rows_ready_l.sem, 1)
                o_low(1)
                add_attention(0)
                for a in range(2):
                    modulate(lay, 2 * NP + a, a, ym[0])
                w_low(lay, w1_lo, w1_hi, 4)
                for a in range(2):
                    yT_low(lay, 2 * NP + a, a, zT_hi, zT_lo)
                w_low(lay, w2_lo, w2_hi, 5)
                for p in range(NP):
                    if p + 1 < NP:
                        add_attention(p + 1)
                    for c in range(4):
                        wait(v, h_done, lay, 4 * p + c)
                        v.tensor_tensor(hT_lo[:, c, :], hT[:, c, :], hT_hi[:, c, :].bitcast(fp32), ALU.subtract)\
                            .then_inc(h_lo_done.sem, 1)
                    if p + 2 < NP:
                        o_low(p + 2)
                    if p + 1 < NP:
                        modulate(lay, 2 * NP + 2 * p + 2, 0, ym[(p + 1) % 2])
                    for a in range(2):
                        wait(v, w2_ps, lay, 2 * p + a)
                        x = x_slot[p % 2]
                        v.tensor_tensor(x[:, a, :], PS[0:T, bank_of(MLP_GROUPS, x_done, 2 * p + a), :], x[:, a, :],
                                        ALU.add).then_inc(x_done.sem, 1)
                        if a == 0 and p + 1 < NP:
                            modulate(lay, 2 * NP + 2 * p + 3, 1, ym[(p + 1) % 2])
                    if p + 1 < NP:
                        for a in range(2):
                            yT_low(lay, 2 * NP + 2 * p + 2 + a, a, zT_hi, zT_lo)
                    if p < 2:
                        wait(v, x_done, lay, 2 * p + 1)
                        norm_stats(lay, NEXT_NORM[p], x_slot[p])
                        norm_apply(lay, NEXT_NORM[p], x_slot[p], yt[p])
                    if p == NP - 2:
                        w_low(lay, wk_lo, wk_hi, 6)
                        wait(v, mod_ps, lay, 4 * NP - 1)
                        split_mods(lay, 1)
                v.drain().then_inc(dve_end.sem, 1)

            phase_begins(v, "final", -1)
            for l in range(2):
                if l:
                    v.wait_ge(r_end[0], 2)
                    v.wait_ge(r_end[1], 2)

                def weights_low(l, n):
                    v.wait_ge(r_w_hi, 3 * l + n + 1)
                    v.tensor_tensor(wr_lo[n][:], w_rawr[:], wr_hi[n][:].bitcast(fp32), ALU.subtract).then_inc(r_w_lo, 1)

                def normalise(p):
                    x, y = xr[p % 2], yr[p % 2]
                    v.wait_ge(r_x_in[p % 2], 32 * (p // 2 + 1))
                    v.tensor_tensor(x[:], x[:], lr[p % 2][:], ALU.add).then_inc(r_x1_ready, 1)
                    v.wait_ge(r_x1_ready, p + 1)
                    norm_stats("final", p, x)
                    if p >= 2:
                        v.wait_ge(r_hT_ps, 2 * (p - 1))
                    norm_apply("final", p, x, y)
                    v.tensor_scalar(y[:], y[:], 0.0, None, ALU.max).then_inc(r_h_ready, 1)

                def nodes_low(p):
                    n = NP * l + p
                    for a in range(2):
                        v.wait_ge(r_hT_hi, 2 * n + a + 1)
                        c = slice(T * a, T * (a + 1))
                        v.tensor_tensor(rT_lo[n % 2][:, :, c], PS[:, a, 0:4 * T].rearrange("p (c t) -> p c t", c=4),
                                        rT_hi[n % 2][:, :, c].bitcast(fp32), ALU.subtract).then_inc(r_hT_lo, 1)

                if l == 0:
                    normalise(0)
                    weights_low(0, 0)
                nodes_low(0)
                gw = cols_all[:, 3, R * 4 * l:R * 4 * (l + 1)].rearrange("p (r c) -> p c r", c=4)
                link(v.tensor_copy(gw_hl[:, :, 0:R], gw), "final")
                v.tensor_tensor(gw_hl[:, :, R:2 * R], gw, gw_hl[:, :, 0:R].bitcast(fp32), ALU.subtract)
                v.wait_ge(r_small_in, 16 * (l + 1))
                split_row("final", rb3, rb_raw[:]).then_inc(r_rows_ready, 1)
                if l == 0:
                    weights_low(0, 1)
                    weights_low(0, 2)
                for p in range(NP):
                    if l == 0 and p + 1 < NP:
                        normalise(p + 1)
                    for a in range(2):
                        i = 2 * (NP * l + p) + a
                        v.wait_ge(r_gate_ps, i + 1)
                        if i:
                            v.wait_ge(r_m_hi, 2 * i)
                            v.wait_ge(r_m_lo, 2 * i)
                        g = gate_sb[0:T, 0, :]
                        link(v.tensor_copy(g, PS[0:T, 2, 0:R]), "final")
                        link(v.tensor_tensor(g, PS[0:T, 2, R:2 * R], g, ALU.add), "final")
                        v.tensor_tensor(g, PS[0:T, 3, 0:R], g, ALU.add).then_inc(r_gate_exp, 1)
                        v.wait_ge(r_gate_exp, 2 * i + 2)
                        link(v.tensor_scalar(gate_sb[0:T, 1, :], gate_sb[0:T, 1, :], 1.0, None, ALU.add), "final")
                        v.reciprocal(g, gate_sb[0:T, 1, :]).then_inc(r_gate, 1)
                        v.wait_ge(r_gate, i + 1)
                        for r in range(R):
                            v.wait_ge(r_m_hi, 2 * i + r + 1)
                            v.scalar_tensor_tensor(msg_lo[r][:, 2 * p + a, :], PS[0:T, 4 + r, :], gate_sb[0:T, 0, r:r + 1],
                                                   msg_hi[r][:, 2 * p + a, :].bitcast(fp32), ALU.mult, ALU.subtract)\
                                .then_inc(r_m_lo, 1)
                        if a == 0 and p + 1 < NP:
                            nodes_low(p + 1)
                v.drain().then_inc(r_end[2], 1)
                v.wait_ge(r_end[0], 2 * l + 1)
                v.wait_ge(r_end[1], 2 * l + 1)

                def adj_low(t):
                    n = NT * l + t
                    v.wait_ge(r_adj_hi, n + 1)
                    if t:
                        v.wait_ge(r_agg_ps, n)
                    v.tensor_tensor(adj_lo[:], adj16[t % 2][:], adj_hi[t % 2][:].bitcast(fp32), ALU.subtract)\
                        .then_inc(r_adj_lo, 1)

                adj_low(0)
                for t in range(NT):
                    n = NT * l + t
                    if t + 1 < NT:
                        adj_low(t + 1)
                    v.wait_ge(r_agg_ps, n + 1)
                    if t >= 2:
                        v.wait_ge(r_out_stored[t % 2], 16 * (n // 2))
                    link(v.tensor_tensor(res[t % 2][:], PS[0:T, t % 2, :], self_term[:, t, :], ALU.add), "final")
                    if l == 0:
                        v.tensor_scalar(res[t % 2][:], res[t % 2][:], 0.0, None, ALU.max).then_inc(r_res_ready, 1)
                        if t in SPLIT_AT:
                            weights_low(1, SPLIT_AT.index(t))
                    else:
                        v.wait_ge(r_xres_in[t % 2], 16 * (t // 2 + 1))
                        v.tensor_tensor(res[t % 2][:], res[t % 2][:], xres[t % 2][:], ALU.add).then_inc(r_res_ready, 1)
                v.drain().then_inc(r_end[2], 1)
            assert (links["setup"], links["layer"]) == (chain.setup, chain.layer), links


_INS = ['x', 'src', 'dst', 'edge_type_2', 'node_vec1',
        'L0_gnn_f_w1', 'L0_gnn_f_b1', 'L0_gnn_f_w2', 'L0_gnn_f_b2', 'L0_gnn_s1_w', 'L0_gnn_s1_b', 'L0_gnn_b1_w',
        'L0_gnn_b1_b', 'L0_gnn_wq', 'L0_gnn_bq', 'L0_gnn_wk', 'L0_gnn_bk', 'L0_gnn_wv', 'L0_gnn_bv', 'L0_gnn_wo',
        'L0_gnn_bo', 'L0_gnn_s2_w', 'L0_gnn_s2_b', 'L0_gnn_b2_w', 'L0_gnn_b2_b', 'L0_gnn_m_w1', 'L0_gnn_m_b1',
        'L0_gnn_m_w2', 'L0_gnn_m_b2',
        'L1_gnn_basis1', 'L1_gnn_att1', 'L1_gnn_gate_w1', 'L1_gnn_root1', 'L1_gnn_bias1',
        'L1_gnn_basis2', 'L1_gnn_att2', 'L1_gnn_gate_w2', 'L1_gnn_root2', 'L1_gnn_bias2']
_OUTS = [((1250, 512), 'float32')]
_SCRATCH = [("edge_table", (25088, 2)), ("x_lat", (1250, 512)), ("score_bias", (10, 125, 1254)),
            ("adj", (10, 125, 20, 125), "int16"), ("rel_w", (2, 2, 512, 512)),
            ("h_rgcn", (1250, 512))]


def kernel(**inputs):
    import numpy as _np
    import concourse.bacc as _bacc
    from concourse import mybir as _mybir
    from concourse.bass_utils import run_bass_kernel_spmd as _run

    nc = _bacc.Bacc("TRN2", target_bir_lowering=False, num_devices=1)
    arrays, args = {}, []
    for name in _INS:
        a = _np.ascontiguousarray(inputs[name])
        arrays[f"in_{name}_dram"] = a
        args.append(nc.dram_tensor(f"in_{name}_dram", a.shape, _mybir.dt.from_np(a.dtype), kind="ExternalInput").ap())
    for i, (shape, dtype) in enumerate(_OUTS):
        dt = _mybir.dt.from_np(_np.dtype(dtype))
        args.append(nc.dram_tensor(f"out_{i}_dram", shape, dt, kind="ExternalOutput").ap())
    for name, shape, *dtype in _SCRATCH:
        dt = _mybir.dt.from_np(_np.dtype(dtype[0] if dtype else "float32"))
        args.append(nc.dram_tensor(name, shape, dt, kind="Internal").ap())
    gnn_kernel(nc, *args)
    r = _run(nc, [arrays], core_ids=[0])
    return r.results[0]["out_0_dram"]
```
